# Optimizing a Trainium2 kernel written in Bass

```python
import numpy as np
import jax
import jax.numpy as jnp

def _softmax(x, axis=-1):
    return jax.nn.softmax(x, axis=axis)

def _gelu(x):
    return jax.nn.gelu(x, approximate=True)

def _silu(x):
    return jax.nn.silu(x)

def _sigmoid(x):
    return jax.nn.sigmoid(x)

def _layernorm(x, axis=-1, eps=1e-05):
    m = jnp.mean(x, axis=axis, keepdims=True)
    v = jnp.var(x, axis=axis, keepdims=True)
    return (x - m) / jnp.sqrt(v + eps)

def _scatter_add(tgt, idx, src, axis=0):
    return tgt.at[idx].add(src)

def _segment_sum(src, seg, n):
    return jax.ops.segment_sum(src, seg, n)
kernel_name = 'mk_perceiver_d1_seqx_r2_bea2ff'

def setup_inputs(seed: int=0):
    np.random.seed(seed)
    _w = jnp.asarray

    def _rec_inputs():
        import jax
        import jax.numpy as jnp
        _rk = jax.random.key(seed)
        x = 7.22e-05 + 1 * jax.random.normal(jax.random.fold_in(_rk, 1), (32, 64, 512), jnp.float32)
        _lenS = 64 - jax.random.randint(jax.random.fold_in(_rk, 7), (32,), 0, max(1, 64 // 4) + 1, jnp.int32)
        _lenS2 = 1601 - jax.random.randint(jax.random.fold_in(_rk, 8), (32,), 0, max(1, 1601 // 4) + 1, jnp.int32)
        _ctx_1024P = jax.random.normal(jax.random.fold_in(_rk, 11), (32, 16, 512), jnp.float32)
        _ctx_1024c = jax.random.dirichlet(jax.random.fold_in(_rk, 511), 0.3 * jnp.ones((16,), jnp.float32), (32, 1601))
        _ctx_1024t = jnp.einsum('bsk,bkd->bsd', _ctx_1024c, _ctx_1024P)
        _ctx_1024t = _ctx_1024t * jax.lax.rsqrt(jnp.mean(jnp.square(_ctx_1024t)) + 1e-12) * 0.953939
        ctx_1024 = 4.13588e-05 + 0.999923 * (_ctx_1024t + 0.3 * jax.random.normal(jax.random.fold_in(_rk, 611), (32, 1601, 512), jnp.float32))
        return (x, ctx_1024)
    x, ctx_1024 = _rec_inputs()

    def _L0_xattn_setup():
        import jax, jax.numpy as jnp
        import numpy as np
        B, SQ, SK, D = (4, 1024, 1024, 512)
        key = jax.random.key(seed)
        ks = jax.random.split(key, 8)
        s = 1.0 / np.sqrt(D)
        return {'input_seq': jax.random.normal(ks[0], (B, SQ, D), jnp.float32), 'condition_seq': jax.random.normal(ks[1], (B, SK, D), jnp.float32), 'Wq': jax.random.normal(ks[2], (D, D), jnp.float32) * s, 'bq': jnp.zeros((D,), jnp.float32), 'Wk': jax.random.normal(ks[3], (D, D), jnp.float32) * s, 'bk': jnp.zeros((D,), jnp.float32), 'Wv': jax.random.normal(ks[4], (D, D), jnp.float32) * s, 'bv': jnp.zeros((D,), jnp.float32)}
    _L0_xattn_all = _L0_xattn_setup()
    _L0_xattn_in = {k: v for k, v in _L0_xattn_all.items() if k in ('Wq', 'bq', 'Wk', 'bk', 'Wv', 'bv')}
    del _L0_xattn_all

    def _L0_attn_setup():
        import jax, jax.numpy as jnp
        import numpy as np
        import math
        DIM = 512
        HEADS = 16
        HEAD_DIM = DIM // HEADS
        key = jax.random.key(seed)
        ks = jax.random.split(key, 7)
        b, n = (2, 1024)
        scale = 1.0 / math.sqrt(DIM)
        x = jax.random.normal(ks[0], (b, n, DIM), dtype=jnp.float32)
        Wq = jax.random.normal(ks[1], (DIM, DIM), dtype=jnp.float32) * scale
        Wk = jax.random.normal(ks[2], (DIM, DIM), dtype=jnp.float32) * scale
        Wv = jax.random.normal(ks[3], (DIM, DIM), dtype=jnp.float32) * scale
        Wo = jax.random.normal(ks[4], (DIM, DIM), dtype=jnp.float32) * scale
        bo = jnp.zeros((DIM,), dtype=jnp.float32)
        denom_bias = jnp.zeros((1, HEADS, 1, 1), dtype=jnp.float32)
        return {'x': x, 'Wq': Wq, 'Wk': Wk, 'Wv': Wv, 'Wo': Wo, 'bo': bo, 'denom_bias': denom_bias}
    _L0_attn_all = _L0_attn_setup()
    _L0_attn_in = {k: v for k, v in _L0_attn_all.items() if k in ('Wq', 'Wk', 'Wv', 'Wo', 'bo', 'denom_bias')}
    del _L0_attn_all

    def _L0_ffn_setup():
        import jax, jax.numpy as jnp
        import numpy as np
        D_MODEL = 512
        D1, D2 = (32, 32)
        F1, F2 = (64, 64)
        E = 64
        TOP_K = 2

        def kmoe(x_flat, W_router, A, B, scale, bias, d_in1, d_in2, d_out1, d_out2, top_k):
            logits = x_flat @ W_router.T
            vals, idx = jax.lax.top_k(logits, top_k)
            probs = jax.nn.softmax(vals, axis=-1)
            xs = x_flat.reshape(-1, d_in1, d_in2)
            Ag = A[idx]
            Bg = B[idx]
            Y = jnp.einsum('nkoi,nij,nkpj->nkop', Ag, xs, Bg)
            out = jnp.einsum('nkop,nk->nop', Y, probs).reshape(-1, d_out1 * d_out2)
            return out * scale + bias
        key = jax.random.key(seed)
        ks = jax.random.split(key, 12)
        s = 0.02
        return {'x': jax.random.normal(ks[0], (4, 1024, D_MODEL), dtype=jnp.float32), 'W_up': jax.random.normal(ks[1], (E, D1 * D2), dtype=jnp.float32) * s, 'A_up': jax.random.normal(ks[2], (E, F1, D1), dtype=jnp.float32) * s, 'B_up': jax.random.normal(ks[3], (E, F2, D2), dtype=jnp.float32) * s, 'scale_up': jnp.ones((1,), dtype=jnp.float32), 'bias_up': jnp.zeros((F1 * F2,), dtype=jnp.float32), 'W_down': jax.random.normal(ks[4], (E, F1 * F2), dtype=jnp.float32) * s, 'A_down': jax.random.normal(ks[5], (E, D1, F1), dtype=jnp.float32) * s, 'B_down': jax.random.normal(ks[6], (E, D2, F2), dtype=jnp.float32) * s, 'scale_down': jnp.ones((1,), dtype=jnp.float32), 'bias_down': jnp.zeros((D1 * D2,), dtype=jnp.float32)}
    _L0_ffn_all = _L0_ffn_setup()
    _L0_ffn_in = {k: v for k, v in _L0_ffn_all.items() if k in ('W_up', 'A_up', 'B_up', 'scale_up', 'bias_up', 'W_down', 'A_down', 'B_down', 'scale_down', 'bias_down')}
    del _L0_ffn_all
    return {'x': x, 'ctx_1024': ctx_1024, 'L0_xattn_Wq': _L0_xattn_in['Wq'], 'L0_xattn_bq': _L0_xattn_in['bq'], 'L0_xattn_Wk': _L0_xattn_in['Wk'], 'L0_xattn_bk': _L0_xattn_in['bk'], 'L0_xattn_Wv': _L0_xattn_in['Wv'], 'L0_xattn_bv': _L0_xattn_in['bv'], 'L0_attn_Wq': _L0_attn_in['Wq'], 'L0_attn_Wk': _L0_attn_in['Wk'], 'L0_attn_Wv': _L0_attn_in['Wv'], 'L0_attn_Wo': _L0_attn_in['Wo'], 'L0_attn_bo': _L0_attn_in['bo'], 'L0_attn_denom_bias': _L0_attn_in['denom_bias'], 'L0_ffn_W_up': _L0_ffn_in['W_up'], 'L0_ffn_A_up': _L0_ffn_in['A_up'], 'L0_ffn_B_up': _L0_ffn_in['B_up'], 'L0_ffn_scale_up': _L0_ffn_in['scale_up'], 'L0_ffn_bias_up': _L0_ffn_in['bias_up'], 'L0_ffn_W_down': _L0_ffn_in['W_down'], 'L0_ffn_A_down': _L0_ffn_in['A_down'], 'L0_ffn_B_down': _L0_ffn_in['B_down'], 'L0_ffn_scale_down': _L0_ffn_in['scale_down'], 'L0_ffn_bias_down': _L0_ffn_in['bias_down']}

def reference(x, ctx_1024, L0_xattn_Wq, L0_xattn_bq, L0_xattn_Wk, L0_xattn_bk, L0_xattn_Wv, L0_xattn_bv, L0_attn_Wq, L0_attn_Wk, L0_attn_Wv, L0_attn_Wo, L0_attn_bo, L0_attn_denom_bias, L0_ffn_W_up, L0_ffn_A_up, L0_ffn_B_up, L0_ffn_scale_up, L0_ffn_bias_up, L0_ffn_W_down, L0_ffn_A_down, L0_ffn_B_down, L0_ffn_scale_down, L0_ffn_bias_down):
    import jax
    import jax.numpy as jnp

    def _L0_xattn_ref(input_seq, condition_seq, Wq, bq, Wk, bk, Wv, bv):
        import jax, jax.numpy as jnp
        import numpy as np
        B, SQ, SK, D = (4, 1024, 1024, 512)
        q = jnp.einsum('bsd,ed->bse', input_seq, Wq) + bq
        k = jnp.einsum('btd,ed->bte', condition_seq, Wk) + bk
        v = jnp.einsum('btd,ed->bte', condition_seq, Wv) + bv
        scores = jnp.einsum('bse,bte->bst', q, k)
        attn = jax.nn.softmax(scores, axis=-1)
        attended = jnp.einsum('bst,bte->bse', attn, v)
        return attended

    def _L0_attn_ref(x, Wq, Wk, Wv, Wo, bo, denom_bias):
        import jax, jax.numpy as jnp
        import numpy as np
        import math
        DIM = 512
        HEADS = 16
        HEAD_DIM = DIM // HEADS
        b, n, d = x.shape
        h, hd = (HEADS, HEAD_DIM)

        def split_heads(t):
            return t.reshape(b, n, h, hd).transpose(0, 2, 1, 3)
        q = split_heads(x @ Wq.T)
        k = split_heads(x @ Wk.T)
        v = split_heads(x @ Wv.T)
        sim = jnp.einsum('bhid,bhjd->bhij', q, k) / math.sqrt(hd)
        causal_mask = jnp.triu(jnp.ones((n, n), dtype=bool), k=1)
        neg = -jnp.finfo(sim.dtype).max
        sim = jnp.where(causal_mask, neg, sim)
        sim_max = jnp.max(sim, axis=-1, keepdims=True)
        exp_sim = jnp.exp(sim - sim_max)
        denom = jnp.sum(exp_sim, axis=-1, keepdims=True) + jnp.exp(denom_bias)
        attn = exp_sim / denom
        out = jnp.einsum('bhij,bhjd->bhid', attn, v)
        out = out.transpose(0, 2, 1, 3).reshape(b, n, d)
        return out @ Wo.T + bo

    def _L0_ffn_ref(x, W_up, A_up, B_up, scale_up, bias_up, W_down, A_down, B_down, scale_down, bias_down):
        import jax, jax.numpy as jnp
        import numpy as np
        D_MODEL = 512
        D1, D2 = (32, 32)
        F1, F2 = (64, 64)
        E = 64
        TOP_K = 2

        def kmoe(x_flat, W_router, A, B, scale, bias, d_in1, d_in2, d_out1, d_out2, top_k):
            logits = x_flat @ W_router.T
            vals, idx = jax.lax.top_k(logits, top_k)
            probs = jax.nn.softmax(vals, axis=-1)
            xs = x_flat.reshape(-1, d_in1, d_in2)
            Ag = A[idx]
            Bg = B[idx]
            Y = jnp.einsum('nkoi,nij,nkpj->nkop', Ag, xs, Bg)
            out = jnp.einsum('nkop,nk->nop', Y, probs).reshape(-1, d_out1 * d_out2)
            return out * scale + bias
        orig_shape = x.shape
        x_flat = x.reshape(-1, D1 * D2)
        h = kmoe(x_flat, W_up, A_up, B_up, scale_up, bias_up, D1, D2, F1, F2, TOP_K)
        h = jax.nn.gelu(h, approximate=False)
        y = kmoe(h, W_down, A_down, B_down, scale_down, bias_down, F1, F2, D1, D2, TOP_K)
        return y.reshape(*orig_shape[:-1], D_MODEL)
    x = x + _L0_xattn_ref(_layernorm(x, axis=-1), ctx_1024, L0_xattn_Wq, L0_xattn_bq, L0_xattn_Wk, L0_xattn_bk, L0_xattn_Wv, L0_xattn_bv)
    x = x + _L0_attn_ref(_layernorm(x, axis=-1), L0_attn_Wq, L0_attn_Wk, L0_attn_Wv, L0_attn_Wo, L0_attn_bo, L0_attn_denom_bias)
    x = x + _L0_ffn_ref(_layernorm(x, axis=-1), L0_ffn_W_up, L0_ffn_A_up, L0_ffn_B_up, L0_ffn_scale_up, L0_ffn_bias_up, L0_ffn_W_down, L0_ffn_A_down, L0_ffn_B_down, L0_ffn_scale_down, L0_ffn_bias_down)
    return x

_drawn_inputs = setup_inputs


def setup_inputs(seed=0):
    import zlib

    import numpy as np

    out = dict(_drawn_inputs(seed))
    spreads = {'L0_xattn_bq': (0.0, 0.1),
     'L0_xattn_bk': (0.0, 0.8),
     'L0_xattn_bv': (0.0, 0.1),
     'L0_attn_bo': (0.0, 0.1),
     'L0_attn_denom_bias': (0.0, 0.8),
     'L0_ffn_bias_up': (0.0, 0.8),
     'L0_ffn_bias_down': (0.0, 0.1)}
    factors = {'L0_ffn_W_up': 8.0,
     'L0_ffn_A_up': 8.0,
     'L0_ffn_B_up': 8.0,
     'L0_ffn_W_down': 8.0,
     'L0_ffn_A_down': 8.0,
     'L0_ffn_B_down': 8.0}
    for name, (base, spread) in spreads.items():
        noise = np.random.default_rng([zlib.crc32(name.encode()), seed]).standard_normal(out[name].shape)
        drawn = base * np.exp(spread * noise) if base else spread * noise
        out[name] = jnp.asarray(drawn.astype(out[name].dtype))
    for name, factor in factors.items():
        out[name] = (out[name] * factor).astype(out[name].dtype)
    return out
```

```python
from contextlib import ExitStack
from math import prod

import concourse.bass as bass
from concourse import mybir

F32 = mybir.dt.float32
U32 = mybir.dt.uint32
ALU = mybir.AluOpType
ACT = mybir.ActivationFunctionType
AX = mybir.AxisListType
SPARE = {}
PE_ONLY = [mybir.EngineType.PE]

P = 128
SEQS, SEQ, D, CTX = 32, 64, 512, 1601
DC = D // P
QUADS = SEQS // 4
QROWS = 4 * SEQ
EPS = 1e-5
HEADS = 16
HD = D // HEADS
HPC = P // HD
E = 64
D1, F1 = 32, 64
FULL = CTX // P
REST = CTX - FULL * P
TILES = FULL + 1
GROUPS = 4
GT = 4
MASKED = -3.0e38


def apart(e, spare):
    e.sem_inc(spare[e.engine], 1)


def group_tiles(g):
    return range(GT * g, min(GT * g + GT, TILES))


def tile_rows(j):
    return P if j < FULL else REST


def group_cols(g):
    return sum(tile_rows(j) for j in group_tiles(g))


def program(nc, a, out):
    ctx = ExitStack()
    with ctx:
        arena = ctx.enter_context(nc.sbuf_tensor("arena", [P, 53200], F32))
        ps = ctx.enter_context(nc.psum_tensor("ps", [P, 8, 512], F32))

        def sem(name):
            return ctx.enter_context(nc.semaphore(name))

        class Area:

            def __init__(self, at):
                self.at = at

            def __call__(self, *dims, dt=F32):
                n = prod(dims)
                v = arena[:, self.at:self.at + n]
                self.at += n
                assert self.at <= 53200, self.at
                if dt != F32:
                    v = v.bitcast(dt)
                if len(dims) == 1:
                    return v
                names = "abcd"[:len(dims)]
                return v.rearrange(f"p ({' '.join(names)}) -> p {' '.join(names)}",
                                   **{k: d for k, d in zip(names[1:], dims[1:])})

        for n, e in (("pe", nc.tensor), ("dve", nc.vector), ("pool", nc.gpsimd)):
            SPARE[e.engine] = sem("spare_" + n)
        keep = Area(0)
        ident = keep(P)
        qa = keep(DC, SEQS * SEQ)
        qbias = keep(2 * QUADS)
        halves = keep(2)
        after_keep = keep.at

        prepare(nc, sem, Area(after_keep), ps, a, ident, qa, qbias, halves)
        cross(nc, sem, Area(after_keep), ps, a, ident, qa, qbias)
        late = Area(after_keep)
        x2 = late(QUADS, 2 * D)
        x3 = late(QUADS, 2 * D)
        self_attention(nc, sem, Area(late.at), ps, a, ident, qa, halves, x2, x3)
        mixture(nc, sem, Area(late.at), ps, a, ident, qa, x2, x3, out)


def layer_norm_stats(vec, stats, mv, x, s_stat, s_mv, n0):
    for par in range(2):
        vec.bn_stats(stats[:, par, :], x[:, par * D:(par + 1) * D]).then_inc(s_stat, 1)
    vec.wait_ge(s_stat, n0 * 2 + 2)
    apart(vec, SPARE)
    for par in range(2):
        vec.bn_aggr(mv[:, par, :], stats[:, par, :]).then_inc(s_mv, 1)


def layer_norm_rstd(pool, mv, veps, rstd, halves, s_mv, s_veps, s_rstd, n0):
    apart(pool, SPARE)
    pool.tensor_scalar(veps[:, :], mv[:, :, 1], EPS, None, ALU.add).then_inc(s_veps, 1)
    pool.wait_ge(s_veps, n0 + 1)
    pool.tensor_tensor(rstd[:, :], veps[:, :], halves[:, :], ALU.pow).then_inc(s_rstd, 1)


def prepare(nc, sem, area, ps, a, ident, qa, qbias, halves):
    wq, wk = area(DC, D), area(DC, D)
    wqk = area(DC, D)
    bqc, bkc = area(DC), area(DC)
    bq_wide = area(DC, P)
    cols = area(2 * DC)
    xt = [area(2 * D) for _ in range(2)]
    xn = [area(2 * D) for _ in range(2)]
    lnt = [area(DC, QROWS) for _ in range(2)]
    stats, mv = area(2, 6), area(2, 2)
    veps, rstd = area(2), area(2)
    x_h = a["x"].rearrange("(q n r) d -> q n (r d)", q=QUADS, r=2)

    s_w, s_b = sem("pr_w"), sem("pr_b")
    s_x = [sem(f"pr_x{u}") for u in range(2)]
    s_id0, s_id, s_wide = sem("pr_id0"), sem("pr_id"), sem("pr_wide")
    s_half = sem("pr_half")
    s_fuse, s_fused = sem("pr_fuse"), sem("pr_fused")
    s_col, s_cold = sem("pr_col"), sem("pr_cold")
    s_stat, s_mv, s_veps, s_rstd, s_xn = (sem("pr_" + n) for n in ("stat", "mv", "veps", "rstd", "xn"))
    s_t, s_te, s_q, s_qe, s_r, s_re = (sem("pr_" + n) for n in ("t", "te", "q", "qe", "r", "re"))

    with nc.Block() as block:
        @block.sync
        def _(sp):
            sp.dma_start(wq, a["wq"].rearrange("(c p) d -> p c d", p=P)).then_inc(s_w, 16)
            sp.dma_start(wk, a["wk"].rearrange("(c p) d -> p c d", p=P)).then_inc(s_w, 16)
            sp.dma_start(bqc, a["bq"]).then_inc(s_b, 16)
            sp.dma_start(bkc, a["bk"]).then_inc(s_b, 16)
            for u in range(2):
                sp.dma_start(xt[u], x_h[u, :, :]).then_inc(s_x[u], 16)
            with sp.Fori(0, QUADS // 2 - 1) as i:
                for u in range(2):
                    sp.wait_ge(s_xn, i * 4 + 2 * u + 2)
                    sp.dma_start(xt[u], x_h[bass.ds(i * 2 + u + 2, 1), :, :].rearrange("q n d -> n (q d)"))\
                      .then_inc(s_x[u], 16)

        @block.gpsimd
        def _(pool):
            pool.memset(ident, 0.0).then_inc(s_id0, 1)
            pool.memset(halves, -0.5).then_inc(s_half, 1)
            pool.wait_ge(s_id0, 1)
            pool.affine_select(out=ident, in_=ident, compare_op=ALU.not_equal, fill=1.0, base=0,
                               pattern=[[-1, P]], channel_multiplier=1).then_inc(s_id, 1)
            pool.wait_ge(s_half, 1)
            with pool.Fori(0, QUADS // 2) as i:
                for u in range(2):
                    pool.wait_ge(s_mv, i * 4 + 2 * u + 2)
                    layer_norm_rstd(pool, mv, veps, rstd, halves, s_mv, s_veps, s_rstd, i * 2 + u)

        @block.vector
        def _(vec):
            vec.wait_ge(s_b, 32)
            for c in range(DC):
                vec.tensor_copy(bq_wide[:, c, :], bqc[:, c:c + 1].to_broadcast([P, P])).then_inc(s_wide, 1)
            for m in range(DC):
                vec.wait_ge(s_fuse, m + 1)
                vec.tensor_copy(wqk[:, m, :], ps[:, m, :]).then_inc(s_fused, 1)
            vec.wait_ge(s_col, 1)
            vec.tensor_copy(cols, ps[:, 4, 0:2 * DC]).then_inc(s_cold, 1)
            with vec.Fori(0, QUADS // 2) as i:
                for u in range(2):
                    n = i * 2 + u
                    vec.wait_ge(s_x[u], i * 16 + 16)
                    layer_norm_stats(vec, stats, mv, xt[u], s_stat, s_mv, n)
                    vec.wait_ge(s_rstd, n + 1)
                    vec.wait_ge(s_mv, n * 2 + 2)
                    for par in range(2):
                        vec.tensor_scalar(xn[u][:, par * D:(par + 1) * D], xt[u][:, par * D:(par + 1) * D],
                                          mv[:, par, 0:1], rstd[:, par:par + 1], ALU.subtract, ALU.mult)\
                           .then_inc(s_xn, 1)
                    vec.wait_ge(s_r, n + 1)
                    vec.tensor_copy(qbias[:, bass.ds(n * 2, 2)], ps[:, 4, 16:18]).then_inc(s_re, 1)

        @block.scalar
        def _(act):
            act.wait_ge(s_cold, 1)
            with act.Fori(0, QUADS // 2) as i:
                for u in range(2):
                    n = i * 2 + u
                    for par in range(2):
                        act.wait_ge(s_t, n * 2 + par + 1)
                        act.copy(lnt[u][:, :, par::2], ps[:, 5 + par, :].rearrange("p (c n) -> p c n", c=DC))\
                           .then_inc(s_te, 1)
                    for m in range(DC):
                        act.wait_ge(s_q, n * DC + m + 1)
                        act.activation(qa[:, m, bass.ds(n * QROWS, QROWS)], ps[:, m, 0:QROWS],
                                       ACT.Identity, bias=cols[:, m:m + 1]).then_inc(s_qe, 1)

        @block.tensor
        def _(pe):
            pe.wait_ge(s_w, 32)
            for m in range(DC):
                for c in range(DC):
                    last = pe.matmul(ps[:, m, :], wq[:, c, m * P:(m + 1) * P], wk[:, c, :],
                                     start=c == 0, stop=c == DC - 1)
                last.then_inc(s_fuse, 1)
            pe.wait_ge(s_b, 32)
            for k, (w, b) in enumerate(((wk, bqc), (wq, bkc))):
                for m in range(DC):
                    for c in range(DC):
                        last = pe.matmul(ps[:, 4, k * DC + m:k * DC + m + 1], w[:, c, m * P:(m + 1) * P],
                                         b[:, c:c + 1], start=c == 0, stop=c == DC - 1)
            last.then_inc(s_col, 1)
            pe.wait_ge(s_id, 1)
            pe.wait_ge(s_fused, DC)
            pe.wait_ge(s_cold, 1)
            pe.wait_ge(s_wide, DC)
            with pe.Fori(0, QUADS // 2) as i:
                for u in range(2):
                    n = i * 2 + u
                    for par in range(2):
                        pe.wait_ge(s_xn, n * 2 + par + 1)
                        pe.wait_ge(s_te, n * 2)
                        for c in range(DC):
                            last = pe.transpose(ps[:, 5 + par, c * P:(c + 1) * P],
                                                xn[u][:, par * D + c * P:par * D + (c + 1) * P], ident)
                        last.then_inc(s_t, 1)
                    pe.wait_ge(s_te, n * 2 + 2)
                    for m in range(DC):
                        pe.wait_ge(s_qe, n * DC)
                        for c in range(DC):
                            last = pe.matmul(ps[:, m, 0:QROWS], wqk[:, c, m * P:(m + 1) * P],
                                             lnt[u][:, c, :], start=c == 0, stop=c == DC - 1)
                        last.then_inc(s_q, 1)
                    pe.wait_ge(s_re, n)
                    for pair in range(2):
                        o = ps[:, 4, 16 + pair:17 + pair]
                        for c in range(DC):
                            pe.matmul(o, lnt[u][:, c, pair * P:(pair + 1) * P], cols[:, DC + c:DC + c + 1],
                                      start=c == 0, stop=False)
                        for c in range(DC):
                            last = pe.matmul(o, bq_wide[:, c, :], bkc[:, c:c + 1],
                                             start=False, stop=c == DC - 1)
                    last.then_inc(s_r, 1)


def cross(nc, sem, area, ps, a, ident, qa, qbias):
    ct = [area(2, TILES, D) for _ in range(2)]
    xt = [area(2, DC, GT * P) for _ in range(2)]
    qs = [area(DC, P) for _ in range(2)]
    prob = area(CTX)
    probt = area(TILES, P)
    att = area(D)
    mx, sums = area(GROUPS), area(GROUPS)
    top, shifted, bias = area(1), area(1), area(1)
    total, recip = area(1), area(1)
    c_main = a["ctx"][:, 0:FULL * P, :].rearrange("s (p j) d -> s p j d", j=FULL)
    c_rest = a["ctx"][:, FULL * P:CTX, :]

    s_c = [[sem(f"cr_c{u}{g}") for g in range(GROUPS)] for u in range(2)]
    s_fill, s_ea, s_ed = sem("cr_fill"), sem("cr_ea"), sem("cr_ed")
    s_s, s_pv = sem("cr_s"), sem("cr_pv")
    s_mx, s_top, s_sh, s_bias = sem("cr_mx"), sem("cr_top"), sem("cr_sh"), sem("cr_bias")
    s_exp, s_tot, s_rec = sem("cr_exp"), sem("cr_tot"), sem("cr_rec")
    s_att, s_at, s_ate, s_qs = sem("cr_att"), sem("cr_at"), sem("cr_ate"), sem("cr_qs")
    TB, OB, AB = 4, 6, 7
    PIECES = 2 * DC
    PTF = GROUPS
    FILLS = GROUPS * PIECES + PTF
    PAIRS = SEQS // 2

    def filled_before(p):
        return p * FILLS + 2 * PIECES

    def pair_fills(last):
        f = [("ctx", g, c, b) for g in range(2 if last else GROUPS) for c in range(DC) for b in range(2)]
        return f + [("prob", g) for g in range(GROUPS)]

    with nc.Block() as block:
        @block.sync
        def _(sp):
            def load(u, pair, static):
                for g in range(GROUPS):
                    for b in range(2):
                        seq = pair * 2 + b
                        if g < GROUPS - 1:
                            src = c_main[bass.ds(seq, 1), :, GT * g:GT * (g + 1), :].rearrange("s p j d -> p (s j) d")
                            dst = ct[u][:, b, GT * g:GT * (g + 1), :]
                        else:
                            src = c_rest[bass.ds(seq, 1), :, :].rearrange("s p d -> p (s d)")
                            dst = ct[u][0:REST, b, FULL, :]
                        sp.dma_start(dst, src).then_inc(s_c[u][g], 16)
            for u in range(2):
                load(u, u, True)
            with sp.Fori(0, PAIRS // 2 - 1) as i:
                for u in range(2):
                    sp.wait_ge(s_pv, i * 2 + u + 1)
                    load(u, i * 2 + u + 2, False)

        @block.gpsimd
        def _(pool):
            for u in range(2):
                pool.tensor_copy(qs[u], qa[:, :, u * P:(u + 1) * P]).then_inc(s_qs, 1)
            with pool.Fori(0, PAIRS // 2 - 1) as i:
                for u in range(2):
                    pool.wait_ge(s_s, (i * 2 + u + 1) * GROUPS * DC)
                    pool.tensor_copy(qs[u], qa[:, :, bass.ds((i * 2 + u + 2) * P, P)]).then_inc(s_qs, 1)

        def evacuate(e, copy, p, k, what, s_done):
            src = ps[:, TB + k % 2, :]
            e.wait_ge(s_fill, filled_before(p) + k + 1)
            if what[0] == "ctx":
                _, g, c, b = what
                e.wait_ge(s_s, p * GROUPS * DC + g * DC + c + 1)
                w = group_cols((g + 2) % GROUPS)
                copy(xt[g % 2][:, b, c, 0:w], src[:, 0:w]).then_inc(s_done, 1)
            else:
                g = what[1]
                e.wait_ge(s_pv, p)
                if g < GROUPS - 1:
                    copy(probt[:, GT * g:GT * (g + 1), :], src).then_inc(s_done, 1)
                else:
                    copy(probt[0:REST, FULL, :], src[0:REST, 0:P]).then_inc(s_done, 1)

        def first_fills(e, copy, parity, s_done):
            for k in range(parity, 2 * PIECES, 2):
                g, c, b = k // PIECES, k % PIECES // 2, k % 2
                e.wait_ge(s_fill, k + 1)
                copy(xt[g][:, b, c, :], ps[:, TB + k % 2, :]).then_inc(s_done, 1)

        @block.scalar
        def _(act):
            first_fills(act, act.copy, 0, s_ea)

            def pair(i, u, last):
                p = i * 2 + u
                fills = pair_fills(last)
                for k, what in enumerate(fills):
                    if k % 2 == 0 and what[0] == "ctx":
                        evacuate(act, act.copy, p, k, what, s_ea)
                act.wait_ge(s_bias, p + 1)
                act.wait_ge(s_fill, filled_before(p))
                for g in range(GROUPS):
                    w = group_cols(g)
                    act.activation(prob[:, g * GT * P:g * GT * P + w], ps[:, g, 0:w], ACT.Exp,
                                   bias=bias[:, 0:1], accum_out=sums[:, g:g + 1]).then_inc(s_exp, 1)
                for k, what in enumerate(fills):
                    if k % 2 == 0 and what[0] == "prob":
                        evacuate(act, act.copy, p, k, what, s_ea)
                act.wait_ge(s_pv, p + 1)
                act.wait_ge(s_rec, p + 1)
                act.wait_ge(s_at, p)
                act.activation(att, ps[:, OB, :], ACT.Copy, scale=recip[:, 0:1]).then_inc(s_att, 1)
            with act.Fori(0, PAIRS // 2 - 1) as i:
                for u in range(2):
                    pair(i, u, False)
            for u in range(2):
                pair(PAIRS // 2 - 1, u, u == 1)

        @block.vector
        def _(vec):
            first_fills(vec, vec.tensor_copy, 1, s_ed)

            def attended(p):
                vec.wait_ge(s_at, p + 1)
                vec.wait_ge(s_qs, p + 1)
                vec.tensor_copy(qa[:, :, bass.ds(p * P, P)],
                                ps[:, AB, :].rearrange("p (c n) -> p c n", c=DC)).then_inc(s_ate, 1)

            def pair(i, u, last, first):
                p = i * 2 + u
                fills = pair_fills(last)
                for g in range(GROUPS):
                    for k, what in enumerate(fills):
                        if k % 2 == 1 and what[0] == "ctx" and what[1] == g:
                            evacuate(vec, vec.tensor_copy, p, k, what, s_ed)
                    vec.wait_ge(s_s, p * GROUPS * DC + (g + 1) * DC)
                    vec.reduce_max(mx[:, g:g + 1], ps[:, g, 0:group_cols(g)], AX.X).then_inc(s_mx, 1)
                    if g == 0 and not first:
                        attended(p - 1)
                vec.wait_ge(s_mx, (p + 1) * GROUPS)
                vec.reduce_max(top, mx, AX.X).then_inc(s_top, 1)
                vec.wait_ge(s_top, p + 1)
                vec.tensor_tensor(shifted, top, qbias[:, bass.ds(p, 1)], ALU.add).then_inc(s_sh, 1)
                vec.wait_ge(s_sh, p + 1)
                vec.tensor_tensor(bias, qbias[:, bass.ds(p, 1)], shifted, ALU.subtract).then_inc(s_bias, 1)
                for k, what in enumerate(fills):
                    if k % 2 == 1 and what[0] == "prob":
                        evacuate(vec, vec.tensor_copy, p, k, what, s_ed)
                vec.wait_ge(s_exp, (p + 1) * GROUPS)
                vec.reduce_sum(total, sums, AX.X).then_inc(s_tot, 1)
                vec.wait_ge(s_tot, p + 1)
                vec.wait_ge(s_att, p)
                vec.reciprocal(recip, total).then_inc(s_rec, 1)
            for u in range(2):
                pair(0, u, False, u == 0)
            with vec.Fori(1, PAIRS // 2 - 1) as i:
                for u in range(2):
                    pair(i, u, False, False)
            for u in range(2):
                pair(PAIRS // 2 - 1, u, u == 1, False)
            attended(PAIRS - 1)

        @block.tensor
        def _(pe):
            def free_bank(n, k):
                if k % 2 == 0:
                    pe.wait_ge(s_ea, n)
                else:
                    pe.wait_ge(s_ed, n)

            def transpose_group(u, g, c, b, k):
                for j in group_tiles(g):
                    r = tile_rows(j)
                    at = (j - GT * g) * P
                    last = pe.transpose(ps[:, TB + k % 2, at:at + r],
                                        ct[u][0:r, b, j, c * P:(c + 1) * P], ident[0:r, 0:r])
                last.then_inc(s_fill, 1)

            for g in range(2):
                pe.wait_ge(s_c[0][g], 32)
                for k in range(PIECES):
                    n = g * PIECES + k
                    if n >= 2:
                        free_bank(n // 2, n)
                    transpose_group(0, g, k // 2, k % 2, n)

            def transpose_attended(p):
                pe.wait_ge(s_att, p + 1)
                pe.wait_ge(s_ate, p)
                for c in range(DC):
                    last = pe.transpose(ps[:, AB, c * P:(c + 1) * P], att[:, c * P:(c + 1) * P], ident)
                last.then_inc(s_at, 1)

            def pair(i, u, last, first):
                p = i * 2 + u
                half = p * (FILLS // 2) + PIECES
                pe.wait_ge(s_qs, p + 1)
                k = 0
                for g in range(GROUPS):
                    w = group_cols(g)
                    ahead = (g + 2) % GROUPS
                    if g < 2:
                        pe.wait_ge(s_c[u][ahead], i * 32 + 32)
                    elif not last:
                        nxt = (i if u == 0 else i + 1)
                        pe.wait_ge(s_c[1 - u][ahead], nxt * 32 + 32)
                    for c in range(DC):
                        done = half + (g - 2) * DC + c + 1
                        pe.wait_ge(s_ea, done)
                        pe.wait_ge(s_ed, done)
                        for b in range(2):
                            x = pe.matmul(ps[b * SEQ:(b + 1) * SEQ, g, 0:w], qs[u][:, c, b * SEQ:(b + 1) * SEQ],
                                          xt[g % 2][:, b, c, 0:w], start=c == 0, stop=c == DC - 1)
                        x.then_inc(s_s, 1)
                        if g < 2 or not last:
                            for b in range(2):
                                free_bank(half + k // 2, k)
                                transpose_group(u if g < 2 else 1 - u, ahead, c, b, k)
                                k += 1
                    if g == 0 and not first:
                        transpose_attended(p - 1)
                k0 = k
                for g in range(GROUPS):
                    pe.wait_ge(s_exp, p * GROUPS + g + 1)
                    free_bank(half + k // 2, k)
                    for j in group_tiles(g):
                        r = tile_rows(j)
                        x = pe.transpose(ps[0:r, TB + k % 2, (j - GT * g) * P:(j - GT * g + 1) * P],
                                         prob[:, j * P:j * P + r], ident)
                    x.then_inc(s_fill, 1)
                    k += 1
                for j in range(TILES):
                    if j % GT == 0:
                        kk = k0 + j // GT
                        (pe.wait_ge(s_ea, half + kk // 2 + 1) if kk % 2 == 0 else
                         pe.wait_ge(s_ed, half + kk // 2 + 1))
                    r = tile_rows(j)
                    for b in range(2):
                        x = pe.matmul(ps[b * SEQ:(b + 1) * SEQ, OB, :], probt[0:r, j, b * SEQ:(b + 1) * SEQ],
                                      ct[u][0:r, b, j, :], start=j == 0, stop=j == TILES - 1)
                x.then_inc(s_pv, 1)
            for u in range(2):
                pair(0, u, False, u == 0)
            with pe.Fori(1, PAIRS // 2 - 1) as i:
                for u in range(2):
                    pair(i, u, False, False)
            for u in range(2):
                pair(PAIRS // 2 - 1, u, u == 1, False)
            transpose_attended(PAIRS - 1)


def self_attention(nc, sem, area, ps, a, ident, qa, halves, x2, x3):
    w_names = ("xwv", "swq", "swk", "swv", "swo")
    w = {n: area(DC, D) for n in w_names}
    bv, bo = area(D), area(D)
    mask = area(P)
    expdb = area(HEADS)
    ats = area(DC, QROWS)
    x = [area(2 * D) for _ in range(2)]
    x1, xn = area(2 * D), area(2 * D)
    lnt, qt = area(DC, QROWS), area(DC, QROWS)
    kd = area(DC, HPC, QROWS)
    v = area(2, D)
    sc = [area(HPC, P) for _ in range(3)]
    pt = [area(HPC, P) for _ in range(2)]
    aot = area(DC, QROWS)
    nmx, rs = [area(HPC) for _ in range(3)], [area(HPC) for _ in range(3)]
    den, rden = [area(HPC) for _ in range(3)], [area(HPC) for _ in range(3)]
    stats, mv, veps, rstd = area(2, 6), area(2, 2), area(2), area(2)
    x_h = a["x"].rearrange("(q n r) d -> q n (r d)", q=QUADS, r=2)
    ITEMS = 2 * DC
    SCALE = HD ** -0.5

    s_w, s_c, s_x = sem("se_w"), sem("se_c"), [sem(f"se_x{u}") for u in range(2)]
    names = ("kd0", "m0", "m1", "edb", "ats", "p1", "r1", "x1b", "stat", "mv", "veps", "rstd", "xn", "lt", "lte",
             "q", "qe", "k", "ke", "v", "ve", "s", "sm", "mx", "ex", "den", "rd", "nrm", "pt", "pte_a", "pte_d",
             "pv", "pve", "o", "r2", "x2", "stat2", "mv2", "veps2", "rstd2", "x3")
    S = {n: sem("se_" + n) for n in names}

    with nc.Block() as block:
        @block.sync
        def _(sp):
            sp.dma_start(w["xwv"], a["xwv"].rearrange("(c p) e -> p c e", p=P)).then_inc(s_w, 16)
            sp.dma_start(bv, a["bv"].to_broadcast([P, D])).then_inc(s_c, 16)
            for u in range(2):
                sp.dma_start(x[u], x_h[u, :, :]).then_inc(s_x[u], 16)
            for n in w_names[1:]:
                sp.dma_start(w[n], a[n].rearrange("(c p) e -> p c e", p=P)).then_inc(s_w, 16)
            sp.dma_start(bo, a["bo"].to_broadcast([P, D])).then_inc(s_c, 16)
            sp.dma_start(expdb, a["db"].to_broadcast([P, HEADS])).then_inc(s_c, 16)
            with sp.Fori(0, QUADS // 2 - 1) as i:
                for u in range(2):
                    sp.wait_ge(S["r1"], (i * 2 + u + 1) * 2)
                    sp.dma_start(x[u], x_h[bass.ds(i * 2 + u + 2, 1), :, :].rearrange("q n d -> n (q d)"))\
                      .then_inc(s_x[u], 16)

        @block.gpsimd
        def _(pool):
            pool.memset(kd, 0.0).then_inc(S["kd0"], 1)
            pool.memset(mask, 0.0).then_inc(S["m0"], 1)
            pool.wait_ge(S["m0"], 1)
            pool.affine_select(out=mask, in_=mask, compare_op=ALU.is_ge, fill=MASKED, base=0,
                               pattern=[[-1, P]], channel_multiplier=1).then_inc(S["m0"], 1)
            pool.wait_ge(S["m0"], 2)
            pool.affine_select(out=mask[SEQ:P, 0:SEQ], in_=mask[SEQ:P, 0:SEQ], compare_op=ALU.is_gt,
                               fill=MASKED, base=-1, pattern=[[0, SEQ]], channel_multiplier=0).then_inc(S["m1"], 1)
            with pool.Fori(0, QUADS) as i:
                pool.wait_ge(S["mv"], i * 2 + 2)
                layer_norm_rstd(pool, mv, veps, rstd, halves, S["mv"], S["veps"], S["rstd"], i)
                for n in range(ITEMS):
                    pool.wait_ge(S["rd"], i * ITEMS + n + 1)
                    pool.tensor_tensor(sc[n % 3], sc[n % 3],
                                       rden[n % 3].unsqueeze(2).to_broadcast([P, HPC, P]), ALU.mult)\
                        .then_inc(S["nrm"], 1)
                pool.wait_ge(S["mv2"], i * 2 + 2)
                layer_norm_rstd(pool, mv, veps, rstd, halves, S["mv2"], S["veps2"], S["rstd2"], i)

        @block.vector
        def _(vec):
            def quad(i, u):
                q = i * 2 + u
                cols = bass.ds(q * QROWS, QROWS)
                vec.wait_ge(S["o"], q * 2)
                vec.tensor_copy(ats, qa[:, :, cols]).then_inc(S["ats"], 1)
                vec.wait_ge(s_x[u], i * 16 + 16)
                for par in range(2):
                    r = slice(par * D, (par + 1) * D)
                    vec.wait_ge(S["p1"], q * 2 + par + 1)
                    vec.tensor_tensor(x1[:, r], ps[:, 2 + par, :], x[u][:, r], ALU.add).then_inc(S["r1"], 1)
                for par in range(2):
                    r = slice(par * D, (par + 1) * D)
                    vec.wait_ge(S["r1"], q * 2 + par + 1)
                    vec.tensor_tensor(x1[:, r], x1[:, r], bv, ALU.add).then_inc(S["x1b"], 1)
                vec.wait_ge(S["x1b"], q * 2 + 2)
                layer_norm_stats(vec, stats, mv, x1, S["stat"], S["mv"], q)
                vec.wait_ge(S["rstd"], q + 1)
                vec.wait_ge(S["mv"], q * 2 + 2)
                for par in range(2):
                    r = slice(par * D, (par + 1) * D)
                    vec.tensor_scalar(xn[:, r], x1[:, r], mv[:, par, 0:1], rstd[:, par:par + 1],
                                      ALU.subtract, ALU.mult).then_inc(S["xn"], 1)
                for h in range(2):
                    vec.wait_ge(S["q"], q * 2 + h + 1)
                    vec.tensor_copy(qt[:, 2 * h:2 * h + 2, :], ps[:, 2 + h, :].rearrange("p (m n) -> p m n", m=2))\
                       .then_inc(S["qe"], 1)
                for pair in range(2):
                    vec.wait_ge(S["v"], q * 2 + pair + 1)
                    vec.tensor_copy(v[:, pair, :], ps[:, 6 + pair, :]).then_inc(S["ve"], 1)

                def soften(n):
                    vec.wait_ge(S["s"], q * ITEMS + n + 1)
                    if n >= 3:
                        vec.wait_ge(S["pt"], q * ITEMS + n - 2)
                    else:
                        vec.wait_ge(S["pt"], q * ITEMS)
                    vec.scalar_tensor_tensor(sc[n % 3], ps[:, 4 + n % 2, :].rearrange("p (h t) -> p h t", h=HPC),
                                             SCALE, mask.unsqueeze(1).to_broadcast([P, HPC, P]),
                                             ALU.mult, ALU.add).then_inc(S["sm"], 1)
                    vec.wait_ge(S["sm"], q * ITEMS + n + 1)
                    vec.tensor_reduce(nmx[n % 3], sc[n % 3], AX.X, ALU.max, negate=True).then_inc(S["mx"], 1)

                def denominators(n):
                    m = n % DC
                    vec.wait_ge(S["ex"], (q * ITEMS + n + 1) * HPC)
                    vec.tensor_tensor(den[n % 3], rs[n % 3], expdb[:, m * HPC:(m + 1) * HPC], ALU.add)\
                       .then_inc(S["den"], 1)
                    vec.wait_ge(S["den"], q * ITEMS + n + 1)
                    vec.reciprocal(rden[n % 3], den[n % 3]).then_inc(S["rd"], 1)

                def result(n):
                    pair, m = divmod(n, DC)
                    vec.wait_ge(S["pv"], q * ITEMS + n + 1)
                    vec.tensor_copy(aot[:, m, pair * P:(pair + 1) * P], ps[:, 6 + n % 2, 0:P])\
                       .then_inc(S["pve"], 1)
                for n in range(ITEMS + 4):
                    if n < ITEMS:
                        soften(n)
                    if 1 <= n <= ITEMS:
                        denominators(n - 1)
                    if 2 <= n < ITEMS + 2 and (n - 2) % 2:
                        vec.wait_ge(S["pt"], q * ITEMS + n - 1)
                        vec.wait_ge(S["pv"], q * ITEMS + max(n - 3, 0))
                        vec.tensor_copy(pt[(n - 2) % 2], ps[:, n % 2, :].rearrange("p (h t) -> p h t", h=HPC))\
                           .then_inc(S["pte_d"], 1)
                    if n >= 4:
                        result(n - 4)
                for par in range(2):
                    r = slice(par * D, (par + 1) * D)
                    vec.wait_ge(S["o"], q * 2 + par + 1)
                    vec.tensor_tensor(x1[:, r], ps[:, 2 + par, :], x1[:, r], ALU.add).then_inc(S["r2"], 1)
                for par in range(2):
                    r = slice(par * D, (par + 1) * D)
                    vec.wait_ge(S["r2"], q * 2 + par + 1)
                    vec.tensor_tensor(x1[:, r], x1[:, r], bo, ALU.add).then_inc(S["x2"], 1)
                vec.wait_ge(S["x2"], q * 2 + 2)
                layer_norm_stats(vec, stats, mv, x1, S["stat2"], S["mv2"], q)
                vec.tensor_copy(x2[:, bass.ds(q, 1), :], x1.unsqueeze(1)).then_inc(S["x3"], 1)
                vec.wait_ge(S["rstd2"], q + 1)
                vec.wait_ge(S["mv2"], q * 2 + 2)
                for par in range(2):
                    r = slice(par * D, (par + 1) * D)
                    vec.tensor_scalar(x3[:, bass.ds(q, 1), r], x1[:, r].unsqueeze(1), mv[:, par, 0:1],
                                      rstd[:, par:par + 1], ALU.subtract, ALU.mult).then_inc(S["x3"], 1)
            vec.wait_ge(s_c, 48)
            vec.wait_ge(S["m1"], 1)
            vec.wait_ge(S["edb"], 1)
            with vec.Fori(0, QUADS // 2) as i:
                for u in range(2):
                    quad(i, u)

        @block.scalar
        def _(act):
            act.wait_ge(s_c, 48)
            act.activation(expdb, expdb, ACT.Exp).then_inc(S["edb"], 1)
            act.wait_ge(S["kd0"], 1)
            with act.Fori(0, QUADS) as q:
                for par in range(2):
                    act.wait_ge(S["lt"], q * 2 + par + 1)
                    act.copy(lnt[:, :, par::2], ps[:, par, :].rearrange("p (c n) -> p c n", c=DC))\
                       .then_inc(S["lte"], 1)
                for m in range(DC):
                    act.wait_ge(S["k"], q * 2 + m // 2 + 1)
                    for h in range(HPC):
                        r = slice(h * HD, (h + 1) * HD)
                        act.copy(kd[r, m, h, :], ps[r, 4 + m // 2, (m % 2) * QROWS:(m % 2 + 1) * QROWS])\
                           .then_inc(S["ke"], 1)
                for n in range(ITEMS + 2):
                    if n < ITEMS:
                        act.wait_ge(S["mx"], q * ITEMS + n + 1)
                        for h in range(HPC):
                            act.activation(sc[n % 3][:, h, :], sc[n % 3][:, h, :], ACT.Exp,
                                           bias=nmx[n % 3][:, h:h + 1],
                                           accum_out=rs[n % 3][:, h:h + 1]).then_inc(S["ex"], 1)
                    if n >= 2 and (n - 2) % 2 == 0:
                        act.wait_ge(S["pt"], q * ITEMS + n - 1)
                        act.wait_ge(S["pv"], q * ITEMS + max(n - 3, 0))
                        act.copy(pt[(n - 2) % 2], ps[:, n % 2, :].rearrange("p (h t) -> p h t", h=HPC))\
                           .then_inc(S["pte_a"], 1)

        @block.tensor
        def _(pe):
            pe.wait_ge(s_w, 5 * 16)
            with pe.Fori(0, QUADS) as q:
                pe.wait_ge(S["ats"], q + 1)
                for par in range(2):
                    for c in range(DC):
                        last = pe.matmul(ps[:, 2 + par, :], ats[:, c, par::2], w["xwv"][:, c, :],
                                         start=c == 0, stop=c == DC - 1)
                    last.then_inc(S["p1"], 1)
                for par in range(2):
                    pe.wait_ge(S["xn"], q * 2 + par + 1)
                    for c in range(DC):
                        last = pe.transpose(ps[:, par, c * P:(c + 1) * P],
                                            xn[:, par * D + c * P:par * D + (c + 1) * P], ident)
                    last.then_inc(S["lt"], 1)
                pe.wait_ge(S["lte"], q * 2 + 2)
                for n, bank in (("swq", 2), ("swk", 4)):
                    for m in range(DC):
                        for c in range(DC):
                            last = pe.matmul(ps[:, bank + m // 2, (m % 2) * QROWS:(m % 2 + 1) * QROWS],
                                             w[n][:, c, m * P:(m + 1) * P], lnt[:, c, :],
                                             start=c == 0, stop=c == DC - 1)
                        if m % 2:
                            last.then_inc(S["q" if n == "swq" else "k"], 1)
                for pair in range(2):
                    for c in range(DC):
                        last = pe.matmul(ps[:, 6 + pair, :], lnt[:, c, pair * P:(pair + 1) * P],
                                         w["swv"][:, c, :], start=c == 0, stop=c == DC - 1)
                    last.then_inc(S["v"], 1)
                pe.wait_ge(S["qe"], q * 2 + 2)
                pe.wait_ge(S["ke"], (q + 1) * DC * HPC)
                pe.wait_ge(S["ve"], q * 2 + 2)
                for n in range(ITEMS + 3):
                    if n < ITEMS:
                        pair, m = divmod(n, DC)
                        if n >= 2:
                            pe.wait_ge(S["sm"], q * ITEMS + n - 1)
                        pe.matmul(ps[:, 4 + n % 2, :], qt[:, m, pair * P:(pair + 1) * P],
                                  kd[:, m, :, pair * P:(pair + 1) * P], start=True, stop=True).then_inc(S["s"], 1)
                    if 2 <= n < ITEMS + 2:
                        k = n - 2
                        pe.wait_ge(S["nrm"], q * ITEMS + k + 1)
                        if k >= 2:
                            pe.wait_ge(S["pte_d" if k % 2 else "pte_a"], q * (ITEMS // 2) + k // 2)
                        for h in range(HPC):
                            last = pe.transpose(ps[:, k % 2, h * P:(h + 1) * P], sc[k % 3][:, h, :], ident)
                        last.then_inc(S["pt"], 1)
                    if n >= 3:
                        k = n - 3
                        pair, m = divmod(k, DC)
                        pe.wait_ge(S["pte_d" if k % 2 else "pte_a"], q * (ITEMS // 2) + k // 2 + 1)
                        if k >= 2:
                            pe.wait_ge(S["pve"], q * ITEMS + k - 1)
                        for h in range(HPC):
                            head = m * HPC + h
                            last = pe.matmul(ps[h * HD:(h + 1) * HD, 6 + k % 2, 0:P],
                                             v[:, pair, head * HD:(head + 1) * HD], pt[k % 2][:, h, :],
                                             start=True, stop=True)
                        last.then_inc(S["pv"], 1)
                pe.wait_ge(S["pve"], (q + 1) * ITEMS)
                for par in range(2):
                    for c in range(DC):
                        last = pe.matmul(ps[:, 2 + par, :], aot[:, c, par::2], w["swo"][:, c, :],
                                         start=c == 0, stop=c == DC - 1)
                    last.then_inc(S["o"], 1)


class Level:

    def __init__(self, name, j, n1, n2, ta, tb):
        self.name, self.j, self.n1, self.n2, self.ta, self.tb = name, j, n1, n2, ta, tb


def mixture(nc, sem, area, ps, a, ident, qa, x2, x3, out):
    ta_up, tb_up = area(E, F1), area(E, F1)
    ta_dn, tb_dn = area(E, D1), area(E, D1)
    wr_up = area(8, E)
    wr_dn = area(F1, E)
    xs = area(P, D1)
    b_up = area(F1)
    b_dn = area(2 * D)
    scales = area(2)
    x3s = area(2 * D)
    xft = area(8, P)
    ones = area(P)
    fold = area(E)
    lt, lg = area(P), area(E)
    top, top_i = area(8), area(8, dt=U32)
    diff, ex, den = area(1), area(1), area(1)
    prob = area(2)
    diag = area(P, 2)
    pb = area(P * 2)
    row = area(P * 2, dt=U32)
    stage = {"up": [area(4 * D1) for _ in range(2)], "dn": [area(4 * F1) for _ in range(2)]}
    mid = {"up": [area(8 * F1) for _ in range(2)], "dn": [area(8 * D1) for _ in range(2)]}
    x2b = xft.rearrange("p c n -> p (c n)")
    h = qa.rearrange("p c n -> p (c n)").rearrange("p (t j) -> p t j", j=F1)
    ybuf = xs
    res = x3s
    UP = Level("up", D1, F1, F1, ta_up, tb_up)
    DN = Level("dn", F1, D1, D1, ta_dn, tb_dn)
    HALF, STEP = 4, 8
    NSTEP = P // STEP
    CREDIT = 1

    s_t, s_z, s_zd = sem("mo_t"), sem("mo_z"), sem("mo_zd")
    S = {}

    def s(n):
        if n not in S:
            S[n] = sem("mo_" + n)
        return S[n]

    with nc.Block() as block:
        @block.sync
        def _(sp):
            sp.wait_ge(s_z, 6)
            sp.dma_start(ta_up[0:D1, :, :], a["ta_up"]).then_inc(s_t, 16)
            sp.dma_start(tb_up[0:D1, :, :], a["tb_up"]).then_inc(s_t, 16)
            sp.dma_start(ta_dn[0:F1, :, :], a["ta_dn"]).then_inc(s_t, 16)
            sp.dma_start(tb_dn[0:F1, :, :], a["tb_dn"]).then_inc(s_t, 16)
            sp.dma_start(wr_up, a["wr_up"].rearrange("(c p) e -> p c e", p=P)).then_inc(s_t, 16)
            sp.dma_start(wr_dn[0:F1, :, :], a["wr_dn"]).then_inc(s_t, 16)
            sp.dma_start(b_up[0:F1, :], a["b_up"]).then_inc(s_t, 16)
            sp.dma_start(b_dn, a["b_dn"].to_broadcast([P, 2 * D])).then_inc(s_t, 16)
            sp.dma_start(scales[:, 0:1], a["s_up"].to_broadcast([P, 1])).then_inc(s_t, 16)
            sp.dma_start(scales[:, 1:2], a["s_dn"].to_broadcast([P, 1])).then_inc(s_t, 16)
            out_v = out.rearrange("(q n r) d -> q n (r d)", q=QUADS, r=2)
            with sp.Fori(0, QUADS) as t:
                for lv in ("up", "dn"):
                    sp.wait_ge(s(lv + "idx"), t + 1)
                    if lv == "up":
                        sp.wait_ge(s("dnloaded"), t)
                    else:
                        sp.wait_ge(s("uploaded"), t + 1)
                    sp.dma_start(a["choice"], top_i[:, 0:2]).then_inc(s(lv + "ch"), 16)
                    sp.wait_ge(s(lv + "ch"), t * 16 + 16)
                    sp.dma_start(row[0:1, :], a["choice"].rearrange("(o n) k -> o (n k)", o=1))\
                      .then_inc(s(lv + "row"), 16)
                sp.wait_ge(s("res"), t * 2 + 2)
                sp.dma_start(out_v[bass.ds(t, 1), :, :].rearrange("q n d -> n (q d)"), res).then_inc(s("out"), 16)
            sp.wait_ge(s("out"), QUADS * 16)
            for lv in ("up", "dn"):
                sp.wait_ge(s(lv + "row"), QUADS * 16)

        @block.gpsimd
        def _(pool):
            for z in (ta_up, tb_up, ta_dn, tb_dn):
                pool.memset(z, 0.0).then_inc(s_z, 1)
            pool.memset(ones, 1.0).then_inc(s_z, 1)
            pool.tensor_tensor(fold, ident[:, 0:E], ident[:, E:P], ALU.add).then_inc(s_z, 1)
            pool.wait_ge(s_t, 160)
            with pool.Fori(0, QUADS) as t:
                pool.wait_ge(s("out"), t * 16)
                pool.tensor_copy(x3s, x3[:, bass.ds(t, 1), :].rearrange("p q d -> p (q d)")).then_inc(s("x3s"), 1)
                pool.wait_ge(s("uplg"), t + 1)
                pool.tensor_tensor(x2b, x2[:, bass.ds(t, 1), :].rearrange("p q d -> p (q d)"), b_dn, ALU.add)\
                    .then_inc(s("x2b"), 1)
                for lv in (UP, DN):
                    src = xs[0:D1] if lv is UP else h[0:F1]
                    k = D1 if lv is UP else F1
                    if lv is UP:
                        pool.wait_ge(s("xse_a"), t * 4 + 4)
                        pool.wait_ge(s("xse_d"), t * 4 + 4)
                    else:
                        pool.wait_ge(s("gelu"), (t + 1) * NSTEP)
                    apart(pool, SPARE)
                    with pool.Fori(0, NSTEP) as i:
                        n = t * NSTEP + i
                        pool.wait_ge(s("ups1" if lv is UP else "dns1"), n * 2)
                        for z in range(2):
                            pool.tensor_copy(stage[lv.name][z][0:k, :].rearrange("p (t j) -> p t j", j=lv.j),
                                             src[:, bass.ds(i * STEP + z * HALF, HALF), :])\
                                .then_inc(s(lv.name + "st"), 1)

        def choose(vec, lv, t):
            n = lv.name
            vec.wait_ge(s(n + "lg"), t + 1)
            vec.tensor_copy(lg, ps[:, 2, 0:E]).then_inc(s(n + "lge"), 1)
            vec.wait_ge(s(n + "lge"), t + 1)
            apart(vec, SPARE)
            vec.max(top, lg).then_inc(s(n + "top"), 1)
            vec.wait_ge(s(n + "top"), t + 1)
            if lv is UP:
                vec.wait_ge(s("dnch"), t * 16)
            else:
                vec.wait_ge(s("upch"), t * 16 + 16)
            apart(vec, SPARE)
            vec.max_index(top_i, top, lg).then_inc(s(n + "idx"), 1)
            vec.tensor_tensor(diff, top[:, 1:2], top[:, 0:1], ALU.subtract).then_inc(s(n + "df"), 1)
            vec.wait_ge(s(n + "ex"), t + 1)
            vec.tensor_scalar(den, ex, 1.0, None, ALU.add).then_inc(s(n + "dd"), 1)
            vec.wait_ge(s(n + "dd"), t + 1)
            vec.reciprocal(prob[:, 0:1], den).then_inc(s(n + "p0"), 1)
            vec.wait_ge(s(n + "p0"), t + 1)
            vec.tensor_tensor(prob[:, 1:2], ex, prob[:, 0:1], ALU.mult).then_inc(s(n + "p1"), 1)
            vec.wait_ge(s(n + "p1"), t + 1)
            vec.tensor_tensor(diag, ident.unsqueeze(2).to_broadcast([P, P, 2]),
                              prob.unsqueeze(1).to_broadcast([P, P, 2]), ALU.mult).then_inc(s(n + "dg"), 1)
            vec.wait_ge(s(n + "pb"), t + 1)
            vec.tensor_copy(pb, ps[:, 3, 0:2 * P]).then_inc(s(n + "pbe"), 1)

        def transposed_out(e, copy, t, parity, done):
            for k in range(parity, 8, 2):
                e.wait_ge(s("xst"), t * 8 + k + 1)
                copy(xs[0:D1, :, 4 * k:4 * k + 4].rearrange("p n j -> p j n"),
                     ps[0:D1, 4 + k % 2, :].rearrange("p (j n) -> p j n", j=4)).then_inc(done, 1)

        @block.vector
        def _(vec):
            for z in (*stage["up"], *stage["dn"], *mid["up"], *mid["dn"]):
                vec.memset(z, 0.0).then_inc(s_zd, 1)
            vec.wait_ge(s_zd, 8)
            vec.engine_nop().then_inc(s("hb"), CREDIT)
            vec.wait_ge(s_t, 160)
            with vec.Fori(0, QUADS) as t:
                vec.wait_ge(s("xf"), t * 2 + 1)
                vec.tensor_copy(xft[:, 0:4, :], ps[:, 0, :].rearrange("p (c n) -> p c n", c=4)).then_inc(s("xfe_d"), 1)
                vec.wait_ge(s("y"), t * 2)
                transposed_out(vec, vec.tensor_copy, t, 1, s("xse_d"))
                choose(vec, UP, t)
                with vec.Fori(0, NSTEP // 2) as i:
                    for u in range(2):
                        n = t * NSTEP + i * 2 + u
                        for z in range(2):
                            vec.wait_ge(s("ups1"), n * 2 + z + 1)
                            vec.wait_ge(s("ups2"), n * 2)
                            at = (i * 2 + u) * (2 * STEP) + z * 2 * HALF
                            vec.tensor_tensor(mid["up"][z][0:D1, :].rearrange("p (t o) -> p t o", o=F1),
                                              ps[0:D1, z, :].rearrange("p (t o) -> p t o", o=F1),
                                              pb[0:D1, bass.ds(at, 2 * HALF)].unsqueeze(2)
                                              .to_broadcast([D1, 2 * HALF, F1]), ALU.mult).then_inc(s("upm"), 1)
                        vec.wait_ge(s("ups2"), n * 2 + 2)
                        vec.scalar_tensor_tensor(h[0:F1, bass.ds((i * 2 + u) * STEP, STEP), :],
                                                 ps[0:F1, 6 + u, :].rearrange("p (t o) -> p t o", o=F1),
                                                 scales[0:F1, 0:1],
                                                 b_up[0:F1, :].unsqueeze(1).to_broadcast([F1, STEP, F1]),
                                                 ALU.mult, ALU.add).then_inc(s("hb"), 1)
                vec.wait_ge(s("lt"), t + 1)
                vec.tensor_copy(lt, ps[:, 3, 0:P]).then_inc(s("lte"), 1)
                choose(vec, DN, t)
                with vec.Fori(0, NSTEP) as i:
                    n = t * NSTEP + i
                    for z in range(2):
                        vec.wait_ge(s("dns1"), n * 2 + z + 1)
                        at = i * (2 * STEP) + z * 2 * HALF
                        vec.wait_ge(s("dns2"), n)
                        vec.tensor_tensor(mid["dn"][z][0:F1, :].rearrange("p (t o) -> p t o", o=D1),
                                          ps[0:F1, z, 0:2 * HALF * D1].rearrange("p (t o) -> p t o", o=D1),
                                          pb[0:F1, bass.ds(at, 2 * HALF)].unsqueeze(2)
                                          .to_broadcast([F1, 2 * HALF, D1]), ALU.mult).then_inc(s("dnm"), 1)
                for half in range(2):
                    vec.wait_ge(s("y"), t * 2 + half + 1)
                    vec.wait_ge(s("x2b"), t + 1)
                    sl = slice(16 * half, 16 * half + 16)
                    vec.scalar_tensor_tensor(
                        res.rearrange("n (o p) -> n p o", o=D1)[:, sl, :],
                        ps[:, 4 + half, :].rearrange("n (p o) -> n p o", o=D1), scales[:, 1:2],
                        x2b.rearrange("n (o p) -> n p o", o=D1)[:, sl, :], ALU.mult, ALU.add).then_inc(s("res"), 1)

        @block.scalar
        def _(act):
            act.wait_ge(s_t, 160)
            with act.Fori(0, QUADS) as t:
                act.wait_ge(s("xf"), t * 2 + 2)
                act.copy(xft[:, 4:8, :], ps[:, 1, :].rearrange("p (c n) -> p c n", c=4)).then_inc(s("xfe_a"), 1)
                act.wait_ge(s("y"), t * 2)
                transposed_out(act, act.copy, t, 0, s("xse_a"))
                act.wait_ge(s("updf"), t + 1)
                act.activation(ex, diff, ACT.Exp).then_inc(s("upex"), 1)
                with act.Fori(0, NSTEP // 2) as i:
                    for u in range(2):
                        n = t * NSTEP + i * 2 + u
                        act.wait_ge(s("hb"), n + 1 + CREDIT)
                        act.activation(h[0:F1, bass.ds((i * 2 + u) * STEP, STEP), :],
                                       h[0:F1, bass.ds((i * 2 + u) * STEP, STEP), :], ACT.Gelu)\
                           .then_inc(s("gelu"), 1)
                act.wait_ge(s("dndf"), t + 1)
                act.activation(ex, diff, ACT.Exp).then_inc(s("dnex"), 1)
                with act.Fori(0, NSTEP) as i:
                    n = t * NSTEP + i
                    act.wait_ge(s("dns2"), n + 1)
                    act.copy(ybuf[0:D1, bass.ds(i * STEP, STEP), :],
                             ps[0:D1, 6, 0:STEP * D1].rearrange("p (t o) -> p t o", o=D1)).then_inc(s("ye"), 1)

        @block.tensor
        def _(pe):
            def spread(lv, t):
                pe.wait_ge(s(lv.name + "dg"), t + 1)
                pe.matmul(ps[:, 3, 0:2 * P], ones, diag.rearrange("p n k -> p (n k)"), start=True, stop=True)\
                  .then_inc(s(lv.name + "pb"), 1)
                pe.wait_ge(s(lv.name + "pbe"), t + 1)
                pe.wait_ge(s(lv.name + "row"), t * 16 + 16)
                apart(pe, SPARE)

            def experts(at):
                return nc.values_load_multi_w_load_instructions(
                    row[0:1, bass.ds(at, 8)], engines=PE_ONLY, min_val=0, max_val=E - 1,
                    skip_runtime_bounds_check_because="indices of a maximum over 64 logits")[1]

            def first(lv, st, z, chosen):
                for k in range(2 * HALF):
                    last = pe.matmul(ps[0:lv.j, z, k * lv.n1:(k + 1) * lv.n1],
                                     st[:, (k // 2) * lv.j:(k // 2 + 1) * lv.j],
                                     lv.ta.rearrange("p e o -> p (e o)")[:, bass.ds(chosen[k] * lv.n1, lv.n1)],
                                     start=True, stop=True)
                return last

            def second(lv, md, bank, z, chosen):
                for k in range(2 * HALF):
                    t = z * HALF + k // 2
                    last = pe.matmul(ps[0:lv.n1, bank, t * lv.n2:(t + 1) * lv.n2],
                                     md[:, k * lv.n1:(k + 1) * lv.n1],
                                     lv.tb.rearrange("p e o -> p (e o)")[:, bass.ds(chosen[k] * lv.n2, lv.n2)],
                                     start=k % 2 == 0, stop=k % 2 == 1)
                return last
            pe.wait_ge(s_t, 160)
            pe.wait_ge(s_zd, 8)
            pe.wait_ge(s_z, 6)
            with pe.Fori(0, QUADS) as t:
                pe.wait_ge(s("x3s"), t + 1)
                pe.wait_ge(s("res"), t * 2)
                for c in range(8):
                    last = pe.transpose(ps[:, c // 4, (c % 4) * P:(c % 4 + 1) * P], x3s[:, c * P:(c + 1) * P], ident)
                    if c % 4 == 3:
                        last.then_inc(s("xf"), 1)
                x3v = x3s.rearrange("n (i j) -> n i j", j=D1)
                for k in range(8):
                    if k == 2:
                        pe.wait_ge(s("xfe_d"), t + 1)
                        pe.wait_ge(s("xfe_a"), t + 1)
                        for c in range(8):
                            last = pe.matmul(ps[:, 2, 0:E], xft[:, c, :], wr_up[:, c, :], start=c == 0, stop=c == 7)
                        last.then_inc(s("uplg"), 1)
                    if k >= 2:
                        pe.wait_ge(s("xse_d" if k % 2 else "xse_a"), t * 4 + k // 2)
                    for j in range(4):
                        last = pe.transpose(ps[0:D1, 4 + k % 2, j * P:(j + 1) * P], x3v[:, :, 4 * k + j], ident)
                    last.then_inc(s("xst"), 1)
                spread(UP, t)
                with pe.Fori(0, NSTEP // 2) as i:
                    for u in range(2):
                        n = t * NSTEP + i * 2 + u
                        chosen = []
                        for z in range(2):
                            chosen.append(experts((i * 2 + u) * (2 * STEP) + z * 2 * HALF))
                            pe.wait_ge(s("upst"), n * 2 + z + 1)
                            first(UP, stage["up"][z], z, chosen[z]).then_inc(s("ups1"), 1)
                        pe.wait_ge(s("hb"), n)
                        for z in range(2):
                            pe.wait_ge(s("upm"), n * 2 + z + 1)
                            second(UP, mid["up"][z], 6 + u, z, chosen[z]).then_inc(s("ups2"), 1)
                pe.nop().then_inc(s("uploaded"), 1)
                pe.wait_ge(s("gelu"), (t + 1) * NSTEP)
                apart(pe, SPARE)
                for p in range(F1):
                    b = p % 2
                    last = pe.matmul(ps[b * E:(b + 1) * E, 3, 0:P], wr_dn[0:F1, p, :], h[0:F1, :, p],
                                     start=p < 2, stop=p >= F1 - 2)
                last.then_inc(s("lt"), 1)
                pe.wait_ge(s("lte"), t + 1)
                pe.matmul(ps[:, 2, 0:E], lt, fold, start=True, stop=True).then_inc(s("dnlg"), 1)
                spread(DN, t)
                with pe.Fori(0, NSTEP) as i:
                    n = t * NSTEP + i
                    chosen = []
                    for z in range(2):
                        chosen.append(experts(i * (2 * STEP) + z * 2 * HALF))
                        pe.wait_ge(s("dnst"), n * 2 + z + 1)
                        first(DN, stage["dn"][z], z, chosen[z]).then_inc(s("dns1"), 1)
                    pe.wait_ge(s("ye"), n)
                    for z in range(2):
                        pe.wait_ge(s("dnm"), n * 2 + z + 1)
                        last = second(DN, mid["dn"][z], 6, z, chosen[z])
                    last.then_inc(s("dns2"), 1)
                pe.nop().then_inc(s("dnloaded"), 1)
                pe.wait_ge(s("ye"), (t + 1) * NSTEP)
                apart(pe, SPARE)
                for p in range(D1):
                    last = pe.transpose(ps[:, 4 + p // 16, (p % 16) * D1:(p % 16 + 1) * D1],
                                        ybuf[0:D1, :, p], ident[0:D1, 0:D1])
                    if p % 16 == 15:
                        last.then_inc(s("y"), 1)


_IN = ["x", "ctx", "wq", "wk", "bq", "bk", "bv", "xwv", "swq", "swk", "swv", "swo", "bo", "db",
       "wr_up", "wr_dn", "ta_up", "tb_up", "ta_dn", "tb_dn", "b_up", "b_dn", "s_up", "s_dn"]


def kernel(x, ctx_1024, L0_xattn_Wq, L0_xattn_bq, L0_xattn_Wk, L0_xattn_bk, L0_xattn_Wv, L0_xattn_bv,
           L0_attn_Wq, L0_attn_Wk, L0_attn_Wv, L0_attn_Wo, L0_attn_bo, L0_attn_denom_bias,
           L0_ffn_W_up, L0_ffn_A_up, L0_ffn_B_up, L0_ffn_scale_up, L0_ffn_bias_up,
           L0_ffn_W_down, L0_ffn_A_down, L0_ffn_B_down, L0_ffn_scale_down, L0_ffn_bias_down):
    import numpy as np
    import concourse.bacc as bacc
    from concourse.bass_utils import run_bass_kernel_spmd

    def column(b):
        return np.asarray(b).reshape(DC, P).T

    def factor(w):
        return np.asarray(w).transpose(2, 0, 1)

    laid = {
        "x": np.asarray(x).reshape(SEQS * SEQ, D), "ctx": ctx_1024, "wq": L0_xattn_Wq, "wk": L0_xattn_Wk,
        "bq": column(L0_xattn_bq), "bk": column(L0_xattn_bk), "bv": np.asarray(L0_xattn_bv).reshape(1, D),
        "xwv": np.asarray(L0_xattn_Wv).T, "swq": np.asarray(L0_attn_Wq).T, "swk": np.asarray(L0_attn_Wk).T,
        "swv": np.asarray(L0_attn_Wv).T, "swo": np.asarray(L0_attn_Wo).T,
        "bo": np.asarray(L0_attn_bo).reshape(1, D), "db": np.asarray(L0_attn_denom_bias).reshape(1, HEADS),
        "wr_up": np.asarray(L0_ffn_W_up).T,
        "wr_dn": np.asarray(L0_ffn_W_down).reshape(E, F1, F1).transpose(1, 2, 0),
        "ta_up": factor(L0_ffn_A_up), "tb_up": factor(L0_ffn_B_up),
        "ta_dn": factor(L0_ffn_A_down), "tb_dn": factor(L0_ffn_B_down),
        "b_up": np.asarray(L0_ffn_bias_up).reshape(F1, F1), "b_dn": np.asarray(L0_ffn_bias_down).reshape(1, 2 * D),
        "s_up": np.asarray(L0_ffn_scale_up).reshape(1, 1), "s_dn": np.asarray(L0_ffn_scale_down).reshape(1, 1),
    }
    nc = bacc.Bacc("TRN2", target_bir_lowering=False, num_devices=1)
    arrays, a = {}, {}
    for name in _IN:
        v = np.ascontiguousarray(laid[name])
        arrays[name] = v
        a[name] = nc.dram_tensor(name, v.shape, mybir.dt.from_np(v.dtype), kind="ExternalInput").ap()
    a["choice"] = nc.dram_tensor("choice", (P, 2), U32, kind="Internal").ap()
    out = nc.dram_tensor("out", (SEQS * SEQ, D), F32, kind="ExternalOutput").ap()
    program(nc, a, out)
    r = run_bass_kernel_spmd(nc, [arrays], core_ids=[0])
    return r.results[0]["out"].reshape(SEQS, SEQ, D)
```

```python
from contextlib import ExitStack
from math import prod

import concourse.bass as bass
from concourse import mybir

F32 = mybir.dt.float32
U32 = mybir.dt.uint32
ALU = mybir.AluOpType
ACT = mybir.ActivationFunctionType
AX = mybir.AxisListType
SPARE = {}
PE_ONLY = [mybir.EngineType.PE]

P = 128
SEQS, SEQ, D, CTX = 32, 64, 512, 1601
DC = D // P
QUADS = SEQS // 4
QROWS = 4 * SEQ
EPS = 1e-5
HEADS = 16
HD = D // HEADS
HPC = P // HD
E = 64
D1, F1 = 32, 64
FULL = CTX // P
REST = CTX - FULL * P
TILES = FULL + 1
GROUPS = 4
GT = 4
MASKED = -3.0e38


def apart(e, spare):
    e.sem_inc(spare[e.engine], 1)


def group_tiles(g):
    return range(GT * g, min(GT * g + GT, TILES))


def tile_rows(j):
    return P if j < FULL else REST


def group_cols(g):
    return sum(tile_rows(j) for j in group_tiles(g))


def program(nc, a, out):
    ctx = ExitStack()
    with ctx:
        arena = ctx.enter_context(nc.sbuf_tensor("arena", [P, 53200], F32))
        ps = ctx.enter_context(nc.psum_tensor("ps", [P, 8, 512], F32))

        def sem(name):
            return ctx.enter_context(nc.semaphore(name))

        class Area:

            def __init__(self, at):
                self.at = at

            def __call__(self, *dims, dt=F32):
                n = prod(dims)
                v = arena[:, self.at:self.at + n]
                self.at += n
                assert self.at <= 53200, self.at
                if dt != F32:
                    v = v.bitcast(dt)
                if len(dims) == 1:
                    return v
                names = "abcd"[:len(dims)]
                return v.rearrange(f"p ({' '.join(names)}) -> p {' '.join(names)}",
                                   **{k: d for k, d in zip(names[1:], dims[1:])})

        for n, e in (("pe", nc.tensor), ("dve", nc.vector), ("pool", nc.gpsimd)):
            SPARE[e.engine] = sem("spare_" + n)
        keep = Area(0)
        ident = keep(P)
        qa = keep(DC, SEQS * SEQ)
        qbias = keep(2 * QUADS)
        halves = keep(2)
        after_keep = keep.at

        prepare(nc, sem, Area(after_keep), ps, a, ident, qa, qbias, halves)
        cross(nc, sem, Area(after_keep), ps, a, ident, qa, qbias)
        late = Area(after_keep)
        tables = {"up": [late(F1, 2, D1) for _ in range(2)], "dn": [late(D1, F1) for _ in range(2)],
                  "wr_up": late(8, E), "b_up": late(F1), "scales": late(2), "iota": late(E)}
        self_attention(nc, sem, Area(late.at), ps, a, ident, qa, halves, tables)
        mixture(nc, sem, Area(late.at), ps, a, ident, qa.rearrange("p c n -> p (c n)"), tables, out)


def layer_norm_stats(vec, stats, mv, x, s_stat, s_mv, n0):
    for par in range(2):
        vec.bn_stats(stats[:, par, :], x[:, par * D:(par + 1) * D]).then_inc(s_stat, 1)
    vec.wait_ge(s_stat, n0 * 2 + 2)
    apart(vec, SPARE)
    for par in range(2):
        vec.bn_aggr(mv[:, par, :], stats[:, par, :]).then_inc(s_mv, 1)


def layer_norm_rstd(pool, mv, veps, rstd, halves, s_mv, s_veps, s_rstd, n0):
    apart(pool, SPARE)
    pool.tensor_scalar(veps[:, :], mv[:, :, 1], EPS, None, ALU.add).then_inc(s_veps, 1)
    pool.wait_ge(s_veps, n0 + 1)
    pool.tensor_tensor(rstd[:, :], veps[:, :], halves[:, :], ALU.pow).then_inc(s_rstd, 1)


def prepare(nc, sem, area, ps, a, ident, qa, qbias, halves):
    wq, wk = area(DC, D), area(DC, D)
    wqk = area(DC, D)
    bqc, bkc = area(DC), area(DC)
    bq_wide = area(DC, P)
    cols = area(2 * DC)
    xt = [area(2 * D) for _ in range(2)]
    xn = [area(2 * D) for _ in range(2)]
    lnt = [area(DC, QROWS) for _ in range(2)]
    stats, mv = area(2, 6), area(2, 2)
    veps, rstd = area(2), area(2)
    x_h = a["x"].rearrange("(q n r) d -> q n (r d)", q=QUADS, r=2)

    s_w, s_b = sem("pr_w"), sem("pr_b")
    s_x = [sem(f"pr_x{u}") for u in range(2)]
    s_id0, s_id, s_wide = sem("pr_id0"), sem("pr_id"), sem("pr_wide")
    s_half = sem("pr_half")
    s_fuse, s_fused = sem("pr_fuse"), sem("pr_fused")
    s_col, s_cold = sem("pr_col"), sem("pr_cold")
    s_stat, s_mv, s_veps, s_rstd, s_xn = (sem("pr_" + n) for n in ("stat", "mv", "veps", "rstd", "xn"))
    s_t, s_te, s_q, s_qe, s_r, s_re = (sem("pr_" + n) for n in ("t", "te", "q", "qe", "r", "re"))

    with nc.Block() as block:
        @block.sync
        def _(sp):
            sp.dma_start(wq, a["wq"].rearrange("(c p) d -> p c d", p=P)).then_inc(s_w, 16)
            sp.dma_start(wk, a["wk"].rearrange("(c p) d -> p c d", p=P)).then_inc(s_w, 16)
            sp.dma_start(bqc, a["bq"]).then_inc(s_b, 16)
            sp.dma_start(bkc, a["bk"]).then_inc(s_b, 16)
            for u in range(2):
                sp.dma_start(xt[u], x_h[u, :, :]).then_inc(s_x[u], 16)
            with sp.Fori(0, QUADS // 2 - 1) as i:
                for u in range(2):
                    sp.wait_ge(s_xn, i * 4 + 2 * u + 2)
                    sp.dma_start(xt[u], x_h[bass.ds(i * 2 + u + 2, 1), :, :].rearrange("q n d -> n (q d)"))\
                      .then_inc(s_x[u], 16)

        @block.gpsimd
        def _(pool):
            pool.memset(ident, 0.0).then_inc(s_id0, 1)
            pool.memset(halves, -0.5).then_inc(s_half, 1)
            pool.wait_ge(s_id0, 1)
            pool.affine_select(out=ident, in_=ident, compare_op=ALU.not_equal, fill=1.0, base=0,
                               pattern=[[-1, P]], channel_multiplier=1).then_inc(s_id, 1)
            pool.wait_ge(s_half, 1)
            with pool.Fori(0, QUADS // 2) as i:
                for u in range(2):
                    pool.wait_ge(s_mv, i * 4 + 2 * u + 2)
                    layer_norm_rstd(pool, mv, veps, rstd, halves, s_mv, s_veps, s_rstd, i * 2 + u)

        @block.vector
        def _(vec):
            vec.wait_ge(s_b, 32)
            for c in range(DC):
                vec.tensor_copy(bq_wide[:, c, :], bqc[:, c:c + 1].to_broadcast([P, P])).then_inc(s_wide, 1)
            for m in range(DC):
                vec.wait_ge(s_fuse, m + 1)
                vec.tensor_copy(wqk[:, m, :], ps[:, m, :]).then_inc(s_fused, 1)
            vec.wait_ge(s_col, 1)
            vec.tensor_copy(cols, ps[:, 4, 0:2 * DC]).then_inc(s_cold, 1)
            with vec.Fori(0, QUADS // 2) as i:
                for u in range(2):
                    n = i * 2 + u
                    vec.wait_ge(s_x[u], i * 16 + 16)
                    layer_norm_stats(vec, stats, mv, xt[u], s_stat, s_mv, n)
                    vec.wait_ge(s_rstd, n + 1)
                    vec.wait_ge(s_mv, n * 2 + 2)
                    for par in range(2):
                        vec.tensor_scalar(xn[u][:, par * D:(par + 1) * D], xt[u][:, par * D:(par + 1) * D],
                                          mv[:, par, 0:1], rstd[:, par:par + 1], ALU.subtract, ALU.mult)\
                           .then_inc(s_xn, 1)
                    vec.wait_ge(s_r, n + 1)
                    vec.tensor_copy(qbias[:, bass.ds(n * 2, 2)], ps[:, 4, 16:18]).then_inc(s_re, 1)

        @block.scalar
        def _(act):
            act.wait_ge(s_cold, 1)
            with act.Fori(0, QUADS // 2) as i:
                for u in range(2):
                    n = i * 2 + u
                    for par in range(2):
                        act.wait_ge(s_t, n * 2 + par + 1)
                        act.copy(lnt[u][:, :, par::2], ps[:, 5 + par, :].rearrange("p (c n) -> p c n", c=DC))\
                           .then_inc(s_te, 1)
                    for m in range(DC):
                        act.wait_ge(s_q, n * DC + m + 1)
                        act.activation(qa[:, m, bass.ds(n * QROWS, QROWS)], ps[:, m, 0:QROWS],
                                       ACT.Identity, bias=cols[:, m:m + 1]).then_inc(s_qe, 1)

        @block.tensor
        def _(pe):
            pe.wait_ge(s_w, 32)
            for m in range(DC):
                for c in range(DC):
                    last = pe.matmul(ps[:, m, :], wq[:, c, m * P:(m + 1) * P], wk[:, c, :],
                                     start=c == 0, stop=c == DC - 1)
                last.then_inc(s_fuse, 1)
            pe.wait_ge(s_b, 32)
            for k, (w, b) in enumerate(((wk, bqc), (wq, bkc))):
                for m in range(DC):
                    for c in range(DC):
                        last = pe.matmul(ps[:, 4, k * DC + m:k * DC + m + 1], w[:, c, m * P:(m + 1) * P],
                                         b[:, c:c + 1], start=c == 0, stop=c == DC - 1)
            last.then_inc(s_col, 1)
            pe.wait_ge(s_id, 1)
            pe.wait_ge(s_fused, DC)
            pe.wait_ge(s_cold, 1)
            pe.wait_ge(s_wide, DC)
            with pe.Fori(0, QUADS // 2) as i:
                for u in range(2):
                    n = i * 2 + u
                    for par in range(2):
                        pe.wait_ge(s_xn, n * 2 + par + 1)
                        pe.wait_ge(s_te, n * 2)
                        for c in range(DC):
                            last = pe.transpose(ps[:, 5 + par, c * P:(c + 1) * P],
                                                xn[u][:, par * D + c * P:par * D + (c + 1) * P], ident)
                        last.then_inc(s_t, 1)
                    pe.wait_ge(s_te, n * 2 + 2)
                    for m in range(DC):
                        pe.wait_ge(s_qe, n * DC)
                        for c in range(DC):
                            last = pe.matmul(ps[:, m, 0:QROWS], wqk[:, c, m * P:(m + 1) * P],
                                             lnt[u][:, c, :], start=c == 0, stop=c == DC - 1)
                        last.then_inc(s_q, 1)
                    pe.wait_ge(s_re, n)
                    for pair in range(2):
                        o = ps[:, 4, 16 + pair:17 + pair]
                        for c in range(DC):
                            pe.matmul(o, lnt[u][:, c, pair * P:(pair + 1) * P], cols[:, DC + c:DC + c + 1],
                                      start=c == 0, stop=False)
                        for c in range(DC):
                            last = pe.matmul(o, bq_wide[:, c, :], bkc[:, c:c + 1],
                                             start=False, stop=c == DC - 1)
                    last.then_inc(s_r, 1)


def cross(nc, sem, area, ps, a, ident, qa, qbias):
    ct = [area(2, TILES, D) for _ in range(2)]
    xt = [area(2, DC, GT * P) for _ in range(2)]
    qs = [area(DC, P) for _ in range(2)]
    prob = area(CTX)
    probt = area(TILES, P)
    att = area(D)
    mx, sums = area(GROUPS), area(GROUPS)
    top, shifted, bias = area(1), area(1), area(1)
    total, recip = area(1), area(1)
    c_main = a["ctx"][:, 0:FULL * P, :].rearrange("s (p j) d -> s p j d", j=FULL)
    c_rest = a["ctx"][:, FULL * P:CTX, :]

    s_c = [[sem(f"cr_c{u}{g}") for g in range(GROUPS)] for u in range(2)]
    s_fill, s_ea, s_ed = sem("cr_fill"), sem("cr_ea"), sem("cr_ed")
    s_s, s_pv = sem("cr_s"), sem("cr_pv")
    s_mx, s_top, s_sh, s_bias = sem("cr_mx"), sem("cr_top"), sem("cr_sh"), sem("cr_bias")
    s_exp, s_tot, s_rec = sem("cr_exp"), sem("cr_tot"), sem("cr_rec")
    s_att, s_at, s_ate, s_qs = sem("cr_att"), sem("cr_at"), sem("cr_ate"), sem("cr_qs")
    TB, OB, AB = 4, 6, 7
    PIECES = 2 * DC
    PTF = GROUPS
    FILLS = GROUPS * PIECES + PTF
    PAIRS = SEQS // 2

    def filled_before(p):
        return p * FILLS + 2 * PIECES

    def pair_fills(last):
        f = [("ctx", g, c, b) for g in range(2 if last else GROUPS) for c in range(DC) for b in range(2)]
        return f + [("prob", g) for g in range(GROUPS)]

    with nc.Block() as block:
        @block.sync
        def _(sp):
            def load(u, pair, static):
                for g in range(GROUPS):
                    for b in range(2):
                        seq = pair * 2 + b
                        if g < GROUPS - 1:
                            src = c_main[bass.ds(seq, 1), :, GT * g:GT * (g + 1), :].rearrange("s p j d -> p (s j) d")
                            dst = ct[u][:, b, GT * g:GT * (g + 1), :]
                        else:
                            src = c_rest[bass.ds(seq, 1), :, :].rearrange("s p d -> p (s d)")
                            dst = ct[u][0:REST, b, FULL, :]
                        sp.dma_start(dst, src).then_inc(s_c[u][g], 16)
            for u in range(2):
                load(u, u, True)
            with sp.Fori(0, PAIRS // 2 - 1) as i:
                for u in range(2):
                    sp.wait_ge(s_pv, i * 2 + u + 1)
                    load(u, i * 2 + u + 2, False)

        @block.gpsimd
        def _(pool):
            for u in range(2):
                pool.tensor_copy(qs[u], qa[:, :, u * P:(u + 1) * P]).then_inc(s_qs, 1)
            with pool.Fori(0, PAIRS // 2 - 1) as i:
                for u in range(2):
                    pool.wait_ge(s_s, (i * 2 + u + 1) * GROUPS * DC)
                    pool.tensor_copy(qs[u], qa[:, :, bass.ds((i * 2 + u + 2) * P, P)]).then_inc(s_qs, 1)

        def evacuate(e, copy, p, k, what, s_done):
            src = ps[:, TB + k % 2, :]
            e.wait_ge(s_fill, filled_before(p) + k + 1)
            if what[0] == "ctx":
                _, g, c, b = what
                e.wait_ge(s_s, p * GROUPS * DC + g * DC + c + 1)
                w = group_cols((g + 2) % GROUPS)
                copy(xt[g % 2][:, b, c, 0:w], src[:, 0:w]).then_inc(s_done, 1)
            else:
                g = what[1]
                e.wait_ge(s_pv, p)
                if g < GROUPS - 1:
                    copy(probt[:, GT * g:GT * (g + 1), :], src).then_inc(s_done, 1)
                else:
                    copy(probt[0:REST, FULL, :], src[0:REST, 0:P]).then_inc(s_done, 1)

        def first_fills(e, copy, parity, s_done):
            for k in range(parity, 2 * PIECES, 2):
                g, c, b = k // PIECES, k % PIECES // 2, k % 2
                e.wait_ge(s_fill, k + 1)
                copy(xt[g][:, b, c, :], ps[:, TB + k % 2, :]).then_inc(s_done, 1)

        @block.scalar
        def _(act):
            first_fills(act, act.copy, 0, s_ea)

            def pair(i, u, last):
                p = i * 2 + u
                fills = pair_fills(last)
                for k, what in enumerate(fills):
                    if k % 2 == 0 and what[0] == "ctx":
                        evacuate(act, act.copy, p, k, what, s_ea)
                act.wait_ge(s_bias, p + 1)
                act.wait_ge(s_fill, filled_before(p))
                for g in range(GROUPS):
                    w = group_cols(g)
                    act.activation(prob[:, g * GT * P:g * GT * P + w], ps[:, g, 0:w], ACT.Exp,
                                   bias=bias[:, 0:1], accum_out=sums[:, g:g + 1]).then_inc(s_exp, 1)
                for k, what in enumerate(fills):
                    if k % 2 == 0 and what[0] == "prob":
                        evacuate(act, act.copy, p, k, what, s_ea)
                act.wait_ge(s_pv, p + 1)
                act.wait_ge(s_rec, p + 1)
                act.wait_ge(s_at, p)
                act.activation(att, ps[:, OB, :], ACT.Copy, scale=recip[:, 0:1]).then_inc(s_att, 1)
            with act.Fori(0, PAIRS // 2 - 1) as i:
                for u in range(2):
                    pair(i, u, False)
            for u in range(2):
                pair(PAIRS // 2 - 1, u, u == 1)

        @block.vector
        def _(vec):
            first_fills(vec, vec.tensor_copy, 1, s_ed)

            def attended(p):
                vec.wait_ge(s_at, p + 1)
                vec.wait_ge(s_qs, p + 1)
                vec.tensor_copy(qa[:, :, bass.ds(p * P, P)],
                                ps[:, AB, :].rearrange("p (c n) -> p c n", c=DC)).then_inc(s_ate, 1)

            def pair(i, u, last, first):
                p = i * 2 + u
                fills = pair_fills(last)
                for g in range(GROUPS):
                    for k, what in enumerate(fills):
                        if k % 2 == 1 and what[0] == "ctx" and what[1] == g:
                            evacuate(vec, vec.tensor_copy, p, k, what, s_ed)
                    vec.wait_ge(s_s, p * GROUPS * DC + (g + 1) * DC)
                    vec.reduce_max(mx[:, g:g + 1], ps[:, g, 0:group_cols(g)], AX.X).then_inc(s_mx, 1)
                    if g == 0 and not first:
                        attended(p - 1)
                vec.wait_ge(s_mx, (p + 1) * GROUPS)
                vec.reduce_max(top, mx, AX.X).then_inc(s_top, 1)
                vec.wait_ge(s_top, p + 1)
                vec.tensor_tensor(shifted, top, qbias[:, bass.ds(p, 1)], ALU.add).then_inc(s_sh, 1)
                vec.wait_ge(s_sh, p + 1)
                vec.tensor_tensor(bias, qbias[:, bass.ds(p, 1)], shifted, ALU.subtract).then_inc(s_bias, 1)
                for k, what in enumerate(fills):
                    if k % 2 == 1 and what[0] == "prob":
                        evacuate(vec, vec.tensor_copy, p, k, what, s_ed)
                vec.wait_ge(s_exp, (p + 1) * GROUPS)
                vec.reduce_sum(total, sums, AX.X).then_inc(s_tot, 1)
                vec.wait_ge(s_tot, p + 1)
                vec.wait_ge(s_att, p)
                vec.reciprocal(recip, total).then_inc(s_rec, 1)
            for u in range(2):
                pair(0, u, False, u == 0)
            with vec.Fori(1, PAIRS // 2 - 1) as i:
                for u in range(2):
                    pair(i, u, False, False)
            for u in range(2):
                pair(PAIRS // 2 - 1, u, u == 1, False)
            attended(PAIRS - 1)

        @block.tensor
        def _(pe):
            def free_bank(n, k):
                if k % 2 == 0:
                    pe.wait_ge(s_ea, n)
                else:
                    pe.wait_ge(s_ed, n)

            def transpose_group(u, g, c, b, k):
                for j in group_tiles(g):
                    r = tile_rows(j)
                    at = (j - GT * g) * P
                    last = pe.transpose(ps[:, TB + k % 2, at:at + r],
                                        ct[u][0:r, b, j, c * P:(c + 1) * P], ident[0:r, 0:r])
                last.then_inc(s_fill, 1)

            for g in range(2):
                pe.wait_ge(s_c[0][g], 32)
                for k in range(PIECES):
                    n = g * PIECES + k
                    if n >= 2:
                        free_bank(n // 2, n)
                    transpose_group(0, g, k // 2, k % 2, n)

            def transpose_attended(p):
                pe.wait_ge(s_att, p + 1)
                pe.wait_ge(s_ate, p)
                for c in range(DC):
                    last = pe.transpose(ps[:, AB, c * P:(c + 1) * P], att[:, c * P:(c + 1) * P], ident)
                last.then_inc(s_at, 1)

            def pair(i, u, last, first):
                p = i * 2 + u
                half = p * (FILLS // 2) + PIECES
                pe.wait_ge(s_qs, p + 1)
                k = 0
                for g in range(GROUPS):
                    w = group_cols(g)
                    ahead = (g + 2) % GROUPS
                    if g < 2:
                        pe.wait_ge(s_c[u][ahead], i * 32 + 32)
                    elif not last:
                        nxt = (i if u == 0 else i + 1)
                        pe.wait_ge(s_c[1 - u][ahead], nxt * 32 + 32)
                    for c in range(DC):
                        done = half + (g - 2) * DC + c + 1
                        pe.wait_ge(s_ea, done)
                        pe.wait_ge(s_ed, done)
                        for b in range(2):
                            x = pe.matmul(ps[b * SEQ:(b + 1) * SEQ, g, 0:w], qs[u][:, c, b * SEQ:(b + 1) * SEQ],
                                          xt[g % 2][:, b, c, 0:w], start=c == 0, stop=c == DC - 1)
                        x.then_inc(s_s, 1)
                        if g < 2 or not last:
                            for b in range(2):
                                free_bank(half + k // 2, k)
                                transpose_group(u if g < 2 else 1 - u, ahead, c, b, k)
                                k += 1
                    if g == 0 and not first:
                        transpose_attended(p - 1)
                k0 = k
                for g in range(GROUPS):
                    pe.wait_ge(s_exp, p * GROUPS + g + 1)
                    free_bank(half + k // 2, k)
                    for j in group_tiles(g):
                        r = tile_rows(j)
                        x = pe.transpose(ps[0:r, TB + k % 2, (j - GT * g) * P:(j - GT * g + 1) * P],
                                         prob[:, j * P:j * P + r], ident)
                    x.then_inc(s_fill, 1)
                    k += 1
                for j in range(TILES):
                    if j % GT == 0:
                        kk = k0 + j // GT
                        (pe.wait_ge(s_ea, half + kk // 2 + 1) if kk % 2 == 0 else
                         pe.wait_ge(s_ed, half + kk // 2 + 1))
                    r = tile_rows(j)
                    for b in range(2):
                        x = pe.matmul(ps[b * SEQ:(b + 1) * SEQ, OB, :], probt[0:r, j, b * SEQ:(b + 1) * SEQ],
                                      ct[u][0:r, b, j, :], start=j == 0, stop=j == TILES - 1)
                x.then_inc(s_pv, 1)
            for u in range(2):
                pair(0, u, False, u == 0)
            with pe.Fori(1, PAIRS // 2 - 1) as i:
                for u in range(2):
                    pair(i, u, False, False)
            for u in range(2):
                pair(PAIRS // 2 - 1, u, u == 1, False)
            transpose_attended(PAIRS - 1)


def self_attention(nc, sem, area, ps, a, ident, qa, halves, tables):
    w_names = ("xwv", "swq", "swk", "swv", "swo")
    w = {n: area(DC, D) for n in w_names}
    bv, bo = area(D), area(D)
    mask = area(P)
    expdb = area(HEADS)
    ats = area(DC, QROWS)
    x = [area(2 * D) for _ in range(2)]
    x1, xn = area(2 * D), area(2 * D)
    x2b, b_dn = area(2 * D), area(2 * D)
    lnt, qt = area(DC, QROWS), area(DC, QROWS)
    kd = area(DC, HPC, QROWS)
    v = area(2, D)
    sc = [area(HPC, P) for _ in range(3)]
    pt = [area(HPC, P) for _ in range(2)]
    aot = area(DC, QROWS)
    nmx, rs = [area(HPC) for _ in range(3)], [area(HPC) for _ in range(3)]
    den, rden = [area(HPC) for _ in range(3)], [area(HPC) for _ in range(3)]
    stats, mv, veps, rstd = area(2, 6), area(2, 2), area(2), area(2)
    x_h = a["x"].rearrange("(q n r) d -> q n (r d)", q=QUADS, r=2)
    ITEMS = 2 * DC
    SCALE = HD ** -0.5

    s_w, s_c, s_x = sem("se_w"), sem("se_c"), [sem(f"se_x{u}") for u in range(2)]
    names = ("kd0", "m0", "m1", "edb", "ats", "p1", "r1", "x1b", "stat", "mv", "veps", "rstd", "xn", "lt", "lte",
             "q", "qe", "k", "ke", "v", "ve", "s", "sm", "mx", "ex", "den", "rd", "nrm", "pt", "pte_a", "pte_d",
             "pv", "pve", "o", "r2", "x2", "stat2", "mv2", "veps2", "rstd2", "x3", "stored", "z", "t", "tb", "out")
    S = {n: sem("se_" + n) for n in names}

    with nc.Block() as block:
        @block.sync
        def _(sp):
            sp.dma_start(w["xwv"], a["xwv"].rearrange("(c p) e -> p c e", p=P)).then_inc(s_w, 16)
            sp.dma_start(bv, a["bv"].to_broadcast([P, D])).then_inc(s_c, 16)
            for u in range(2):
                sp.dma_start(x[u], x_h[u, :, :]).then_inc(s_x[u], 16)
            for n in w_names[1:]:
                sp.dma_start(w[n], a[n].rearrange("(c p) e -> p c e", p=P)).then_inc(s_w, 16)
            sp.dma_start(bo, a["bo"].to_broadcast([P, D])).then_inc(s_c, 16)
            sp.dma_start(expdb, a["db"].to_broadcast([P, HEADS])).then_inc(s_c, 16)
            sp.dma_start(b_dn, a["b_dn"].to_broadcast([P, 2 * D])).then_inc(s_c, 16)
            sp.wait_ge(S["z"], 2)
            for k in range(2):
                r = slice(k * E, (k + 1) * E)
                for v, (up, dn) in enumerate((("a_up", "a_dn"), ("b_up_f", "b_dn_f"))):
                    sp.dma_start(tables["up"][v][r, :, k, :], a[up]).then_inc(S["t"], 16)
                    sp.dma_start(tables["dn"][v][r, :, :], a[dn]).then_inc(S["t"], 16)
                sp.dma_start(tables["b_up"][r, :], a["b_up"]).then_inc(S["t"], 16)
                sp.dma_start(tables["scales"][:, k:k + 1], a[("s_up", "s_dn")[k]].to_broadcast([P, 1]))\
                  .then_inc(S["t"], 16)
            sp.dma_start(tables["wr_up"], a["wr_up"].rearrange("(c p) e -> p c e", p=P)).then_inc(S["t"], 16)
            sp.dma_start(tables["iota"], a["iota"].to_broadcast([P, E])).then_inc(S["t"], 16)

            def quad(i, u, more):
                q = i * 2 + u
                if more:
                    sp.wait_ge(S["r1"], (q + 1) * 2)
                    sp.dma_start(x[u], x_h[bass.ds(q + 2, 1), :, :].rearrange("q n d -> n (q d)"))\
                      .then_inc(s_x[u], 16)
                sp.wait_ge(S["x3"], (q + 1) * 3)
                for n, v in (("x2", x2b), ("x3", xn)):
                    sp.dma_start(a[n][bass.ds(q, 1), :, :].rearrange("q n d -> n (q d)"), v).then_inc(S["out"], 16)
                sp.wait_ge(S["out"], (q + 1) * 32)
                sp.sem_inc(S["stored"], 1)
            with sp.Fori(0, QUADS // 2 - 1) as i:
                for u in range(2):
                    quad(i, u, True)
            for u in range(2):
                quad(QUADS // 2 - 1, u, False)
            sp.wait_ge(S["t"], 14 * 16)

        @block.gpsimd
        def _(pool):
            pool.memset(kd, 0.0).then_inc(S["kd0"], 1)
            for v in tables["up"]:
                pool.memset(v, 0.0).then_inc(S["z"], 1)
            pool.memset(mask, 0.0).then_inc(S["m0"], 1)
            pool.wait_ge(S["m0"], 1)
            pool.affine_select(out=mask, in_=mask, compare_op=ALU.is_ge, fill=MASKED, base=0,
                               pattern=[[-1, P]], channel_multiplier=1).then_inc(S["m0"], 1)
            pool.wait_ge(S["m0"], 2)
            pool.affine_select(out=mask[SEQ:P, 0:SEQ], in_=mask[SEQ:P, 0:SEQ], compare_op=ALU.is_gt,
                               fill=MASKED, base=-1, pattern=[[0, SEQ]], channel_multiplier=0).then_inc(S["m1"], 1)
            with pool.Fori(0, QUADS) as i:
                pool.wait_ge(S["mv"], i * 2 + 2)
                layer_norm_rstd(pool, mv, veps, rstd, halves, S["mv"], S["veps"], S["rstd"], i)
                for n in range(ITEMS):
                    pool.wait_ge(S["rd"], i * ITEMS + n + 1)
                    pool.tensor_tensor(sc[n % 3], sc[n % 3],
                                       rden[n % 3].unsqueeze(2).to_broadcast([P, HPC, P]), ALU.mult)\
                        .then_inc(S["nrm"], 1)
                pool.wait_ge(S["mv2"], i * 2 + 2)
                layer_norm_rstd(pool, mv, veps, rstd, halves, S["mv2"], S["veps2"], S["rstd2"], i)

        @block.vector
        def _(vec):
            def quad(i, u):
                q = i * 2 + u
                cols = bass.ds(q * QROWS, QROWS)
                vec.wait_ge(S["o"], q * 2)
                vec.tensor_copy(ats, qa[:, :, cols]).then_inc(S["ats"], 1)
                vec.wait_ge(s_x[u], i * 16 + 16)
                for par in range(2):
                    r = slice(par * D, (par + 1) * D)
                    vec.wait_ge(S["p1"], q * 2 + par + 1)
                    vec.tensor_tensor(x1[:, r], ps[:, 2 + par, :], x[u][:, r], ALU.add).then_inc(S["r1"], 1)
                for par in range(2):
                    r = slice(par * D, (par + 1) * D)
                    vec.wait_ge(S["r1"], q * 2 + par + 1)
                    vec.tensor_tensor(x1[:, r], x1[:, r], bv, ALU.add).then_inc(S["x1b"], 1)
                vec.wait_ge(S["x1b"], q * 2 + 2)
                layer_norm_stats(vec, stats, mv, x1, S["stat"], S["mv"], q)
                vec.wait_ge(S["rstd"], q + 1)
                vec.wait_ge(S["mv"], q * 2 + 2)
                vec.wait_ge(S["stored"], q)
                for par in range(2):
                    r = slice(par * D, (par + 1) * D)
                    vec.tensor_scalar(xn[:, r], x1[:, r], mv[:, par, 0:1], rstd[:, par:par + 1],
                                      ALU.subtract, ALU.mult).then_inc(S["xn"], 1)
                for h in range(2):
                    vec.wait_ge(S["q"], q * 2 + h + 1)
                    vec.tensor_copy(qt[:, 2 * h:2 * h + 2, :], ps[:, 2 + h, :].rearrange("p (m n) -> p m n", m=2))\
                       .then_inc(S["qe"], 1)
                for pair in range(2):
                    vec.wait_ge(S["v"], q * 2 + pair + 1)
                    vec.tensor_copy(v[:, pair, :], ps[:, 6 + pair, :]).then_inc(S["ve"], 1)

                def soften(n):
                    vec.wait_ge(S["s"], q * ITEMS + n + 1)
                    if n >= 3:
                        vec.wait_ge(S["pt"], q * ITEMS + n - 2)
                    else:
                        vec.wait_ge(S["pt"], q * ITEMS)
                    vec.scalar_tensor_tensor(sc[n % 3], ps[:, 4 + n % 2, :].rearrange("p (h t) -> p h t", h=HPC),
                                             SCALE, mask.unsqueeze(1).to_broadcast([P, HPC, P]),
                                             ALU.mult, ALU.add).then_inc(S["sm"], 1)
                    vec.wait_ge(S["sm"], q * ITEMS + n + 1)
                    vec.tensor_reduce(nmx[n % 3], sc[n % 3], AX.X, ALU.max, negate=True).then_inc(S["mx"], 1)

                def denominators(n):
                    m = n % DC
                    vec.wait_ge(S["ex"], (q * ITEMS + n + 1) * HPC)
                    vec.tensor_tensor(den[n % 3], rs[n % 3], expdb[:, m * HPC:(m + 1) * HPC], ALU.add)\
                       .then_inc(S["den"], 1)
                    vec.wait_ge(S["den"], q * ITEMS + n + 1)
                    vec.reciprocal(rden[n % 3], den[n % 3]).then_inc(S["rd"], 1)

                def result(n):
                    pair, m = divmod(n, DC)
                    vec.wait_ge(S["pv"], q * ITEMS + n + 1)
                    vec.tensor_copy(aot[:, m, pair * P:(pair + 1) * P], ps[:, 6 + n % 2, 0:P])\
                       .then_inc(S["pve"], 1)
                for n in range(ITEMS + 4):
                    if n < ITEMS:
                        soften(n)
                    if 1 <= n <= ITEMS:
                        denominators(n - 1)
                    if 2 <= n < ITEMS + 2 and (n - 2) % 2:
                        vec.wait_ge(S["pt"], q * ITEMS + n - 1)
                        vec.wait_ge(S["pv"], q * ITEMS + max(n - 3, 0))
                        vec.tensor_copy(pt[(n - 2) % 2], ps[:, n % 2, :].rearrange("p (h t) -> p h t", h=HPC))\
                           .then_inc(S["pte_d"], 1)
                    if n >= 4:
                        result(n - 4)
                for par in range(2):
                    r = slice(par * D, (par + 1) * D)
                    vec.wait_ge(S["o"], q * 2 + par + 1)
                    vec.tensor_tensor(x1[:, r], ps[:, 2 + par, :], x1[:, r], ALU.add).then_inc(S["r2"], 1)
                for par in range(2):
                    r = slice(par * D, (par + 1) * D)
                    vec.wait_ge(S["r2"], q * 2 + par + 1)
                    vec.tensor_tensor(x1[:, r], x1[:, r], bo, ALU.add).then_inc(S["x2"], 1)
                vec.wait_ge(S["x2"], q * 2 + 2)
                layer_norm_stats(vec, stats, mv, x1, S["stat2"], S["mv2"], q)
                vec.tensor_tensor(x2b, x1, b_dn, ALU.add).then_inc(S["x3"], 1)
                vec.wait_ge(S["rstd2"], q + 1)
                vec.wait_ge(S["mv2"], q * 2 + 2)
                for par in range(2):
                    r = slice(par * D, (par + 1) * D)
                    vec.tensor_scalar(xn[:, r], x1[:, r], mv[:, par, 0:1],
                                      rstd[:, par:par + 1], ALU.subtract, ALU.mult).then_inc(S["x3"], 1)
            vec.wait_ge(s_c, 64)
            vec.wait_ge(S["m1"], 1)
            vec.wait_ge(S["edb"], 1)
            with vec.Fori(0, QUADS // 2) as i:
                for u in range(2):
                    quad(i, u)

        @block.scalar
        def _(act):
            act.wait_ge(s_c, 64)
            act.activation(expdb, expdb, ACT.Exp).then_inc(S["edb"], 1)
            act.wait_ge(S["kd0"], 1)
            with act.Fori(0, QUADS) as q:
                for par in range(2):
                    act.wait_ge(S["lt"], q * 2 + par + 1)
                    act.copy(lnt[:, :, par::2], ps[:, par, :].rearrange("p (c n) -> p c n", c=DC))\
                       .then_inc(S["lte"], 1)
                for m in range(DC):
                    act.wait_ge(S["k"], q * 2 + m // 2 + 1)
                    for h in range(HPC):
                        r = slice(h * HD, (h + 1) * HD)
                        act.copy(kd[r, m, h, :], ps[r, 4 + m // 2, (m % 2) * QROWS:(m % 2 + 1) * QROWS])\
                           .then_inc(S["ke"], 1)
                for n in range(ITEMS + 2):
                    if n < ITEMS:
                        act.wait_ge(S["mx"], q * ITEMS + n + 1)
                        for h in range(HPC):
                            act.activation(sc[n % 3][:, h, :], sc[n % 3][:, h, :], ACT.Exp,
                                           bias=nmx[n % 3][:, h:h + 1],
                                           accum_out=rs[n % 3][:, h:h + 1]).then_inc(S["ex"], 1)
                    if n >= 2 and (n - 2) % 2 == 0:
                        act.wait_ge(S["pt"], q * ITEMS + n - 1)
                        act.wait_ge(S["pv"], q * ITEMS + max(n - 3, 0))
                        act.copy(pt[(n - 2) % 2], ps[:, n % 2, :].rearrange("p (h t) -> p h t", h=HPC))\
                           .then_inc(S["pte_a"], 1)

        @block.tensor
        def _(pe):
            pe.wait_ge(s_w, 5 * 16)
            with pe.Fori(0, QUADS) as q:
                pe.wait_ge(S["ats"], q + 1)
                for par in range(2):
                    for c in range(DC):
                        last = pe.matmul(ps[:, 2 + par, :], ats[:, c, par::2], w["xwv"][:, c, :],
                                         start=c == 0, stop=c == DC - 1)
                    last.then_inc(S["p1"], 1)
                for par in range(2):
                    pe.wait_ge(S["xn"], q * 2 + par + 1)
                    for c in range(DC):
                        last = pe.transpose(ps[:, par, c * P:(c + 1) * P],
                                            xn[:, par * D + c * P:par * D + (c + 1) * P], ident)
                    last.then_inc(S["lt"], 1)
                pe.wait_ge(S["lte"], q * 2 + 2)
                for n, bank in (("swq", 2), ("swk", 4)):
                    for m in range(DC):
                        for c in range(DC):
                            last = pe.matmul(ps[:, bank + m // 2, (m % 2) * QROWS:(m % 2 + 1) * QROWS],
                                             w[n][:, c, m * P:(m + 1) * P], lnt[:, c, :],
                                             start=c == 0, stop=c == DC - 1)
                        if m % 2:
                            last.then_inc(S["q" if n == "swq" else "k"], 1)
                for pair in range(2):
                    for c in range(DC):
                        last = pe.matmul(ps[:, 6 + pair, :], lnt[:, c, pair * P:(pair + 1) * P],
                                         w["swv"][:, c, :], start=c == 0, stop=c == DC - 1)
                    last.then_inc(S["v"], 1)
                pe.wait_ge(S["qe"], q * 2 + 2)
                pe.wait_ge(S["ke"], (q + 1) * DC * HPC)
                pe.wait_ge(S["ve"], q * 2 + 2)
                for n in range(ITEMS + 3):
                    if n < ITEMS:
                        pair, m = divmod(n, DC)
                        if n >= 2:
                            pe.wait_ge(S["sm"], q * ITEMS + n - 1)
                        pe.matmul(ps[:, 4 + n % 2, :], qt[:, m, pair * P:(pair + 1) * P],
                                  kd[:, m, :, pair * P:(pair + 1) * P], start=True, stop=True).then_inc(S["s"], 1)
                    if 2 <= n < ITEMS + 2:
                        k = n - 2
                        pe.wait_ge(S["nrm"], q * ITEMS + k + 1)
                        if k >= 2:
                            pe.wait_ge(S["pte_d" if k % 2 else "pte_a"], q * (ITEMS // 2) + k // 2)
                        for h in range(HPC):
                            last = pe.transpose(ps[:, k % 2, h * P:(h + 1) * P], sc[k % 3][:, h, :], ident)
                        last.then_inc(S["pt"], 1)
                    if n >= 3:
                        k = n - 3
                        pair, m = divmod(k, DC)
                        pe.wait_ge(S["pte_d" if k % 2 else "pte_a"], q * (ITEMS // 2) + k // 2 + 1)
                        if k >= 2:
                            pe.wait_ge(S["pve"], q * ITEMS + k - 1)
                        for h in range(HPC):
                            head = m * HPC + h
                            last = pe.matmul(ps[h * HD:(h + 1) * HD, 6 + k % 2, 0:P],
                                             v[:, pair, head * HD:(head + 1) * HD], pt[k % 2][:, h, :],
                                             start=True, stop=True)
                        last.then_inc(S["pv"], 1)
                pe.wait_ge(S["pve"], (q + 1) * ITEMS)
                for par in range(2):
                    for c in range(DC):
                        last = pe.matmul(ps[:, 2 + par, :], aot[:, c, par::2], w["swo"][:, c, :],
                                         start=c == 0, stop=c == DC - 1)
                    last.then_inc(S["o"], 1)


def mixture(nc, sem, area, ps, a, ident, h_at, tables, out):
    tab_up, tab_dn, wr_up, b_up, scales, iota = (tables[n] for n in ("up", "dn", "wr_up", "b_up", "scales", "iota"))
    wr_dn = area(F1, E)
    h = h_at.rearrange("p (g j) -> p g j", j=F1)
    gath = [area(64 * P) for _ in range(2)]
    xrep = area(D1, P)
    x3s = area(2, 2 * D)
    stage = [[area(8 * F1) for _ in range(3)] for _ in range(2)]
    mid = [area(8 * F1) for _ in range(2)]
    oh = area(2, 2, 2, P)
    top, top_i, top_f = area(2, 8), area(2, 8, dt=U32), area(2, 2)
    diff, ex, den, prob = area(2), area(2), area(2), area(2, 2)
    xft = gath[0].rearrange("p (t c n) -> p t c n", t=8, c=8)[:, 0:2]
    lg = gath[1][:, 0:2 * E].rearrange("p (t e) -> p t e", t=2)
    lt = gath[1][:, 2048:2048 + P]
    oht = gath[1][:, 1024:1536].rearrange("p (t v k e) -> p t v k e", t=2, v=2, k=2)
    oh_up = mid[0].rearrange("p (t v g) -> p t v g", t=2, v=2)
    x2b = xrep.rearrange("p j g -> p (j g)")[:, 0:2 * 2 * D].rearrange("p (t f) -> p t f", t=2)
    ybuf = xrep.rearrange("p j g -> p (j g)")[:, 4 * D:8 * D].rearrange("p (t g o) -> p t g o", t=2, o=D1)
    yt = h_at[:, 0:4 * D].rearrange("p (t o q) -> p t o q", t=2, o=D1)
    NT = QUADS // 2
    G8, NS = 8, P // 8
    XBANK = (0, 1, 2, 3, 6, 7, 0, 1)
    GB = 16

    S = {}

    def s(n):
        if n not in S:
            S[n] = sem("mo_" + n)
        return S[n]

    def past(e, n, count):
        e.wait_ge(s(n), count * ROW_TILES.get(n, 1) + CREDIT)

    CREDIT = 8
    ROW_TILES = {"s1_up": 4, "s2_up": 2, "s1_dn": 2, "s2_dn": 2, "lt": 2}
    producers = {
        "pe": ("xf", "lt", "lg_up", "lg_dn", "xr", "oht_up", "oht_dn", "ga_up", "gb_up", "ga_dn", "gb_dn",
               "s1_up", "s2_up", "s1_dn", "s2_dn"),
        "act": ("sta_up", "sta_dn", "xfe_a", "xre", "ex_up", "ex_dn", "gae_up", "gae_dn", "me_up", "me_dn", "gelu", "ye"),
        "dve": ("lte", "xfe_d", "lge", "top", "idx", "idf", "df", "dd", "p0", "p1", "ohp", "ohr", "ohe_up", "ohe_dn",
                "gbe_up", "gbe_dn", "stb_up", "stb_dn", "hb", "yt", "res"),
        "pool": ("stx_up", "stx_dn"),
        "sp": ("outd",),
    }

    def start(e, who):
        for n in producers[who]:
            e.sem_inc(s(n), CREDIT)

    def stage_views(lv, u):
        sx, sa, sb = stage[u]
        if lv == "up":
            return (sx[:, 0:G8 * D1].rearrange("p (g j) -> p g j", j=D1),
                    sa.rearrange("p (g o) -> p g o", o=F1), sb.rearrange("p (g o) -> p g o", o=F1))
        return (sx.rearrange("p (c r j) -> p c r j", c=4, r=2),
                sa.rearrange("p (c r k o) -> p c r k o", c=4, r=2, k=2),
                sb.rearrange("p (c r k o) -> p c r k o", c=4, r=2, k=2))

    def stage_factor(copy, lv, u, which, n, done):
        dst = stage_views(lv, u)[1 + which]
        if lv == "up":
            src = gath[which].rearrange("p (o g) -> p g o", g=P)[:, bass.ds(n * G8, G8), :]
            copy(dst, src).then_inc(done, 1)
        else:
            src = gath[which].rearrange("p (o k c g) -> p c g k o", k=2, c=4, g=32)
            for k in range(2):
                x = copy(dst[:, :, :, k, :], src[:, :, bass.ds(n * 2, 2), k, :])
            x.then_inc(done, 1)

    with nc.Block() as block:
        @block.sync
        def _(sp):
            start(sp, "sp")
            x3_d, x2_d = a["x3"], a["x2"]
            out_v = out.rearrange("(q n r) d -> q n (r d)", q=QUADS, r=2)

            def load(dst, src, q, done):
                for t in range(2):
                    sp.dma_start(dst[:, t, :], src[bass.ds(q * 2 + t, 1), :, :].rearrange("q n d -> n (q d)"))\
                      .then_inc(s(done), 16)

            def tile(T, last):
                past(sp, "xr", T * 8 + 8)
                if not last:
                    load(x3s, x3_d, T + 1, "x3")
                past(sp, "stx_up", T * NS + NS)
                load(x2b, x2_d, T, "x2")
                past(sp, "res", T * 2 + 2)
                for t in range(2):
                    sp.dma_start(out_v[bass.ds(T * 2 + t, 1), :, :].rearrange("q n d -> n (q d)"), x2b[:, t, :])\
                      .then_inc(s("out"), 16)
                sp.wait_ge(s("out"), T * 32 + 32)
                sp.sem_inc(s("outd"), 1)
            load(x3s, x3_d, 0, "x3")
            for t in range(2):
                sp.dma_start(wr_dn[t * F1:(t + 1) * F1, :, :], a["wr_dn"]).then_inc(s("wr"), 16)
            with sp.Fori(0, NT - 1) as T:
                tile(T, False)
            tile(NT - 1, True)

        @block.gpsimd
        def _(pool):
            start(pool, "pool")
            with pool.Fori(0, NT) as T:
                for lv in ("up", "dn"):
                    if lv == "up":
                        past(pool, "xre", T * 8 + 8)
                    else:
                        past(pool, "gelu", T * NS + NS)
                    apart(pool, SPARE)
                    with pool.Fori(0, NS // 2) as i:
                        for u in range(2):
                            n = i * 2 + u
                            past(pool, "s1_" + lv, T * NS + n - 1)
                            dst = stage_views(lv, u)[0]
                            if lv == "up":
                                src = xrep[:, :, bass.ds(n * G8, G8)].rearrange("p j g -> p g j")
                            else:
                                src = h.rearrange("p (c g) j -> p c g j", c=4)[:, :, bass.ds(n * 2, 2), :]
                            pool.tensor_copy(dst, src).then_inc(s("stx_" + lv), 1)

        def choose(vec, T, lv):
            m = T * 2 + (lv == "dn")
            if lv == "up":
                past(vec, "lg_up", T * 2 + 2)
                past(vec, "stb_dn", T * NS)
                vec.tensor_copy(lg, ps[:, 4:6, 0:E]).then_inc(s("lge"), 1)
            else:
                past(vec, "stb_up", T * NS + NS)
                past(vec, "lt", T + 1)
                vec.tensor_copy(lt, ps[:, 4, 0:P]).then_inc(s("lte"), 1)
                past(vec, "lg_dn", T + 1)
                vec.tensor_copy(lg, ps[:, 5, 0:P].rearrange("p (t e) -> p t e", t=2)).then_inc(s("lge"), 1)
            past(vec, "lge", m + 1)
            apart(vec, SPARE)
            for t in range(2):
                vec.max(top[:, t, :], lg[:, t, :]).then_inc(s("top"), 1)
            past(vec, "top", m * 2 + 2)
            apart(vec, SPARE)
            for t in range(2):
                vec.max_index(top_i[:, t, :], top[:, t, :], lg[:, t, :]).then_inc(s("idx"), 1)
            vec.tensor_tensor(diff, top[:, :, 1], top[:, :, 0], ALU.subtract).then_inc(s("df"), 1)
            past(vec, "idx", m * 2 + 2)
            vec.tensor_copy(top_f, top_i[:, :, 0:2]).then_inc(s("idf"), 1)
            past(vec, "idf", m + 1)
            apart(vec, SPARE)
            for t in range(2):
                for k in range(2):
                    vec.tensor_scalar(oht[:, t, 1, k, :], iota, top_f[:, t, k:k + 1], None, ALU.is_equal)\
                       .then_inc(s("ohr"), 1)
            past(vec, "ex_" + lv, T + 1)
            vec.tensor_scalar(den, ex, 1.0, None, ALU.add).then_inc(s("dd"), 1)
            past(vec, "dd", m + 1)
            vec.reciprocal(prob[:, :, 0], den).then_inc(s("p0"), 1)
            past(vec, "p0", m + 1)
            vec.tensor_tensor(prob[:, :, 1], ex, prob[:, :, 0], ALU.mult).then_inc(s("p1"), 1)
            past(vec, "p1", m + 1)
            apart(vec, SPARE)
            for t in range(2):
                for k in range(2):
                    vec.tensor_scalar(oht[:, t, 0, k, :], iota, top_f[:, t, k:k + 1], prob[:, t, k:k + 1],
                                      ALU.is_equal, ALU.mult).then_inc(s("ohp"), 1)
            past(vec, "oht_" + lv, T + 1)
            if lv == "up":
                vec.tensor_copy(oh_up, ps[:, 4, :].rearrange("p (t v g) -> p t v g", t=2, v=2)).then_inc(s("ohe_up"), 1)
            else:
                for k in range(2):
                    r = slice(k * E, (k + 1) * E)
                    vec.tensor_copy(oh[r, :, :, k, :], ps[r, 4, :].rearrange("p (t v g) -> p t v g", t=2, v=2))\
                       .then_inc(s("ohe_dn"), 1)

        def gather_out(e, copy, T, lv, which, done):
            for b in range(GB):
                past(e, ("ga_", "gb_")[which] + lv, T * GB + b + 1)
                if b == 0 and lv == "dn":
                    past(e, ("sta_up", "stb_up")[which], T * NS + NS)
                if b == 0 and lv == "up":
                    past(e, ("sta_dn", "stb_dn")[which], T * NS)
                copy(gath[which][:, b * 512:(b + 1) * 512], ps[:, 2 * which + b % 2, :]).then_inc(done, 1)

        @block.vector
        def _(vec):
            start(vec, "dve")
            vec.memset(oh, 0.0).then_inc(s("oh0"), 1)
            vec.wait_ge(s("oh0"), 1)
            with vec.Fori(0, NT) as T:
                for b in range(2):
                    past(vec, "xf", T * 4 + 2 * b + 2)
                    past(vec, "sta_dn", T * NS)
                    vec.tensor_copy(xft[:, b, 4:8, :], ps[:, 2 * b + 1, :].rearrange("p (c n) -> p c n", c=4))\
                       .then_inc(s("xfe_d"), 1)
                choose(vec, T, "up")
                gather_out(vec, vec.tensor_copy, T, "up", 1, s("gbe_up"))
                past(vec, "gbe_up", T * GB + GB)

                def stage_b(lv, n, u, cond=None):
                    past(vec, "s2_" + lv, T * NS + n - 1)
                    stage_factor(vec.tensor_copy, lv, u, 1, n, s("stb_" + lv))

                def biased(n, u):
                    N = T * NS + n
                    past(vec, "s2_up", N + 1)
                    vec.scalar_tensor_tensor(h[:, bass.ds(n * G8, G8), :],
                                             ps[:, 6 + u, :].rearrange("p (g o) -> p g o", o=F1), scales[:, 0:1],
                                             b_up.unsqueeze(1).to_broadcast([P, G8, F1]), ALU.mult, ALU.add)\
                       .then_inc(s("hb"), 1)
                for u in range(2):
                    stage_b("up", u, u)
                with vec.Fori(0, NS // 2 - 1) as i:
                    for u in range(2):
                        biased(i * 2 + u, u)
                        stage_b("up", i * 2 + u + 2, u)
                for u in range(2):
                    biased(NS - 2 + u, u)
                choose(vec, T, "dn")
                gather_out(vec, vec.tensor_copy, T, "dn", 1, s("gbe_dn"))
                past(vec, "gbe_dn", T * GB + GB)
                apart(vec, SPARE)
                with vec.Fori(0, NS // 2) as i:
                    for u in range(2):
                        stage_b("dn", i * 2 + u, u)
                past(vec, "ye", T * NS + NS)
                past(vec, "stx_dn", T * NS + NS)
                for t in range(2):
                    vec.transpose(yt[:, t, :, :].rearrange("n o p -> n p o"),
                                  ybuf[:, t, :, :].rearrange("q g p -> q p g")).then_inc(s("yt"), 1)
                vec.wait_ge(s("x2"), T * 32 + 32)
                for t in range(2):
                    past(vec, "yt", T * 2 + t + 1)
                    vec.scalar_tensor_tensor(x2b[:, t, :], yt[:, t, :, :].rearrange("n o p -> n (o p)"), scales[:, 1:2],
                                             x2b[:, t, :], ALU.mult, ALU.add).then_inc(s("res"), 1)

        @block.scalar
        def _(act):
            start(act, "act")
            with act.Fori(0, NT) as T:
                for b in range(2):
                    past(act, "xf", T * 4 + 2 * b + 1)
                    past(act, "sta_dn", T * NS)
                    act.copy(xft[:, b, 0:4, :], ps[:, 2 * b, :].rearrange("p (c n) -> p c n", c=4)).then_inc(s("xfe_a"), 1)
                past(act, "outd", T)
                for b in range(8):
                    past(act, "xr", T * 8 + b + 1)
                    act.copy(xrep[:, 4 * b:4 * b + 4, :],
                             ps[:, XBANK[b], :].rearrange("p (j g) -> p j g", j=4)).then_inc(s("xre"), 1)
                    if b == 4:
                        past(act, "df", T * 2 + 1)
                        act.activation(ex, diff, ACT.Exp).then_inc(s("ex_up"), 1)
                gather_out(act, act.copy, T, "up", 0, s("gae_up"))

                def mid_out(lv, n, u):
                    past(act, "s1_" + lv, T * NS + n + 1)
                    past(act, "s2_" + lv, T * NS + n - 1)
                    act.copy(mid[u], ps[:, 4 + u, :]).then_inc(s("me_" + lv), 1)

                def gelu(n, u):
                    past(act, "hb", T * NS + n + 1)
                    act.activation(h[:, bass.ds(n * G8, G8), :], h[:, bass.ds(n * G8, G8), :], ACT.Gelu)\
                       .then_inc(s("gelu"), 1)
                def stage_a(lv, n, u):
                    past(act, "s1_" + lv, T * NS + n - 1)
                    stage_factor(act.copy, lv, u, 0, n, s("sta_" + lv))

                def steps(lv, finish):
                    past(act, "gae_" + lv, T * GB + GB)
                    stage_a(lv, 0, 0)
                    stage_a(lv, 1, 1)
                    mid_out(lv, 0, 0)
                    with act.Fori(0, NS // 2 - 1) as i:
                        for u in range(2):
                            stage_a(lv, i * 2 + u + 2, u)
                            mid_out(lv, i * 2 + u + 1, 1 - u)
                            finish(i * 2 + u, u)
                    mid_out(lv, NS - 1, 1)
                    finish(NS - 2, 0)
                    finish(NS - 1, 1)
                steps("up", gelu)
                past(act, "df", T * 2 + 2)
                act.activation(ex, diff, ACT.Exp).then_inc(s("ex_dn"), 1)
                gather_out(act, act.copy, T, "dn", 0, s("gae_dn"))

                def y_out(n, u):
                    past(act, "s2_dn", T * NS + n + 1)
                    act.copy(ybuf[:, :, bass.ds(n * 2, 2), :],
                             ps[:, 2 * u:2 * u + 2, 0:2 * D1].rearrange("p t (r o) -> p t r o", r=2)).then_inc(s("ye"), 1)
                steps("dn", y_out)


        @block.tensor
        def _(pe):
            start(pe, "pe")

            def transpose_choices(T, lv):
                past(pe, "ohr", (T * 2 + (lv == "dn")) * 4 + 4)
                past(pe, "ohp", (T * 2 + (lv == "dn")) * 4 + 4)
                for t in range(2):
                    for v in range(2):
                        last = pe.transpose(ps[:, 4, (2 * t + v) * P:(2 * t + v + 1) * P],
                                            oht[:, t, v, :, :].rearrange("p k e -> p (k e)"), ident)
                last.then_inc(s("oht_" + lv), 1)
                past(pe, "ohe_" + lv, T + 1 if lv == "up" else T * 2 + 2)

            def gather(T, lv):
                width = P if lv == "up" else 2 * P
                for b in range(GB):
                    for v in range(2):
                        if b >= 2:
                            past(pe, ("gae_", "gbe_")[v] + lv, T * GB + b - 1)
                        for r in range(512 // width):
                            o = b * (512 // width) + r
                            for t in range(2):
                                w = tab_up[v][:, o, :, :].rearrange("p k i -> p (k i)") if lv == "up" \
                                    else tab_dn[v][:, o, :]
                                x = oh_up[:, t, v, :] if lv == "up" else oh[:, t, v, :, :].rearrange("p k g -> p (k g)")
                                last = pe.matmul(ps[t * E:(t + 1) * E, 2 * v + b % 2, r * width:(r + 1) * width],
                                                 w, x, start=True, stop=True)
                        last.then_inc(s(("ga_", "gb_")[v] + lv), 1)

            def first(T, lv, n, u):
                past(pe, "stx_" + lv, T * NS + n + 1)
                past(pe, "sta_" + lv, T * NS + n + 1)
                past(pe, "me_" + lv, T * NS + n - 1)
                apart(pe, SPARE)
                sx, sa, _ = stage[u]
                for g in range(G8):
                    if lv == "up":
                        for q in range(4):
                            r = slice(32 * q, 32 * q + 32)
                            x = pe.matmul(ps[r, 4 + u, g * F1:(g + 1) * F1], sx[r, g * D1:(g + 1) * D1],
                                          sa[r, g * F1:(g + 1) * F1], start=True, stop=True)
                            if g == G8 - 1:
                                x.then_inc(s("s1_up"), 1)
                    else:
                        for t in range(2):
                            r = slice(64 * t, 64 * t + 64)
                            x = pe.matmul(ps[r, 4 + u, g * F1:(g + 1) * F1], sx[r, g * F1:(g + 1) * F1],
                                          sa[r, g * F1:(g + 1) * F1], start=True, stop=True)
                            if g == G8 - 1:
                                x.then_inc(s("s1_dn"), 1)

            def second(T, lv, n, u):
                past(pe, "stb_" + lv, T * NS + n + 1)
                past(pe, "me_" + lv, T * NS + n + 1)
                past(pe, "hb" if lv == "up" else "ye", T * NS + n - 1)
                apart(pe, SPARE)
                sb, md = stage[u][2], mid[u]
                if lv == "up":
                    for g in range(G8):
                        for t in range(2):
                            r = slice(64 * t, 64 * t + 64)
                            x = pe.matmul(ps[r, 6 + u, g * F1:(g + 1) * F1], md[r, g * F1:(g + 1) * F1],
                                          sb[r, g * F1:(g + 1) * F1], start=True, stop=True)
                            if g == G8 - 1:
                                x.then_inc(s("s2_up"), 1)
                else:
                    for half in range(2):
                        for t in range(2):
                            r = slice(64 * t, 64 * t + 64)
                            for k in range(2):
                                for c in range(4):
                                    at = (2 * c + half) * F1 + k * D1
                                    x = pe.matmul(ps[32 * c:32 * c + 32, 2 * u + t, half * D1:(half + 1) * D1],
                                                     md[r, at:at + D1], sb[r, at:at + D1], start=k == 0, stop=k == 1)
                            if half == 1:
                                x.then_inc(s("s2_dn"), 1)

            def steps(T, lv):
                first(T, lv, 0, 0)
                with pe.Fori(0, NS // 2 - 1) as i:
                    for u in range(2):
                        first(T, lv, i * 2 + u + 1, 1 - u)
                        second(T, lv, i * 2 + u, u)
                first(T, lv, NS - 1, 1)
                second(T, lv, NS - 2, 0)
                second(T, lv, NS - 1, 1)

            with pe.Fori(0, NT) as T:
                pe.wait_ge(s("x3"), T * 32 + 32)
                past(pe, "ye", T * NS)
                for t in range(2):
                    for c in range(8):
                        last = pe.transpose(ps[:, 2 * t + c // 4, (c % 4) * P:(c % 4 + 1) * P],
                                            x3s[:, t, c * P:(c + 1) * P], ident)
                        if c % 4 == 3:
                            last.then_inc(s("xf"), 1)
                for t in range(2):
                    past(pe, "xfe_a", T * 2 + t + 1)
                    past(pe, "xfe_d", T * 2 + t + 1)
                    for c in range(8):
                        last = pe.matmul(ps[:, 4 + t, 0:E], xft[:, t, c, :], wr_up[:, c, :], start=c == 0, stop=c == 7)
                    last.then_inc(s("lg_up"), 1)
                for b in range(8):
                    if b >= 6:
                        past(pe, "xre", T * 8 + b - 5)
                    for j in range(4):
                        for q in range(4):
                            x = x3s[:, q // 2, :].rearrange("n (i j) -> n j i", j=D1)[:, 4 * b + j, :]
                            last = pe.matmul(ps[q * D1:(q + 1) * D1, XBANK[b], j * P:(j + 1) * P],
                                             x, ident, start=True, stop=True)
                    last.then_inc(s("xr"), 1)
                transpose_choices(T, "up")
                past(pe, "xre", T * 8 + 8)
                gather(T, "up")
                steps(T, "up")
                past(pe, "gelu", T * NS + NS)
                apart(pe, SPARE)
                pe.wait_ge(s("wr"), 32)
                for p in range(F1):
                    for t in range(2):
                        r = slice(64 * t, 64 * t + 64)
                        x = pe.matmul(ps[r, 4, 0:P], wr_dn[r, p, :], h[r, :, p], start=p == 0, stop=p == F1 - 1)
                        if p == F1 - 1:
                            x.then_inc(s("lt"), 1)
                past(pe, "lte", T + 1)
                pe.transpose(ps[:, 5, 0:P], lt, ident).then_inc(s("lg_dn"), 1)
                transpose_choices(T, "dn")
                gather(T, "dn")
                steps(T, "dn")


_IN = ["x", "ctx", "wq", "wk", "bq", "bk", "bv", "xwv", "swq", "swk", "swv", "swo", "bo", "db",
       "wr_up", "wr_dn", "a_up", "b_up_f", "a_dn", "b_dn_f", "iota", "b_up", "b_dn", "s_up", "s_dn"]


def kernel(x, ctx_1024, L0_xattn_Wq, L0_xattn_bq, L0_xattn_Wk, L0_xattn_bk, L0_xattn_Wv, L0_xattn_bv,
           L0_attn_Wq, L0_attn_Wk, L0_attn_Wv, L0_attn_Wo, L0_attn_bo, L0_attn_denom_bias,
           L0_ffn_W_up, L0_ffn_A_up, L0_ffn_B_up, L0_ffn_scale_up, L0_ffn_bias_up,
           L0_ffn_W_down, L0_ffn_A_down, L0_ffn_B_down, L0_ffn_scale_down, L0_ffn_bias_down):
    import numpy as np
    import concourse.bacc as bacc
    from concourse.bass_utils import run_bass_kernel_spmd

    def column(b):
        return np.asarray(b).reshape(DC, P).T

    laid = {
        "x": np.asarray(x).reshape(SEQS * SEQ, D), "ctx": ctx_1024, "wq": L0_xattn_Wq, "wk": L0_xattn_Wk,
        "bq": column(L0_xattn_bq), "bk": column(L0_xattn_bk), "bv": np.asarray(L0_xattn_bv).reshape(1, D),
        "xwv": np.asarray(L0_xattn_Wv).T, "swq": np.asarray(L0_attn_Wq).T, "swk": np.asarray(L0_attn_Wk).T,
        "swv": np.asarray(L0_attn_Wv).T, "swo": np.asarray(L0_attn_Wo).T,
        "bo": np.asarray(L0_attn_bo).reshape(1, D), "db": np.asarray(L0_attn_denom_bias).reshape(1, HEADS),
        "wr_up": np.asarray(L0_ffn_W_up).T,
        "wr_dn": np.asarray(L0_ffn_W_down).reshape(E, F1, F1).transpose(1, 2, 0),
        "a_up": L0_ffn_A_up, "b_up_f": L0_ffn_B_up, "a_dn": L0_ffn_A_down, "b_dn_f": L0_ffn_B_down,
        "iota": np.arange(E, dtype=np.float32).reshape(1, E),
        "b_up": np.asarray(L0_ffn_bias_up).reshape(F1, F1), "b_dn": np.asarray(L0_ffn_bias_down).reshape(1, 2 * D),
        "s_up": np.asarray(L0_ffn_scale_up).reshape(1, 1), "s_dn": np.asarray(L0_ffn_scale_down).reshape(1, 1),
    }
    nc = bacc.Bacc("TRN2", target_bir_lowering=False, num_devices=1)
    arrays, a = {}, {}
    for name in _IN:
        v = np.ascontiguousarray(laid[name])
        arrays[name] = v
        a[name] = nc.dram_tensor(name, v.shape, mybir.dt.from_np(v.dtype), kind="ExternalInput").ap()
    for name in ("x2", "x3"):
        a[name] = nc.dram_tensor(name + "_n", (QUADS, P, 2 * D), F32, kind="Internal").ap()
    out = nc.dram_tensor("out", (SEQS * SEQ, D), F32, kind="ExternalOutput").ap()
    program(nc, a, out)
    r = run_bass_kernel_spmd(nc, [arrays], core_ids=[0])
    return r.results[0]["out"].reshape(SEQS, SEQ, D)
```

```python
from contextlib import ExitStack
from math import prod

import concourse.bass as bass
from concourse import mybir

F32 = mybir.dt.float32
U32 = mybir.dt.uint32
ALU = mybir.AluOpType
ACT = mybir.ActivationFunctionType
AX = mybir.AxisListType
SPARE = {}

P = 128
SBUF = 53208
SEQS, SEQ, D, CTX = 32, 64, 512, 1601
DC = D // P
QUADS = SEQS // 4
QROWS = 4 * SEQ
EPS = 1e-5
HEADS = 16
HD = D // HEADS
HPC = P // HD
E = 64
D1, F1 = 32, 64
FULL = CTX // P
REST = CTX - FULL * P
TILES = FULL + 1
GROUPS = 4
GT = 4
MASKED = -3.0e38


def apart(e, spare):
    e.sem_inc(spare[e.engine], 1)


def group_tiles(g):
    return range(GT * g, min(GT * g + GT, TILES))


def tile_rows(j):
    return P if j < FULL else REST


def group_cols(g):
    return sum(tile_rows(j) for j in group_tiles(g))


def program(nc, a, out):
    ctx = ExitStack()
    with ctx:
        arena = ctx.enter_context(nc.sbuf_tensor("arena", [P, SBUF], F32))
        ps = ctx.enter_context(nc.psum_tensor("ps", [P, 8, 512], F32))

        def sem(name):
            return ctx.enter_context(nc.semaphore(name))

        class Area:

            def __init__(self, at, end=SBUF):
                self.at, self.end = at, end

            def __call__(self, *dims, dt=F32):
                n = prod(dims)
                v = arena[:, self.at:self.at + n]
                self.at += n
                assert self.at <= self.end, (self.at, self.end)
                if dt != F32:
                    v = v.bitcast(dt)
                if len(dims) == 1:
                    return v
                names = "abcd"[:len(dims)]
                return v.rearrange(f"p ({' '.join(names)}) -> p {' '.join(names)}",
                                   **{k: d for k, d in zip(names[1:], dims[1:])})

        for n, e in (("pe", nc.tensor), ("dve", nc.vector), ("pool", nc.gpsimd), ("sp", nc.sync)):
            SPARE[e.engine] = sem("spare_" + n)
        keep = Area(0)
        ident = keep(P)
        qa = keep(DC, SEQS * SEQ)
        qbias = keep(2 * QUADS)
        halves = keep(2)
        after_keep = keep.at

        late = Area(after_keep)
        weights = {n: late(DC, D) for n in ("swq", "swk", "swv", "swo")}
        early = Early(sem, Area(SBUF - 9 * D), weights)
        ct_area = Area(after_keep)
        ct = [ct_area(2, TILES, D)]
        prepare_at = ct_area.at
        ct.append(ct_area(2, TILES, D))
        s_c = [[sem(f"cr_c{u}{g}") for g in range(GROUPS)] for u in range(2)]

        prepare(nc, sem, Area(prepare_at), ps, a, ident, qa, qbias, halves, ct, s_c)
        cross(nc, sem, Area(after_keep, SBUF - 9 * D), ps, a, ident, qa, qbias, ct, s_c, early)
        tables = {"up": [late(F1, 2, D1) for _ in range(2)], "dn": [late(D1, F1) for _ in range(2)],
                  "wr_up": late(8, E), "b_up": late(F1), "scales": late(2), "iota": late(E)}
        self_attention(nc, sem, Area(late.at, SBUF - 9 * D), ps, a, ident, qa, halves, tables, early)
        mixture(nc, sem, Area(late.at, early.low_end), Area(after_keep), early, ps, a, ident,
                qa.rearrange("p c n -> p (c n)"), tables, out)


class Signals:
    CREDIT = 8

    def __init__(self, sem, prefix, producers, times=None):
        self.producers, self.times = producers, times or {}
        self.sems = {n: sem(prefix + n) for names in producers.values() for n in names}

    def __getitem__(self, name):
        return self.sems[name]

    def start(self, e, who):
        for n in self.producers[who]:
            e.sem_inc(self.sems[n], self.CREDIT)

    def past(self, e, name, count):
        e.wait_ge(self.sems[name], count * self.times.get(name, 1) + self.CREDIT)


def layer_norm_stats(vec, stats, mv, x, S, stat, done, n0):
    for par in range(2):
        vec.bn_stats(stats[:, par, :], x[:, par * D:(par + 1) * D]).then_inc(S[stat], 1)
    S.past(vec, stat, n0 + 1)
    apart(vec, SPARE)
    for par in range(2):
        vec.bn_aggr(mv[:, par, :], stats[:, par, :]).then_inc(S[done], 1)


def layer_norm_rstd(pool, mv, veps, rstd, halves, S, summed, done, n0):
    apart(pool, SPARE)
    pool.tensor_scalar(veps[:, :], mv[:, :, 1], EPS, None, ALU.add).then_inc(S[summed], 1)
    S.past(pool, summed, n0 + 1)
    pool.tensor_tensor(rstd[:, :], veps[:, :], halves[:, :], ALU.pow).then_inc(S[done], 1)


def prepare(nc, sem, area, ps, a, ident, qa, qbias, halves, ct, s_c):
    wq, wk = area(DC, D), area(DC, D)
    wqk = area(DC, D)
    bqc, bkc = area(DC), area(DC)
    bq_wide = area(DC, P)
    cols = area(2 * DC + 1)
    xt = [area(2 * D) for _ in range(2)]
    xn = [area(2 * D) for _ in range(2)]
    lnt = [area(DC, QROWS) for _ in range(2)]
    stats, mv = area(2, 6), area(2, 2)
    veps, rstd = area(2), area(2)
    x_h = a["x"].rearrange("(q n r) d -> q n (r d)", q=QUADS, r=2)
    TB, QB, RB = 5, 0, 4

    s_w, s_b = sem("pr_w"), sem("pr_b")
    s_x = [sem(f"pr_x{u}") for u in range(2)]
    S = Signals(sem, "pr_", {
        "pe": ("fuse", "col", "t", "q", "r"),
        "act": ("te", "qe"),
        "dve": ("wide", "fused", "cold", "stat", "mv", "xn", "re"),
        "pool": ("id0", "id", "half", "veps", "rstd"),
    }, {"stat": 2, "mv": 2, "xn": 2, "t": 2, "te": 2, "q": DC, "qe": DC})
    past = S.past

    with nc.Block() as block:
        @block.sync
        def _(sp):
            for u in range(2):
                sp.dma_start(xt[u], x_h[u, :, :]).then_inc(s_x[u], 16)
            sp.dma_start(wq, a["wq"].rearrange("(c p) d -> p c d", p=P)).then_inc(s_w, 16)
            sp.dma_start(wk, a["wk"].rearrange("(c p) d -> p c d", p=P)).then_inc(s_w, 16)
            sp.dma_start(bqc, a["bq"]).then_inc(s_b, 16)
            sp.dma_start(bkc, a["bk"]).then_inc(s_b, 16)
            with sp.Fori(0, QUADS // 2 - 1) as i:
                for u in range(2):
                    past(sp, "xn", i * 2 + u + 1)
                    sp.dma_start(xt[u], x_h[bass.ds(i * 2 + u + 2, 1), :, :].rearrange("q n d -> n (q d)"))\
                      .then_inc(s_x[u], 16)
            load_context(sp, a, ct, s_c, 0, 0)

        @block.gpsimd
        def _(pool):
            S.start(pool, "pool")
            pool.memset(halves, -0.5).then_inc(S["half"], 1)
            pool.memset(ident, 0.0).then_inc(S["id0"], 1)
            past(pool, "id0", 1)
            pool.affine_select(out=ident, in_=ident, compare_op=ALU.not_equal, fill=1.0, base=0,
                               pattern=[[-1, P]], channel_multiplier=1).then_inc(S["id"], 1)
            past(pool, "half", 1)
            with pool.Fori(0, QUADS) as n:
                past(pool, "mv", n + 1)
                layer_norm_rstd(pool, mv, veps, rstd, halves, S, "veps", "rstd", n)

        @block.vector
        def _(vec):
            S.start(vec, "dve")

            def normalise(i, u):
                n = i * 2 + u
                vec.wait_ge(s_x[u], i * 16 + 16)
                layer_norm_stats(vec, stats, mv, xt[u], S, "stat", "mv", n)
                past(vec, "rstd", n + 1)
                past(vec, "mv", n + 1)
                past(vec, "t", n - 1)
                for par in range(2):
                    vec.tensor_scalar(xn[u][:, par * D:(par + 1) * D], xt[u][:, par * D:(par + 1) * D],
                                      mv[:, par, 0:1], rstd[:, par:par + 1], ALU.subtract, ALU.mult)\
                       .then_inc(S["xn"], 1)

            def row_biases(n):
                past(vec, "r", n + 1)
                vec.tensor_tensor(qbias[:, bass.ds(n * 2, 2)], ps[:, RB, 16:18],
                                  cols[:, 2 * DC:2 * DC + 1].to_broadcast([P, 2]), ALU.add).then_inc(S["re"], 1)
            normalise(0, 0)
            vec.wait_ge(s_b, 32)
            for c in range(DC):
                vec.tensor_copy(bq_wide[:, c, :], bqc[:, c:c + 1].to_broadcast([P, P])).then_inc(S["wide"], 1)
            for m in range(DC):
                past(vec, "fuse", m + 1)
                vec.tensor_copy(wqk[:, m, :], ps[:, m, :]).then_inc(S["fused"], 1)
            past(vec, "col", 1)
            vec.tensor_copy(cols, ps[:, RB, 0:2 * DC + 1]).then_inc(S["cold"], 1)
            past(vec, "cold", 1)
            normalise(0, 1)
            with vec.Fori(0, QUADS // 2 - 1) as i:
                for u in range(2):
                    row_biases(i * 2 + u)
                    normalise(i + 1, u)
            for u in range(2):
                row_biases(QUADS - 2 + u)

        @block.scalar
        def _(act):
            S.start(act, "act")

            def transposed(n, u):
                for par in range(2):
                    act.wait_ge(S["t"], n * 2 + par + 1 + S.CREDIT)
                    past(act, "q", n - 1)
                    act.copy(lnt[u][:, :, par::2], ps[:, TB + par, :].rearrange("p (c n) -> p c n", c=DC))\
                       .then_inc(S["te"], 1)

            def results(n):
                for m in range(DC):
                    act.wait_ge(S["q"], n * DC + m + 1 + S.CREDIT)
                    act.activation(qa[:, m, bass.ds(n * QROWS, QROWS)], ps[:, m, 0:QROWS],
                                   ACT.Identity, bias=cols[:, m:m + 1]).then_inc(S["qe"], 1)
            transposed(0, 0)
            past(act, "cold", 1)
            with act.Fori(0, QUADS // 2 - 1) as i:
                for u in range(2):
                    transposed(i * 2 + u + 1, 1 - u)
                    results(i * 2 + u)
            transposed(QUADS - 1, 1)
            for u in range(2):
                results(QUADS - 2 + u)

        @block.tensor
        def _(pe):
            S.start(pe, "pe")

            def transposes(n, u):
                for par in range(2):
                    pe.wait_ge(S["xn"], n * 2 + par + 1 + S.CREDIT)
                    past(pe, "te", n)
                    for c in range(DC):
                        last = pe.transpose(ps[:, TB + par, c * P:(c + 1) * P],
                                            xn[u][:, par * D + c * P:par * D + (c + 1) * P], ident)
                    last.then_inc(S["t"], 1)

            def products(n, u):
                past(pe, "te", n + 1)
                past(pe, "re", n)
                for pair in range(2):
                    for c in range(DC):
                        last = pe.matmul(ps[:, RB, 16 + pair:17 + pair], lnt[u][:, c, pair * P:(pair + 1) * P],
                                         cols[:, DC + c:DC + c + 1], start=c == 0, stop=c == DC - 1)
                last.then_inc(S["r"], 1)
                for m in range(DC):
                    pe.wait_ge(S["qe"], (n - 1) * DC + m + 1 + S.CREDIT)
                    for c in range(DC):
                        last = pe.matmul(ps[:, QB + m, 0:QROWS], wqk[:, c, m * P:(m + 1) * P],
                                         lnt[u][:, c, :], start=c == 0, stop=c == DC - 1)
                    last.then_inc(S["q"], 1)
            past(pe, "id", 1)
            transposes(0, 0)
            pe.wait_ge(s_w, 32)
            for m in range(DC):
                for c in range(DC):
                    last = pe.matmul(ps[:, m, :], wq[:, c, m * P:(m + 1) * P], wk[:, c, :],
                                     start=c == 0, stop=c == DC - 1)
                last.then_inc(S["fuse"], 1)
            pe.wait_ge(s_b, 32)
            for k, (w, b) in enumerate(((wk, bqc), (wq, bkc))):
                for m in range(DC):
                    for c in range(DC):
                        pe.matmul(ps[:, RB, k * DC + m:k * DC + m + 1], w[:, c, m * P:(m + 1) * P],
                                  b[:, c:c + 1], start=c == 0, stop=c == DC - 1)
            past(pe, "wide", DC)
            for c in range(DC):
                last = pe.matmul(ps[:, RB, 2 * DC:2 * DC + 1], bq_wide[:, c, :], bkc[:, c:c + 1],
                                 start=c == 0, stop=c == DC - 1)
            last.then_inc(S["col"], 1)
            past(pe, "fused", DC)
            past(pe, "cold", 1)
            with pe.Fori(0, QUADS // 2 - 1) as i:
                for u in range(2):
                    transposes(i * 2 + u + 1, 1 - u)
                    products(i * 2 + u, u)
            transposes(QUADS - 1, 1)
            for u in range(2):
                products(QUADS - 2 + u, u)


def load_context(sp, a, ct, s_c, u, pair):
    c_main = a["ctx"][:, 0:FULL * P, :].rearrange("s (p j) d -> s p j d", j=FULL)
    c_rest = a["ctx"][:, FULL * P:CTX, :]
    for g in range(GROUPS):
        for b in range(2):
            seq = pair * 2 + b
            if g < GROUPS - 1:
                src = c_main[bass.ds(seq, 1), :, GT * g:GT * (g + 1), :].rearrange("s p j d -> p (s j) d")
                dst = ct[u][:, b, GT * g:GT * (g + 1), :]
            else:
                src = c_rest[bass.ds(seq, 1), :, :].rearrange("s p d -> p (s d)")
                dst = ct[u][0:REST, b, FULL, :]
            sp.dma_start(dst, src).then_inc(s_c[u][g], 16)


class Early:

    def __init__(self, sem, area, weights):
        self.weights = weights
        self.s_w = sem("early_w")
        self.ats, self.x, self.bv = area(DC, QROWS), area(2 * D), area(D)
        self.low_end = area.at
        self.xwv = area(DC, D)
        self.s_x, self.s_bv, self.s_xwv, self.s_x3 = (sem("early_" + n) for n in ("x", "bv", "xwv", "x3"))
        self.s_out = sem("early_out")

    def load(self, sp, a):
        sp.dma_start(self.xwv, a["xwv"].rearrange("(c p) e -> p c e", p=P)).then_inc(self.s_xwv, 16)
        sp.dma_start(self.x, a["x"].rearrange("(q n r) d -> q n (r d)", q=QUADS, r=2)[0, :, :]).then_inc(self.s_x, 16)
        sp.dma_start(self.bv, a["bv"].to_broadcast([P, D])).then_inc(self.s_bv, 16)


def cross(nc, sem, area, ps, a, ident, qa, qbias, ct, s_c, early):
    area(2 * 2 * TILES * D)
    xt = [area(2, DC, GT * P) for _ in range(2)]
    qs = [area(DC, P) for _ in range(2)]
    prob = area(CTX)
    probt = area(TILES, P)
    att = area(D)
    mx, sums = area(GROUPS), area(GROUPS)
    top, bias = area(1), area(1)
    total, recip = area(1), area(1)

    s_fill, s_ea, s_ed = sem("cr_fill"), sem("cr_ea"), sem("cr_ed")
    s_s, s_pv = sem("cr_s"), sem("cr_pv")
    s_mx, s_top, s_bias = sem("cr_mx"), sem("cr_top"), sem("cr_bias")
    s_exp, s_tot, s_rec = sem("cr_exp"), sem("cr_tot"), sem("cr_rec")
    s_att, s_at, s_ate, s_qs = sem("cr_att"), sem("cr_at"), sem("cr_ate"), sem("cr_qs")
    TB, OB, AB = 4, 6, 7
    PIECES = 2 * DC
    PTF = GROUPS
    FILLS = GROUPS * PIECES + PTF
    PAIRS = SEQS // 2

    def filled_before(p):
        return p * FILLS + 2 * PIECES

    def pair_fills(last):
        f = [("ctx", g, c, b) for g in range(2 if last else GROUPS) for c in range(DC) for b in range(2)]
        return f + [("prob", g) for g in range(GROUPS)]

    with nc.Block() as block:
        @block.sync
        def _(sp):
            load_context(sp, a, ct, s_c, 1, 1)
            with sp.Fori(0, PAIRS // 2 - 1) as i:
                for u in range(2):
                    sp.wait_ge(s_pv, i * 2 + u + 1)
                    load_context(sp, a, ct, s_c, u, i * 2 + u + 2)
            early.load(sp, a)
            sp.wait_ge(s_pv, PAIRS - 1)
            for n, w in early.weights.items():
                sp.dma_start(w, a[n].rearrange("(c p) e -> p c e", p=P)).then_inc(early.s_w, 16)

        @block.gpsimd
        def _(pool):
            for u in range(2):
                pool.tensor_copy(qs[u], qa[:, :, u * P:(u + 1) * P]).then_inc(s_qs, 1)
            with pool.Fori(0, PAIRS // 2 - 1) as i:
                for u in range(2):
                    pool.wait_ge(s_s, (i * 2 + u + 1) * GROUPS * DC)
                    pool.tensor_copy(qs[u], qa[:, :, bass.ds((i * 2 + u + 2) * P, P)]).then_inc(s_qs, 1)
            pool.wait_ge(s_ate, 2)
            pool.wait_ge(s_qs, PAIRS)
            pool.tensor_copy(early.ats, qa[:, :, 0:QROWS]).then_inc(s_qs, 1)

        def fill_bank(k, what):
            if what[0] == "ctx" and what[1] == GROUPS - 1:
                return TB + (k - (GROUPS - 1) * PIECES) % 4
            return TB + k % 2

        def evacuate(e, copy, p, k, what, s_done):
            src = ps[:, fill_bank(k, what), :]
            e.wait_ge(s_fill, filled_before(p) + k + 1)
            if what[0] == "ctx":
                _, g, c, b = what
                e.wait_ge(s_s, p * GROUPS * DC + g * DC + c + 1)
                w = group_cols((g + 2) % GROUPS)
                copy(xt[g % 2][:, b, c, 0:w], src[:, 0:w]).then_inc(s_done, 1)
            else:
                g = what[1]
                e.wait_ge(s_pv, p)
                if g < GROUPS - 1:
                    copy(probt[:, GT * g:GT * (g + 1), :], src).then_inc(s_done, 1)
                else:
                    copy(probt[0:REST, FULL, :], src[0:REST, 0:P]).then_inc(s_done, 1)

        def first_fills(e, copy, parity, s_done):
            for k in range(parity, 2 * PIECES, 2):
                g, c, b = k // PIECES, k % PIECES // 2, k % 2
                e.wait_ge(s_fill, k + 1)
                copy(xt[g][:, b, c, :], ps[:, TB + k % 2, :]).then_inc(s_done, 1)

        @block.scalar
        def _(act):
            first_fills(act, act.copy, 0, s_ea)

            def pair(i, u, last):
                p = i * 2 + u
                fills = pair_fills(last)
                mine = [(k, what) for k, what in enumerate(fills) if k % 2 == 0 and what[0] == "ctx"]
                late = [f for f in mine if f[1][1] == GROUPS - 1]
                early = [f for f in mine if f not in late] + late[:2]
                late = late[2:]
                for k, what in early:
                    evacuate(act, act.copy, p, k, what, s_ea)
                act.wait_ge(s_bias, p + 1)
                act.wait_ge(s_fill, filled_before(p))
                for g in range(GROUPS):
                    w = group_cols(g)
                    act.activation(prob[:, g * GT * P:g * GT * P + w], ps[:, g, 0:w], ACT.Exp,
                                   bias=bias[:, 0:1], accum_out=sums[:, g:g + 1]).then_inc(s_exp, 1)
                    if late:
                        k, what = late.pop(0)
                        evacuate(act, act.copy, p, k, what, s_ea)
                for k, what in enumerate(fills):
                    if k % 2 == 0 and what[0] == "prob":
                        evacuate(act, act.copy, p, k, what, s_ea)
                act.wait_ge(s_pv, p + 1)
                act.wait_ge(s_rec, p + 1)
                act.wait_ge(s_at, p)
                act.activation(att, ps[:, OB, :], ACT.Copy, scale=recip[:, 0:1]).then_inc(s_att, 1)
            for u in range(2):
                pair(0, u, False)
            with act.Fori(1, PAIRS // 2 - 1) as i:
                for u in range(2):
                    pair(i, u, False)
            for u in range(2):
                pair(PAIRS // 2 - 1, u, u == 1)

        @block.vector
        def _(vec):
            first_fills(vec, vec.tensor_copy, 1, s_ed)

            def attended(p):
                vec.wait_ge(s_at, p + 1)
                vec.wait_ge(s_qs, p + 1)
                vec.tensor_copy(qa[:, :, bass.ds(p * P, P)],
                                ps[:, AB, :].rearrange("p (c n) -> p c n", c=DC)).then_inc(s_ate, 1)

            def pair(i, u, last, first):
                p = i * 2 + u
                fills = pair_fills(last)

                def fill_out(g):
                    for k, what in enumerate(fills):
                        if k % 2 == 1 and what[0] == "ctx" and what[1] == g:
                            evacuate(vec, vec.tensor_copy, p, k, what, s_ed)
                for g in range(GROUPS):
                    if g < GROUPS - 1:
                        fill_out(g)
                    vec.wait_ge(s_s, p * GROUPS * DC + (g + 1) * DC)
                    vec.reduce_max(mx[:, g:g + 1], ps[:, g, 0:group_cols(g)], AX.X).then_inc(s_mx, 1)
                    if g == 0 and not first:
                        attended(p - 1)
                vec.wait_ge(s_mx, (p + 1) * GROUPS)
                vec.tensor_reduce(top, mx, AX.X, ALU.max, negate=True).then_inc(s_top, 1)
                vec.wait_ge(s_top, p + 1)
                vec.tensor_scalar(bias, top, qbias[:, bass.ds(p, 1)], qbias[:, bass.ds(p, 1)],
                                  ALU.subtract, ALU.add).then_inc(s_bias, 1)
                fill_out(GROUPS - 1)
                for k, what in enumerate(fills):
                    if k % 2 == 1 and what[0] == "prob":
                        evacuate(vec, vec.tensor_copy, p, k, what, s_ed)
                vec.wait_ge(s_exp, (p + 1) * GROUPS)
                vec.reduce_sum(total, sums, AX.X).then_inc(s_tot, 1)
                vec.wait_ge(s_tot, p + 1)
                vec.wait_ge(s_att, p)
                vec.reciprocal(recip, total).then_inc(s_rec, 1)
            for u in range(2):
                pair(0, u, False, u == 0)
            with vec.Fori(1, PAIRS // 2 - 1) as i:
                for u in range(2):
                    pair(i, u, False, False)
            for u in range(2):
                pair(PAIRS // 2 - 1, u, u == 1, False)
            attended(PAIRS - 1)

        @block.tensor
        def _(pe):
            def free_bank(n, k):
                if k % 2 == 0:
                    pe.wait_ge(s_ea, n)
                else:
                    pe.wait_ge(s_ed, n)

            def transpose_group(u, g, c, b, bank):
                for j in group_tiles(g):
                    r = tile_rows(j)
                    at = (j - GT * g) * P
                    last = pe.transpose(ps[:, bank, at:at + r],
                                        ct[u][0:r, b, j, c * P:(c + 1) * P], ident[0:r, 0:r])
                last.then_inc(s_fill, 1)

            for g in range(2):
                pe.wait_ge(s_c[0][g], 32)
                for k in range(PIECES):
                    n = g * PIECES + k
                    if n >= 2:
                        free_bank(n // 2, n)
                    transpose_group(0, g, k // 2, k % 2, TB + n % 2)

            def transpose_attended(p):
                pe.wait_ge(s_att, p + 1)
                pe.wait_ge(s_ate, p)
                for c in range(DC):
                    last = pe.transpose(ps[:, AB, c * P:(c + 1) * P], att[:, c * P:(c + 1) * P], ident)
                last.then_inc(s_at, 1)

            def pair(i, u, last, first):
                p = i * 2 + u
                half = p * (FILLS // 2) + PIECES
                pe.wait_ge(s_qs, p + 1)
                k = 0
                for g in range(GROUPS):
                    w = group_cols(g)
                    ahead = (g + 2) % GROUPS
                    if g < 2:
                        pe.wait_ge(s_c[u][ahead], i * 32 + 32)
                    elif not last:
                        nxt = (i if u == 0 else i + 1)
                        pe.wait_ge(s_c[1 - u][ahead], nxt * 32 + 32)
                    for c in range(DC):
                        done = half + (g - 2) * DC + c + 1
                        pe.wait_ge(s_ea, done)
                        pe.wait_ge(s_ed, done)
                        for b in range(2):
                            x = pe.matmul(ps[b * SEQ:(b + 1) * SEQ, g, 0:w], qs[u][:, c, b * SEQ:(b + 1) * SEQ],
                                          xt[g % 2][:, b, c, 0:w], start=c == 0, stop=c == DC - 1)
                        x.then_inc(s_s, 1)
                        if g < GROUPS - 1:
                            transposed = [c]
                        else:
                            transposed = range(DC) if c == DC - 1 else []
                        if g >= 2 and last:
                            transposed = []
                        for ct_c in transposed:
                            for b in range(2):
                                bank = fill_bank(k, ("ctx", g))
                                if bank < TB + 2 and (g < GROUPS - 1 or k < (GROUPS - 1) * PIECES + 2):
                                    free_bank(half + k // 2, k)
                                elif k >= (GROUPS - 1) * PIECES + 4:
                                    free_bank(half + k // 2 - 1, k)
                                elif bank == AB and not first:
                                    pe.wait_ge(s_ate, p)
                                transpose_group(u if g < 2 else 1 - u, ahead, ct_c, b, bank)
                                k += 1
                    if g == 0 and not first:
                        transpose_attended(p - 1)
                def transpose_prob(g):
                    pe.wait_ge(s_exp, p * GROUPS + g + 1)
                    free_bank(half + (k + g) // 2, k + g)
                    for j in group_tiles(g):
                        r = tile_rows(j)
                        x = pe.transpose(ps[0:r, TB + (k + g) % 2, (j - GT * g) * P:(j - GT * g + 1) * P],
                                         prob[:, j * P:j * P + r], ident)
                    x.then_inc(s_fill, 1)
                transpose_prob(0)
                for g in range(GROUPS):
                    if g < GROUPS - 1:
                        transpose_prob(g + 1)
                    pe.wait_ge(s_ed if (k + g) % 2 else s_ea, half + (k + g) // 2 + 1)
                    for j in group_tiles(g):
                        r = tile_rows(j)
                        for b in range(2):
                            x = pe.matmul(ps[b * SEQ:(b + 1) * SEQ, OB, :], probt[0:r, j, b * SEQ:(b + 1) * SEQ],
                                          ct[u][0:r, b, j, :], start=j == 0, stop=j == TILES - 1)
                x.then_inc(s_pv, 1)
            for u in range(2):
                pair(0, u, False, u == 0)
            with pe.Fori(1, PAIRS // 2 - 1) as i:
                for u in range(2):
                    pair(i, u, False, False)
            for u in range(2):
                pair(PAIRS // 2 - 1, u, u == 1, False)
            transpose_attended(PAIRS - 1)


def self_attention(nc, sem, area, ps, a, ident, qa, halves, tables, early):
    w = {"xwv": early.xwv, **early.weights}
    bv, bo = early.bv, area(D)
    mask = area(P)
    expdb = area(HEADS)
    ats = early.ats
    x = [early.x, area(2 * D)]
    x1s = [area(2 * D) for _ in range(2)]
    xn, x3 = area(2 * D), area(2 * D)
    x2b, b_dn = area(2 * D), area(2 * D)
    lnt, qt = area(DC, QROWS), area(DC, QROWS)
    kd = area(DC, HPC, QROWS)
    v = area(2, D)
    sc = [area(HPC, P) for _ in range(3)]
    pt = [area(HPC, P) for _ in range(2)]
    aot = area(DC, QROWS)
    nmx, rs = [area(HPC) for _ in range(3)], [area(HPC) for _ in range(3)]
    den, rden = [area(HPC) for _ in range(3)], [area(HPC) for _ in range(3)]
    norms = [[area(2, 6), area(2, 2), area(2), area(2)] for _ in range(2)]
    x_h = a["x"].rearrange("(q n r) d -> q n (r d)", q=QUADS, r=2)
    ITEMS = 2 * DC
    SCALE = HD ** -0.5
    HALVES = (slice(0, D), slice(D, 2 * D))

    s_c, s_x = sem("se_c"), [early.s_x, sem("se_x1")]
    s_t, s_out = sem("se_t"), early.s_out
    S = Signals(sem, "se_", {
        "pe": ("p1", "lt", "q", "k", "v", "s", "pt", "pv", "o"),
        "act": ("edb", "lte", "ke", "ex", "pte_a"),
        "dve": ("r1", "x1b", "stat", "mv", "xn", "qe", "ve", "sm", "mx", "den", "rd", "pte_d", "pve", "r2", "x2",
                "stat2", "mv2", "x2b", "x3"),
        "pool": ("kd0", "m0", "m1", "z", "ats", "veps", "rstd", "nrm", "veps2", "rstd2"),
        "sp": ("stored",),
    }, {"p1": 2, "lt": 2, "lte": 2, "q": 2, "k": 2, "v": 2, "qe": 2, "ve": 2, "o": 2, "ke": DC * HPC, "ex": HPC,
        "r1": 2, "x1b": 2, "stat": 2, "mv": 2, "xn": 2, "r2": 2, "x2": 2, "stat2": 2, "mv2": 2, "x3": 2})
    past = S.past

    with nc.Block() as block:
        @block.sync
        def _(sp):
            S.start(sp, "sp")
            sp.dma_start(x[1], x_h[1, :, :]).then_inc(s_x[1], 16)
            sp.dma_start(bo, a["bo"].to_broadcast([P, D])).then_inc(s_c, 16)
            sp.dma_start(expdb, a["db"].to_broadcast([P, HEADS])).then_inc(s_c, 16)
            sp.dma_start(b_dn, a["b_dn"].to_broadcast([P, 2 * D])).then_inc(s_c, 16)
            past(sp, "z", 2)
            for k in range(2):
                r = slice(k * E, (k + 1) * E)
                for n, (up, dn) in enumerate((("a_up", "a_dn"), ("b_up_f", "b_dn_f"))):
                    sp.dma_start(tables["up"][n][r, :, k, :], a[up]).then_inc(s_t, 16)
                    sp.dma_start(tables["dn"][n][r, :, :], a[dn]).then_inc(s_t, 16)
                sp.dma_start(tables["b_up"][r, :], a["b_up"]).then_inc(s_t, 16)
                sp.dma_start(tables["scales"][:, k:k + 1], a[("s_up", "s_dn")[k]].to_broadcast([P, 1]))\
                  .then_inc(s_t, 16)
            sp.dma_start(tables["wr_up"], a["wr_up"].rearrange("(c p) e -> p c e", p=P)).then_inc(s_t, 16)
            sp.dma_start(tables["iota"], a["iota"].to_broadcast([P, E])).then_inc(s_t, 16)

            def quad(i, u, more, final=False):
                q = i * 2 + u
                if more:
                    past(sp, "r1", q + 1)
                    sp.dma_start(x[u], x_h[bass.ds(q + 2, 1), :, :].rearrange("q n d -> n (q d)"))\
                      .then_inc(s_x[u], 16)
                past(sp, "x2b", q + 1)
                past(sp, "x3", q + 1)
                for n, tile in (("x2", x2b), ("x3", x3)):
                    sp.dma_start(a[n][bass.ds(q, 1), :, :].rearrange("q n d -> n (q d)"), tile).then_inc(s_out, 16)
                if not final:
                    sp.wait_ge(s_out, (q + 1) * 32)
                    sp.sem_inc(S["stored"], 1)
            with sp.Fori(0, QUADS // 2 - 1) as i:
                for u in range(2):
                    quad(i, u, True)
            quad(QUADS // 2 - 1, 0, False)
            past(sp, "p1", QUADS)
            for t in range(2):
                sp.dma_start(early.xwv.rearrange("p c e -> p (c e)")[:, t * 2 * D:(t + 1) * 2 * D], a["x3"][t, :, :])\
                  .then_inc(early.s_x3, 16)
            quad(QUADS // 2 - 1, 1, False, True)
            sp.wait_ge(s_t, 14 * 16)

        @block.gpsimd
        def _(pool):
            S.start(pool, "pool")

            def stage_attended(q):
                pool.tensor_copy(ats, qa[:, :, bass.ds(q * QROWS, QROWS)]).then_inc(S["ats"], 1)
            pool.sem_inc(S["ats"], 1)
            pool.memset(kd, 0.0).then_inc(S["kd0"], 1)
            pool.memset(mask, 0.0).then_inc(S["m0"], 1)
            past(pool, "m0", 1)
            pool.affine_select(out=mask, in_=mask, compare_op=ALU.is_ge, fill=MASKED, base=0,
                               pattern=[[-1, P]], channel_multiplier=1).then_inc(S["m0"], 1)
            past(pool, "m0", 2)
            pool.affine_select(out=mask[SEQ:P, 0:SEQ], in_=mask[SEQ:P, 0:SEQ], compare_op=ALU.is_gt,
                               fill=MASKED, base=-1, pattern=[[0, SEQ]], channel_multiplier=0).then_inc(S["m1"], 1)
            def rstd(which, mv, veps, done, n):
                past(pool, mv, n + 1)
                _, m, ve, r = norms[which]
                layer_norm_rstd(pool, m, ve, r, halves, S, veps, done, n)

            def quad(q, more):
                if more:
                    past(pool, "p1", q + 1)
                    stage_attended(q + 1)
                for n in range(ITEMS):
                    past(pool, "rd", q * ITEMS + n + 1)
                    pool.tensor_tensor(sc[n % 3], sc[n % 3],
                                       rden[n % 3].unsqueeze(2).to_broadcast([P, HPC, P]), ALU.mult)\
                        .then_inc(S["nrm"], 1)
                if more:
                    rstd(0, "mv", "veps", "rstd", q + 1)
                rstd(1, "mv2", "veps2", "rstd2", q)
            past(pool, "m1", 1)
            rstd(0, "mv", "veps", "rstd", 0)
            for z in tables["up"]:
                pool.memset(z, 0.0).then_inc(S["z"], 1)
            with pool.Fori(0, QUADS - 1) as q:
                quad(q, True)
            quad(QUADS - 1, False)

        @block.vector
        def _(vec):
            S.start(vec, "dve")

            def front(q, u, i):
                x1 = x1s[u]
                stats, mv, _, rstd = norms[0]
                vec.wait_ge(early.s_bv, 16)
                vec.wait_ge(s_x[u], i * 16 + 16)
                for par, r in enumerate(HALVES):
                    vec.wait_ge(S["p1"], q * 2 + par + 1 + S.CREDIT)
                    vec.tensor_tensor(x1[:, r], ps[:, 2 + par, :], x[u][:, r], ALU.add).then_inc(S["r1"], 1)
                past(vec, "r1", q + 1)
                for r in HALVES:
                    vec.tensor_tensor(x1[:, r], x1[:, r], bv, ALU.add).then_inc(S["x1b"], 1)
                past(vec, "x1b", q + 1)
                layer_norm_stats(vec, stats, mv, x1, S, "stat", "mv", q)
                past(vec, "rstd", q + 1)
                past(vec, "mv", q + 1)
                for par, r in enumerate(HALVES):
                    vec.tensor_scalar(xn[:, r], x1[:, r], mv[:, par, 0:1], rstd[:, par:par + 1],
                                      ALU.subtract, ALU.mult).then_inc(S["xn"], 1)

            def back(q, u):
                x1 = x1s[u]
                stats, mv, _, rstd = norms[1]
                for par, r in enumerate(HALVES):
                    vec.wait_ge(S["o"], q * 2 + par + 1 + S.CREDIT)
                    vec.tensor_tensor(x1[:, r], ps[:, 4 + par, :], x1[:, r], ALU.add).then_inc(S["r2"], 1)
                past(vec, "r2", q + 1)
                for r in HALVES:
                    vec.tensor_tensor(x1[:, r], x1[:, r], bo, ALU.add).then_inc(S["x2"], 1)
                past(vec, "x2", q + 1)
                layer_norm_stats(vec, stats, mv, x1, S, "stat2", "mv2", q)
                past(vec, "stored", q)
                vec.tensor_tensor(x2b, x1, b_dn, ALU.add).then_inc(S["x2b"], 1)
                past(vec, "rstd2", q + 1)
                past(vec, "mv2", q + 1)
                for par, r in enumerate(HALVES):
                    vec.tensor_scalar(x3[:, r], x1[:, r], mv[:, par, 0:1], rstd[:, par:par + 1],
                                      ALU.subtract, ALU.mult).then_inc(S["x3"], 1)

            def quad(i, u, more):
                q = i * 2 + u
                for m in range(2):
                    vec.wait_ge(S["q"], q * 2 + m + 1 + S.CREDIT)
                    vec.tensor_copy(qt[:, 2 * m:2 * m + 2, :], ps[:, 2 + m, :].rearrange("p (m n) -> p m n", m=2))\
                       .then_inc(S["qe"], 1)

                def values(pair):
                    vec.wait_ge(S["v"], q * 2 + pair + 1 + S.CREDIT)
                    vec.tensor_copy(v[:, pair, :], ps[:, 6 + pair, :]).then_inc(S["ve"], 1)

                def soften(n):
                    past(vec, "s", q * ITEMS + n + 1)
                    past(vec, "pt", q * ITEMS + max(n - 2, 0))
                    vec.scalar_tensor_tensor(sc[n % 3], ps[:, 4 + n % 2, :].rearrange("p (h t) -> p h t", h=HPC),
                                             SCALE, mask.unsqueeze(1).to_broadcast([P, HPC, P]),
                                             ALU.mult, ALU.add).then_inc(S["sm"], 1)
                    past(vec, "sm", q * ITEMS + n + 1)
                    vec.tensor_reduce(nmx[n % 3], sc[n % 3], AX.X, ALU.max, negate=True).then_inc(S["mx"], 1)

                def denominators(n):
                    m = n % DC
                    past(vec, "ex", q * ITEMS + n + 1)
                    vec.tensor_tensor(den[n % 3], rs[n % 3], expdb[:, m * HPC:(m + 1) * HPC], ALU.add)\
                       .then_inc(S["den"], 1)
                    past(vec, "den", q * ITEMS + n + 1)
                    vec.reciprocal(rden[n % 3], den[n % 3]).then_inc(S["rd"], 1)

                def result(n):
                    pair, m = divmod(n, DC)
                    past(vec, "pv", q * ITEMS + n + 1)
                    vec.tensor_copy(aot[:, m, pair * P:(pair + 1) * P], ps[:, 6 + n % 2, 0:P])\
                       .then_inc(S["pve"], 1)
                for n in range(ITEMS + 4):
                    if n < ITEMS:
                        soften(n)
                    if 1 <= n <= ITEMS:
                        denominators(n - 1)
                    if n in (1, 2):
                        values(n - 1)
                    if 2 <= n < ITEMS + 2 and (n - 2) % 2:
                        past(vec, "pt", q * ITEMS + n - 1)
                        past(vec, "pv", q * ITEMS + max(n - 3, 0))
                        vec.tensor_copy(pt[(n - 2) % 2], ps[:, n % 2, :].rearrange("p (h t) -> p h t", h=HPC))\
                           .then_inc(S["pte_d"], 1)
                    if n >= 4:
                        result(n - 4)
                if more:
                    front(q + 1, 1 - u, i if u == 0 else i + 1)
                back(q, u)
            front(0, 0, 0)
            vec.wait_ge(s_c, 48)
            past(vec, "m1", 1)
            past(vec, "edb", 1)
            with vec.Fori(0, QUADS // 2 - 1) as i:
                for u in range(2):
                    quad(i, u, True)
            for u in range(2):
                quad(QUADS // 2 - 1, u, u == 0)

        @block.scalar
        def _(act):
            S.start(act, "act")
            act.wait_ge(s_c, 48)
            act.activation(expdb, expdb, ACT.Exp).then_inc(S["edb"], 1)
            past(act, "kd0", 1)
            with act.Fori(0, QUADS) as q:
                for par in range(2):
                    act.wait_ge(S["lt"], q * 2 + par + 1 + S.CREDIT)
                    act.copy(lnt[:, :, par::2], ps[:, par, :].rearrange("p (c n) -> p c n", c=DC))\
                       .then_inc(S["lte"], 1)
                for m in range(DC):
                    act.wait_ge(S["k"], q * 2 + m // 2 + 1 + S.CREDIT)
                    for h in range(HPC):
                        r = slice(h * HD, (h + 1) * HD)
                        act.copy(kd[r, m, h, :], ps[r, 4 + m // 2, (m % 2) * QROWS:(m % 2 + 1) * QROWS])\
                           .then_inc(S["ke"], 1)
                for n in range(ITEMS + 2):
                    if n < ITEMS:
                        past(act, "mx", q * ITEMS + n + 1)
                        for h in range(HPC):
                            act.activation(sc[n % 3][:, h, :], sc[n % 3][:, h, :], ACT.Exp,
                                           bias=nmx[n % 3][:, h:h + 1],
                                           accum_out=rs[n % 3][:, h:h + 1]).then_inc(S["ex"], 1)
                    if n >= 2 and (n - 2) % 2 == 0:
                        past(act, "pt", q * ITEMS + n - 1)
                        past(act, "pv", q * ITEMS + max(n - 3, 0))
                        act.copy(pt[(n - 2) % 2], ps[:, n % 2, :].rearrange("p (h t) -> p h t", h=HPC))\
                           .then_inc(S["pte_a"], 1)

        @block.tensor
        def _(pe):
            S.start(pe, "pe")

            def values(par, c):
                x = pe.matmul(ps[:, 2 + par, :], ats[:, c, par::2], w["xwv"][:, c, :], start=c == 0, stop=c == DC - 1)
                if c == DC - 1:
                    x.then_inc(S["p1"], 1)

            def quad(q, more):
                past(pe, "pte_a", q * (ITEMS // 2))
                past(pe, "pte_d", q * (ITEMS // 2))
                for par in range(2):
                    pe.wait_ge(S["xn"], q * 2 + par + 1 + S.CREDIT)
                    for c in range(DC):
                        last = pe.transpose(ps[:, par, c * P:(c + 1) * P],
                                            xn[:, par * D + c * P:par * D + (c + 1) * P], ident)
                    last.then_inc(S["lt"], 1)
                past(pe, "lte", q + 1)
                for n, bank in (("swq", 2), ("swk", 4)):
                    if n == "swk":
                        past(pe, "r2", q)
                    for m in range(DC):
                        for c in range(DC):
                            last = pe.matmul(ps[:, bank + m // 2, (m % 2) * QROWS:(m % 2 + 1) * QROWS],
                                             w[n][:, c, m * P:(m + 1) * P], lnt[:, c, :],
                                             start=c == 0, stop=c == DC - 1)
                        if m % 2:
                            last.then_inc(S["q" if n == "swq" else "k"], 1)
                own = [(pair, c) for pair in range(2) for c in range(DC)]
                ahead = [(par, c) for par in range(2) for c in range(DC)] if more else []
                past(pe, "qe", q + 1)
                if more:
                    past(pe, "ats", q + 2)
                def fill():
                    nonlocal own, ahead
                    for pair, c in own[0:3]:
                        x = pe.matmul(ps[:, 6 + pair, :], lnt[:, c, pair * P:(pair + 1) * P],
                                      w["swv"][:, c, :], start=c == 0, stop=c == DC - 1)
                        if c == DC - 1:
                            x.then_inc(S["v"], 1)
                    own = own[3:]
                    if n >= 3 and ahead:
                        values(*ahead.pop(0))
                for n in range(ITEMS + 3):
                    if n == 0:
                        fill()
                    if n < ITEMS:
                        pair, m = divmod(n, DC)
                        if n < DC:
                            pe.wait_ge(S["ke"], q * DC * HPC + (m + 1) * HPC + S.CREDIT)
                        if n == DC - 1 or n < 2:
                            past(pe, "ke", q + 1)
                        if n >= 2:
                            past(pe, "sm", q * ITEMS + n - 1)
                        pe.matmul(ps[:, 4 + n % 2, :], qt[:, m, pair * P:(pair + 1) * P],
                                  kd[:, m, :, pair * P:(pair + 1) * P], start=True, stop=True).then_inc(S["s"], 1)
                    if n > 0:
                        fill()
                    if 2 <= n < ITEMS + 2:
                        k = n - 2
                        past(pe, "nrm", q * ITEMS + k + 1)
                        if k >= 2:
                            past(pe, "pte_d" if k % 2 else "pte_a", q * (ITEMS // 2) + k // 2)
                        for h in range(HPC):
                            last = pe.transpose(ps[:, k % 2, h * P:(h + 1) * P], sc[k % 3][:, h, :], ident)
                        last.then_inc(S["pt"], 1)
                    if n >= 3:
                        k = n - 3
                        pair, m = divmod(k, DC)
                        if m == 0:
                            pe.wait_ge(S["ve"], q * 2 + pair + 1 + S.CREDIT)
                        past(pe, "pte_d" if k % 2 else "pte_a", q * (ITEMS // 2) + k // 2 + 1)
                        if k >= 2:
                            past(pe, "pve", q * ITEMS + k - 1)
                        for h in range(HPC):
                            head = m * HPC + h
                            last = pe.matmul(ps[h * HD:(h + 1) * HD, 6 + k % 2, 0:P],
                                             v[:, pair, head * HD:(head + 1) * HD], pt[k % 2][:, h, :],
                                             start=True, stop=True)
                        last.then_inc(S["pv"], 1)
                past(pe, "sm", (q + 1) * ITEMS)
                past(pe, "pve", (q + 1) * ITEMS)
                for par in range(2):
                    for c in range(DC):
                        last = pe.matmul(ps[:, 4 + par, :], aot[:, c, par::2], w["swo"][:, c, :],
                                         start=c == 0, stop=c == DC - 1)
                    last.then_inc(S["o"], 1)
            pe.wait_ge(early.s_xwv, 16)
            past(pe, "ats", 1)
            for par in range(2):
                for c in range(DC):
                    values(par, c)
            pe.wait_ge(early.s_w, 4 * 16)
            with pe.Fori(0, QUADS - 1) as q:
                quad(q, True)
            quad(QUADS - 1, False)


def mixture(nc, sem, area, low, early, ps, a, ident, h_at, tables, out):
    tab_up, tab_dn, wr_up, b_up, scales, iota = (tables[n] for n in ("up", "dn", "wr_up", "b_up", "scales", "iota"))
    wr_dn = area(F1, E)
    h = h_at.rearrange("p (g j) -> p g j", j=F1)
    gath = [low(64 * P), area(64 * P)]
    x2b = area(2, 2 * D)
    cols = area(4 * D)
    xrep = cols.rearrange("p (j g) -> p j g", g=P)
    lg = area(2, E)
    x3s = early.xwv.rearrange("p c e -> p (c e)").rearrange("p (t f) -> p t f", t=2)
    stage = [[area(8 * F1) for _ in range(3)] for _ in range(2)]
    mid = [area(8 * F1) for _ in range(2)]
    oh = area(2, 2, 2, P)
    top, top_i, top_f = area(2, 8), area(2, 8, dt=U32), area(2, 2)
    diff, ex, den, prob = area(2), area(2), area(2), area(2, 2)
    xft = gath[0].rearrange("p (t c n) -> p t c n", t=8, c=8)[:, 0:2]
    wbd = gath[0].rearrange("p (q t e) -> p q t e", q=F1, t=2)
    oht = gath[0][:, 60 * P:64 * P].rearrange("p (v t k e) -> p v t k e", v=2, t=2, k=2)
    oh_up = mid[0].rearrange("p (v t g) -> p v t g", v=2, t=2)
    ybuf = cols.rearrange("p (t g o) -> p t g o", t=2, o=D1)
    yt = h_at[:, 0:4 * D].rearrange("p (t o q) -> p t o q", t=2, o=D1)
    NT = QUADS // 2
    G8, NS = 8, P // 8
    XB = 4
    GB = 16

    plain = {"x3": early.s_x3, **{n: sem("mo_" + n) for n in ("wr", "x2", "out", "oh0")}}
    S = Signals(sem, "mo_", {
        "pe": ("xf", "lg_up", "lg_dn", "xr", "oht_up", "oht_dn", "ga_up", "gb_up", "ga_dn", "gb_dn",
               "s1_up", "s2_up", "s1_dn", "s2_dn"),
        "act": ("wa", "sta_up", "sta_dn", "xfe", "xre", "ex_up", "ex_dn", "gae_up", "gae_dn", "me_up", "me_dn",
                "gelu", "ye"),
        "dve": ("wd", "lge", "top", "idx", "idf", "df", "soft", "ohr", "ohp", "ohe_up", "ohe_dn",
                "gbe_up", "gbe_dn", "stb_up", "stb_dn", "hb", "yt", "res"),
        "pool": ("stx_up", "stx_dn", "wz", "xz"),
    }, {"stx_up": 8, "xz": 2, "wz": 2,
        "s1_up": 2, "s2_up": 2, "s1_dn": 2, "s2_dn": 2})
    past, start = S.past, S.start

    def s(n):
        return plain[n] if n in plain else S[n]

    def stage_views(lv, u):
        sx, sa, sb = stage[u]
        if lv == "up":
            return (sx.rearrange("p (g k j) -> p g k j", k=2, j=D1),
                    sa.rearrange("p (g o) -> p g o", o=F1), sb.rearrange("p (g o) -> p g o", o=F1))
        return (sx.rearrange("p (c r j) -> p c r j", c=4, r=2),
                sa.rearrange("p (c r k o) -> p c r k o", c=4, r=2, k=2),
                sb.rearrange("p (c r k o) -> p c r k o", c=4, r=2, k=2))

    def stage_factor(copy, lv, u, which, n, done):
        dst = stage_views(lv, u)[1 + which]
        if lv == "up":
            src = gath[which].rearrange("p (o g) -> p g o", g=P)[:, bass.ds(n * G8, G8), :]
            copy(dst, src).then_inc(done, 1)
        else:
            src = gath[which].rearrange("p (o k c g) -> p c g k o", k=2, c=4, g=32)
            for k in range(2):
                x = copy(dst[:, :, :, k, :], src[:, :, bass.ds(n * 2, 2), k, :])
            x.then_inc(done, 1)

    with nc.Block() as block:
        @block.sync
        def _(sp):
            x3_d, x2_d = a["x3"], a["x2"]
            sp.wait_ge(early.s_out, QUADS * 32)
            out_v = out.rearrange("(q n r) d -> q n (r d)", q=QUADS, r=2)

            def load(dst, src, q, done):
                for t in range(2):
                    sp.dma_start(dst[:, t, :], src[bass.ds(q * 2 + t, 1), :, :].rearrange("q n d -> n (q d)"))\
                      .then_inc(s(done), 16)

            def tile(T, last):
                past(sp, "xr", T * XB + XB)
                load(x3s, x3_d, 0 if last else T + 1, "x3")
                load(x2b, x2_d, T, "x2")
                past(sp, "res", T * 2 + 2)
                for t in range(2):
                    sp.dma_start(out_v[bass.ds(T * 2 + t, 1), :, :].rearrange("q n d -> n (q d)"), x2b[:, t, :])\
                      .then_inc(s("out"), 16)
                sp.wait_ge(s("out"), T * 32 + 32)
                apart(sp, SPARE)
            for t in range(2):
                sp.dma_start(wr_dn[t * F1:(t + 1) * F1, :, :], a["wr_dn"]).then_inc(s("wr"), 16)
            with sp.Fori(0, NT - 1) as T:
                tile(T, False)
            tile(NT - 1, True)

        @block.gpsimd
        def _(pool):
            start(pool, "pool")
            pool.wait_ge(early.s_out, QUADS * 32)
            with pool.Fori(0, NT) as T:
                for lv in ("up", "dn"):
                    if lv == "up":
                        past(pool, "s1_dn", T * NS)
                        past(pool, "stx_dn", T * NS)
                        apart(pool, SPARE)
                        for u in range(2):
                            pool.memset(stage[u][0], 0.0).then_inc(s("xz"), 1)
                        past(pool, "xz", T + 1)
                        past(pool, "xre", T * XB + XB)
                    else:
                        past(pool, "gelu", T * NS + NS)
                        past(pool, "wz", T + 1)
                    apart(pool, SPARE)
                    with pool.Fori(0, NS // 2) as i:
                        for u in range(2):
                            n = i * 2 + u
                            past(pool, "s1_" + lv, T * NS + n - 1)
                            dst = stage_views(lv, u)[0]
                            if lv == "up":
                                for q in range(4):
                                    r = slice(q * D1, (q + 1) * D1)
                                    for par in range(2):
                                        at = (q // 2 * 2 + par) * D1
                                        src = xrep[at:at + D1, :, bass.ds(n * G8, G8)].rearrange("p j g -> p g j")
                                        pool.tensor_copy(dst[r, :, q % 2, par::2], src).then_inc(s("stx_up"), 1)
                            else:
                                src = h.rearrange("p (c g) j -> p c g j", c=4)[:, :, bass.ds(n * 2, 2), :]
                                pool.tensor_copy(dst, src).then_inc(s("stx_dn"), 1)
                    if lv == "up":
                        past(pool, "stx_up", T * NS + NS)
                        past(pool, "sta_up", T * NS + NS)
                        apart(pool, SPARE)
                        for t in range(2):
                            pool.memset(wbd[t * F1:(t + 1) * F1, :, 1 - t, :], 0.0).then_inc(s("wz"), 1)

        def choose(vec, T, lv):
            m = T * 2 + (lv == "dn")
            past(vec, "lg_" + lv, T * 2 + 2 if lv == "up" else T + 1)
            src = ps[:, 6:8, 0:E] if lv == "up" else ps[:, 5, 0:P].rearrange("p (t e) -> p t e", t=2)
            vec.tensor_copy(lg, src).then_inc(s("lge"), 1)
            past(vec, "lge", m + 1)
            apart(vec, SPARE)
            for t in range(2):
                vec.max(top[:, t, :], lg[:, t, :]).then_inc(s("top"), 1)
            past(vec, "top", m * 2 + 2)
            apart(vec, SPARE)
            for t in range(2):
                vec.max_index(top_i[:, t, :], top[:, t, :], lg[:, t, :]).then_inc(s("idx"), 1)
            vec.tensor_tensor(diff, top[:, :, 1], top[:, :, 0], ALU.subtract).then_inc(s("df"), 1)
            past(vec, "idx", m * 2 + 2)
            vec.tensor_copy(top_f, top_i[:, :, 0:2]).then_inc(s("idf"), 1)
            past(vec, "idf", m + 1)
            past(vec, "ex_" + lv, T + 1)
            vec.tensor_scalar(den, ex, 1.0, None, ALU.add).then_inc(s("soft"), 1)
            past(vec, "soft", m * 3 + 1)
            vec.reciprocal(prob[:, :, 0], den).then_inc(s("soft"), 1)
            past(vec, "soft", m * 3 + 2)
            vec.tensor_tensor(prob[:, :, 1], ex, prob[:, :, 0], ALU.mult).then_inc(s("soft"), 1)
            past(vec, "soft", m * 3 + 3)

        def one_hot(vec, T, lv):
            m = T * 2 + (lv == "dn")
            if lv == "up":
                past(vec, "sta_dn", T * NS)
            vec.tensor_tensor(oht[:, 1], iota.unsqueeze(1).unsqueeze(1).to_broadcast([P, 2, 2, E]),
                              top_f.unsqueeze(3).to_broadcast([P, 2, 2, E]), ALU.is_equal).then_inc(s("ohr"), 1)
            past(vec, "ohr", m + 1)
            vec.tensor_tensor(oht[:, 0], oht[:, 1], prob.unsqueeze(3).to_broadcast([P, 2, 2, E]), ALU.mult)\
               .then_inc(s("ohp"), 1)

        def choices_out(vec, T, lv, v):
            past(vec, "oht_" + lv, T * 2 + 2 - v)
            src = ps[:, 4 + v, 0:2 * P].rearrange("p (t g) -> p t g", t=2)
            if lv == "up":
                vec.tensor_copy(oh_up[:, v], src).then_inc(s("ohe_up"), 1)
            else:
                for k in range(2):
                    r = slice(k * E, (k + 1) * E)
                    vec.tensor_copy(oh[r, :, v, k, :], src[r]).then_inc(s("ohe_dn"), 1)

        def gather_out(e, copy, T, lv, which, done):
            for b in range(GB):
                past(e, ("ga_", "gb_")[which] + lv, T * GB + b + 1)
                if b == 0 and lv == "dn":
                    past(e, ("sta_up", "stb_up")[which], T * NS + NS)
                if b == 0 and lv == "up":
                    past(e, ("sta_dn", "stb_dn")[which], T * NS)
                copy(gath[which][:, b * 512:(b + 1) * 512], ps[:, 2 * which + b % 2, :]).then_inc(done, 1)

        @block.vector
        def _(vec):
            start(vec, "dve")
            vec.wait_ge(early.s_out, QUADS * 32)
            vec.memset(oh, 0.0).then_inc(s("oh0"), 1)
            vec.wait_ge(s("oh0"), 1)
            choose(vec, 0, "up")
            one_hot(vec, 0, "up")
            with vec.Fori(0, NT) as T:
                choices_out(vec, T, "up", 1)
                choices_out(vec, T, "up", 0)
                gather_out(vec, vec.tensor_copy, T, "up", 1, s("gbe_up"))
                past(vec, "gbe_up", T * GB + GB)

                def stage_b(lv, n, u):
                    past(vec, "s2_" + lv, T * NS + n - 1)
                    stage_factor(vec.tensor_copy, lv, u, 1, n, s("stb_" + lv))

                def biased(n, u):
                    N = T * NS + n
                    past(vec, "s2_up", N + 1)
                    vec.scalar_tensor_tensor(h[:, bass.ds(n * G8, G8), :],
                                             ps[:, 6 + u, :].rearrange("p (g o) -> p g o", o=F1), scales[:, 0:1],
                                             b_up.unsqueeze(1).to_broadcast([P, G8, F1]), ALU.mult, ALU.add)\
                       .then_inc(s("hb"), 1)
                for u in range(2):
                    stage_b("up", u, u)
                with vec.Fori(0, NS // 2 - 1) as i:
                    for u in range(2):
                        biased(i * 2 + u, u)
                        stage_b("up", i * 2 + u + 2, u)
                vec.wait_ge(s("wr"), 32)
                past(vec, "sta_up", T * NS + NS)
                vec.tensor_copy(wbd[0:F1, :, 0, :], wr_dn[0:F1, :, :]).then_inc(s("wd"), 1)
                for u in range(2):
                    biased(NS - 2 + u, u)
                choose(vec, T, "dn")
                one_hot(vec, T, "dn")
                choices_out(vec, T, "dn", 1)
                choices_out(vec, T, "dn", 0)
                choose(vec, T + 1, "up")
                gather_out(vec, vec.tensor_copy, T, "dn", 1, s("gbe_dn"))
                past(vec, "gbe_dn", T * GB + GB)
                apart(vec, SPARE)
                with vec.Fori(0, NS // 2) as i:
                    for u in range(2):
                        stage_b("dn", i * 2 + u, u)
                one_hot(vec, T + 1, "up")
                past(vec, "ye", T * NS + NS)
                past(vec, "stx_dn", T * NS + NS)
                for t in range(2):
                    vec.transpose(yt[:, t, :, :].rearrange("n o p -> n p o"),
                                  ybuf[:, t, :, :].rearrange("q g p -> q p g")).then_inc(s("yt"), 1)
                vec.wait_ge(s("x2"), T * 32 + 32)
                for t in range(2):
                    past(vec, "yt", T * 2 + t + 1)
                    vec.scalar_tensor_tensor(x2b[:, t, :], yt[:, t, :, :].rearrange("n o p -> n (o p)"),
                                             scales[:, 1:2], x2b[:, t, :], ALU.mult, ALU.add)\
                       .then_inc(s("res"), 1)

        @block.scalar
        def _(act):
            start(act, "act")

            def rows_out(T, banks):
                for b in banks:
                    past(act, "xf", T * 4 + b + 1)
                    act.copy(xft[:, b // 2, b % 2 * 4:b % 2 * 4 + 4, :],
                             ps[:, b, :].rearrange("p (c n) -> p c n", c=4)).then_inc(s("xfe"), 1)

            def exponential(T):
                past(act, "df", T * 2 + 1)
                act.activation(ex, diff, ACT.Exp).then_inc(s("ex_up"), 1)
            rows_out(0, range(4))
            act.wait_ge(early.s_out, QUADS * 32)
            exponential(0)
            with act.Fori(0, NT) as T:
                past(act, "yt", T * 2)
                for b in range(XB):
                    past(act, "xr", T * XB + b + 1)
                    act.copy(xrep[:, 4 * b:4 * b + 4, :], ps[:, b, :].rearrange("p (j g) -> p j g", j=4))\
                       .then_inc(s("xre"), 1)
                gather_out(act, act.copy, T, "up", 0, s("gae_up"))

                def mid_out(lv, n, u):
                    past(act, "s1_" + lv, T * NS + n + 1)
                    past(act, "s2_" + lv, T * NS + n - 1)
                    act.copy(mid[u], ps[:, 4 + u, :]).then_inc(s("me_" + lv), 1)

                def gelu(n, u):
                    past(act, "hb", T * NS + n + 1)
                    act.activation(h[:, bass.ds(n * G8, G8), :], h[:, bass.ds(n * G8, G8), :], ACT.Gelu)\
                       .then_inc(s("gelu"), 1)
                def stage_a(lv, n, u):
                    past(act, "s1_" + lv, T * NS + n - 1)
                    stage_factor(act.copy, lv, u, 0, n, s("sta_" + lv))

                def steps(lv, finish):
                    past(act, "gae_" + lv, T * GB + GB)
                    stage_a(lv, 0, 0)
                    stage_a(lv, 1, 1)
                    mid_out(lv, 0, 0)
                    with act.Fori(0, NS // 2 - 1) as i:
                        for u in range(2):
                            stage_a(lv, i * 2 + u + 2, u)
                            mid_out(lv, i * 2 + u + 1, 1 - u)
                            finish(i * 2 + u, u)
                    mid_out(lv, NS - 1, 1)
                    if lv == "up":
                        act.wait_ge(s("wr"), 32)
                        past(act, "sta_up", T * NS + NS)
                        act.copy(wbd[F1:P, :, 1, :], wr_dn[F1:P, :, :]).then_inc(s("wa"), 1)
                    finish(NS - 2, 0)
                    finish(NS - 1, 1)
                steps("up", gelu)
                past(act, "lg_dn", T + 1)
                rows_out(T + 1, range(2))
                past(act, "df", T * 2 + 2)
                act.activation(ex, diff, ACT.Exp).then_inc(s("ex_dn"), 1)
                rows_out(T + 1, range(2, 4))
                exponential(T + 1)
                gather_out(act, act.copy, T, "dn", 0, s("gae_dn"))

                def y_out(n, u):
                    past(act, "s2_dn", T * NS + n + 1)
                    act.copy(ybuf[:, :, bass.ds(n * 2, 2), :],
                             ps[:, 2 * u:2 * u + 2, 0:2 * D1].rearrange("p t (r o) -> p t r o", r=2))\
                       .then_inc(s("ye"), 1)
                steps("dn", y_out)


        @block.tensor
        def _(pe):
            start(pe, "pe")

            def transpose_choices(T, lv):
                for v in (1, 0):
                    past(pe, "ohr" if v else "ohp", T * 2 + (lv == "dn") + 1)
                    for t in range(2):
                        last = pe.transpose(ps[:, 4 + v, t * P:(t + 1) * P],
                                            oht[:, v, t, :, :].rearrange("p k e -> p (k e)"), ident)
                    last.then_inc(s("oht_" + lv), 1)

            def gather(T, lv):
                width = P if lv == "up" else 2 * P
                each = 1 if lv == "up" else 2
                past(pe, "ohe_" + lv, (T * 2 + 1) * each)
                for v, banks in ((1, range(GB - 2)), (0, range(GB)), (1, range(GB - 2, GB))):
                    if v == 0:
                        past(pe, "ohe_" + lv, (T * 2 + 2) * each)
                    for b in banks:
                        if b >= 2:
                            past(pe, ("gae_", "gbe_")[v] + lv, T * GB + b - 1)
                        for r in range(512 // width):
                            o = b * (512 // width) + r
                            for t in range(2):
                                w = tab_up[v][:, o, :, :].rearrange("p k i -> p (k i)") if lv == "up" \
                                    else tab_dn[v][:, o, :]
                                x = oh_up[:, v, t, :] if lv == "up" \
                                    else oh[:, t, v, :, :].rearrange("p k g -> p (k g)")
                                last = pe.matmul(ps[t * E:(t + 1) * E, 2 * v + b % 2, r * width:(r + 1) * width],
                                                 w, x, start=True, stop=True)
                        last.then_inc(s(("ga_", "gb_")[v] + lv), 1)

            def first(T, lv, n, u):
                past(pe, "stx_" + lv, T * NS + n + 1)
                past(pe, "sta_" + lv, T * NS + n + 1)
                past(pe, "me_" + lv, T * NS + n - 1)
                apart(pe, SPARE)
                sx, sa, _ = stage[u]
                for g in range(G8):
                    for t in range(2):
                        r = slice(64 * t, 64 * t + 64)
                        x = pe.matmul(ps[r, 4 + u, g * F1:(g + 1) * F1], sx[r, g * F1:(g + 1) * F1],
                                      sa[r, g * F1:(g + 1) * F1], start=True, stop=True)
                        if g == G8 - 1:
                            x.then_inc(s("s1_" + lv), 1)

            def second(T, lv, n, u):
                past(pe, "stb_" + lv, T * NS + n + 1)
                past(pe, "me_" + lv, T * NS + n + 1)
                past(pe, "hb" if lv == "up" else "ye", T * NS + n - 1)
                apart(pe, SPARE)
                sb, md = stage[u][2], mid[u]
                if lv == "up":
                    for g in range(G8):
                        for t in range(2):
                            r = slice(64 * t, 64 * t + 64)
                            x = pe.matmul(ps[r, 6 + u, g * F1:(g + 1) * F1], md[r, g * F1:(g + 1) * F1],
                                          sb[r, g * F1:(g + 1) * F1], start=True, stop=True)
                            if g == G8 - 1:
                                x.then_inc(s("s2_up"), 1)
                else:
                    for half in range(2):
                        for t in range(2):
                            r = slice(64 * t, 64 * t + 64)
                            for k in range(2):
                                for c in range(4):
                                    at = (2 * c + half) * F1 + k * D1
                                    x = pe.matmul(ps[32 * c:32 * c + 32, 2 * u + t, half * D1:(half + 1) * D1],
                                                     md[r, at:at + D1], sb[r, at:at + D1], start=k == 0, stop=k == 1)
                            if half == 1:
                                x.then_inc(s("s2_dn"), 1)

            def steps(T, lv):
                first(T, lv, 0, 0)
                with pe.Fori(0, NS // 2 - 1) as i:
                    for u in range(2):
                        first(T, lv, i * 2 + u + 1, 1 - u)
                        second(T, lv, i * 2 + u, u)
                first(T, lv, NS - 1, 1)
                second(T, lv, NS - 2, 0)
                second(T, lv, NS - 1, 1)

            def route(T, between=lambda: None):
                pe.wait_ge(s("x3"), T * 32 + 32)
                for t in range(2):
                    for c in range(8):
                        last = pe.transpose(ps[:, 2 * t + c // 4, (c % 4) * P:(c % 4 + 1) * P],
                                            x3s[:, t, c * P:(c + 1) * P], ident)
                        if c % 4 == 3:
                            last.then_inc(s("xf"), 1)
                for t in range(2):
                    if t == 1:
                        between()
                    past(pe, "xfe", T * 4 + 2 * t + 2)
                    for c in range(8):
                        last = pe.matmul(ps[:, 6 + t, 0:E], xft[:, t, c, :], wr_up[:, c, :],
                                         start=c == 0, stop=c == 7)
                    last.then_inc(s("lg_up"), 1)
            route(0)
            with pe.Fori(0, NT) as T:
                past(pe, "ye", T * NS)
                past(pe, "xfe", T * 4 + 4)
                for b in range(XB):
                    if b == 2:
                        transpose_choices(T, "up")
                    for jj in range(4):
                        for q in range(4):
                            x = x3s[:, q // 2, :].rearrange("n (i j) -> n j i", j=D1)[:, 8 * b + 2 * jj + q % 2, :]
                            last = pe.matmul(ps[q * D1:(q + 1) * D1, b, jj * P:(jj + 1) * P],
                                             x, ident, start=True, stop=True)
                    last.then_inc(s("xr"), 1)
                past(pe, "xre", T * XB + XB)
                gather(T, "up")
                steps(T, "up")
                past(pe, "gelu", T * NS + NS)
                apart(pe, SPARE)
                past(pe, "wz", T + 1)
                past(pe, "wa", T + 1)
                past(pe, "wd", T + 1)
                for p in range(F1):
                    last = pe.matmul(ps[:, 5, 0:P], h[:, :, p], wbd[:, p, :, :].rearrange("p t e -> p (t e)"),
                                     start=p == 0, stop=p == F1 - 1)
                last.then_inc(s("lg_dn"), 1)
                route(T + 1, lambda: transpose_choices(T, "dn"))
                gather(T, "dn")
                steps(T, "dn")


_IN = ["x", "ctx", "wq", "wk", "bq", "bk", "bv", "xwv", "swq", "swk", "swv", "swo", "bo", "db",
       "wr_up", "wr_dn", "a_up", "b_up_f", "a_dn", "b_dn_f", "iota", "b_up", "b_dn", "s_up", "s_dn"]


def kernel(x, ctx_1024, L0_xattn_Wq, L0_xattn_bq, L0_xattn_Wk, L0_xattn_bk, L0_xattn_Wv, L0_xattn_bv,
           L0_attn_Wq, L0_attn_Wk, L0_attn_Wv, L0_attn_Wo, L0_attn_bo, L0_attn_denom_bias,
           L0_ffn_W_up, L0_ffn_A_up, L0_ffn_B_up, L0_ffn_scale_up, L0_ffn_bias_up,
           L0_ffn_W_down, L0_ffn_A_down, L0_ffn_B_down, L0_ffn_scale_down, L0_ffn_bias_down):
    import numpy as np
    import concourse.bacc as bacc
    from concourse.bass_utils import run_bass_kernel_spmd

    def column(b):
        return np.asarray(b).reshape(DC, P).T

    laid = {
        "x": np.asarray(x).reshape(SEQS * SEQ, D), "ctx": ctx_1024, "wq": L0_xattn_Wq, "wk": L0_xattn_Wk,
        "bq": column(L0_xattn_bq), "bk": column(L0_xattn_bk), "bv": np.asarray(L0_xattn_bv).reshape(1, D),
        "xwv": np.asarray(L0_xattn_Wv).T, "swq": np.asarray(L0_attn_Wq).T, "swk": np.asarray(L0_attn_Wk).T,
        "swv": np.asarray(L0_attn_Wv).T, "swo": np.asarray(L0_attn_Wo).T,
        "bo": np.asarray(L0_attn_bo).reshape(1, D), "db": np.asarray(L0_attn_denom_bias).reshape(1, HEADS),
        "wr_up": np.asarray(L0_ffn_W_up).T,
        "wr_dn": np.asarray(L0_ffn_W_down).reshape(E, F1, F1).transpose(1, 2, 0),
        "a_up": L0_ffn_A_up, "b_up_f": L0_ffn_B_up, "a_dn": L0_ffn_A_down, "b_dn_f": L0_ffn_B_down,
        "iota": np.arange(E, dtype=np.float32).reshape(1, E),
        "b_up": np.asarray(L0_ffn_bias_up).reshape(F1, F1), "b_dn": np.asarray(L0_ffn_bias_down).reshape(1, 2 * D),
        "s_up": np.asarray(L0_ffn_scale_up).reshape(1, 1), "s_dn": np.asarray(L0_ffn_scale_down).reshape(1, 1),
    }
    nc = bacc.Bacc("TRN2", target_bir_lowering=False, num_devices=1)
    arrays, a = {}, {}
    for name in _IN:
        v = np.ascontiguousarray(laid[name])
        arrays[name] = v
        a[name] = nc.dram_tensor(name, v.shape, mybir.dt.from_np(v.dtype), kind="ExternalInput").ap()
    for name in ("x2", "x3"):
        a[name] = nc.dram_tensor(name + "_n", (QUADS, P, 2 * D), F32, kind="Internal").ap()
    out = nc.dram_tensor("out", (SEQS * SEQ, D), F32, kind="ExternalOutput").ap()
    program(nc, a, out)
    r = run_bass_kernel_spmd(nc, [arrays], core_ids=[0])
    return r.results[0]["out"].reshape(SEQS, SEQ, D)
```
